# Optimizing a Trainium2 kernel written in Bass

```python
import numpy as np
import jax
import jax.numpy as jnp

def _softmax(x, axis=-1):
    return jax.nn.softmax(x, axis=axis)

def _gelu(x):
    return jax.nn.gelu(x, approximate=True)

def _silu(x):
    return jax.nn.silu(x)

def _sigmoid(x):
    return jax.nn.sigmoid(x)

def _layernorm(x, axis=-1, eps=1e-05):
    m = jnp.mean(x, axis=axis, keepdims=True)
    v = jnp.var(x, axis=axis, keepdims=True)
    return (x - m) / jnp.sqrt(v + eps)

def _scatter_add(tgt, idx, src, axis=0):
    return tgt.at[idx].add(src)

def _segment_sum(src, seg, n):
    return jax.ops.segment_sum(src, seg, n)
kernel_name = 'mk_flamingo_gated_d2_seqx_r4_c59b8e'

def setup_inputs(seed: int=0):
    np.random.seed(seed)
    _w = jnp.asarray

    def _rec_inputs():
        import jax
        import jax.numpy as jnp
        _rk = jax.random.key(seed)
        x = -0.0002928 + 1 * jax.random.normal(jax.random.fold_in(_rk, 1), (8, 256, 256), jnp.float32)
        _lenS = 256 - jax.random.randint(jax.random.fold_in(_rk, 7), (8,), 0, max(1, 256 // 4) + 1, jnp.int32)
        _lenS2 = 77 - jax.random.randint(jax.random.fold_in(_rk, 8), (8,), 0, max(1, 77 // 4) + 1, jnp.int32)
        _ctx_1024P = jax.random.normal(jax.random.fold_in(_rk, 11), (8, 16, 256), jnp.float32)
        _ctx_1024c = jax.random.dirichlet(jax.random.fold_in(_rk, 511), 0.3 * jnp.ones((16,), jnp.float32), (8, 77))
        _ctx_1024t = jnp.einsum('bsk,bkd->bsd', _ctx_1024c, _ctx_1024P)
        _ctx_1024t = _ctx_1024t * jax.lax.rsqrt(jnp.mean(jnp.square(_ctx_1024t)) + 1e-12) * 0.953939
        ctx_1024 = -1.78809e-06 + 0.0312453 * (_ctx_1024t + 0.3 * jax.random.normal(jax.random.fold_in(_rk, 611), (8, 77, 256), jnp.float32))
        _g = jax.random.normal(jax.random.fold_in(_rk, 9001), (2, 2), jnp.float32)
        _g = jnp.sign(_g) * jnp.maximum(jnp.abs(_g), 1.0) + (_g == 0) * 1.0
        g_xattn = _g[0]
        g_ffn = _g[1]
        return (x, ctx_1024, g_xattn, g_ffn)
    x, ctx_1024, g_xattn, g_ffn = _rec_inputs()

    def _L0_xattn_setup():
        import jax, jax.numpy as jnp
        import numpy as np
        E, TPE, H, F = (64, 64, 256, 256)
        key = jax.random.key(seed)
        k1, k2, k3, k4 = jax.random.split(key, 4)
        scale = 1.0 / np.sqrt(H)
        return {'x': jax.random.normal(k1, (E, TPE, H), dtype=jnp.float32), 'w1': jax.random.normal(k2, (E, F, H), dtype=jnp.float32) * scale, 'v1': jax.random.normal(k3, (E, F, H), dtype=jnp.float32) * scale, 'w2': jax.random.normal(k4, (E, F, H), dtype=jnp.float32) * scale}
    _L0_xattn_all = _L0_xattn_setup()
    _L0_xattn_in = {k: v for k, v in _L0_xattn_all.items() if k in ()}
    del _L0_xattn_all

    def _L0_ffn_setup():
        import jax, jax.numpy as jnp
        import numpy as np
        DIM = 256

        def _reference_tuple_inner(x, W_r, W_k, W_v, mu_r, mu_k):
            B, T, C = x.shape
            x_prev = jnp.concatenate([jnp.zeros((B, 1, C), x.dtype), x[:, :-1, :]], axis=1)
            xr = mu_r * x + (1.0 - mu_r) * x_prev
            xk = mu_k * x + (1.0 - mu_k) * x_prev
            r = jax.nn.sigmoid(jnp.einsum('btc,dc->btd', xr, W_r))
            k = jnp.einsum('btc,dc->btd', xk, W_k)
            k_act = jnp.square(jax.nn.relu(k))
            out = r * jnp.einsum('btc,dc->btd', k_act, W_v)
            new_state = x[:, -1, :]
            return (out, new_state)
        key = jax.random.key(seed)
        ks = jax.random.split(key, 6)
        B, T, C = (8, 512, DIM)
        x = jax.random.normal(ks[0], (B, T, C), dtype=jnp.float32)
        s = 1.0 / np.sqrt(C)
        W_r = jax.random.uniform(ks[1], (C, C), jnp.float32, -s, s)
        W_k = jax.random.uniform(ks[2], (C, C), jnp.float32, -s, s)
        W_v = jax.random.uniform(ks[3], (C, C), jnp.float32, -s, s)
        mu_r = jax.random.uniform(ks[4], (C,), jnp.float32)
        mu_k = jax.random.uniform(ks[5], (C,), jnp.float32)
        return {'x': x, 'W_r': W_r, 'W_k': W_k, 'W_v': W_v, 'mu_r': mu_r, 'mu_k': mu_k}
    _L0_ffn_all = _L0_ffn_setup()
    _L0_ffn_in = {k: v for k, v in _L0_ffn_all.items() if k in ('W_r', 'W_k', 'W_v', 'mu_r', 'mu_k')}
    del _L0_ffn_all

    def _L1_xattn_setup():
        import jax, jax.numpy as jnp
        import numpy as np
        EMBED_DIM = 256
        NUM_HEADS = 16
        HEAD_DIM = EMBED_DIM // NUM_HEADS
        SCALE = HEAD_DIM ** (-0.5)
        key = jax.random.key(seed)
        ks = jax.random.split(key, 8)
        B, Nq, Nkv, C = (2, 512, 512, EMBED_DIM)
        s = C ** (-0.5)
        return {'q': jax.random.normal(ks[0], (B, Nq, C), dtype=jnp.float32), 'kv': jax.random.normal(ks[1], (B, Nkv, C), dtype=jnp.float32), 'w_q': jax.random.normal(ks[2], (C, C), dtype=jnp.float32) * s, 'b_q': jnp.zeros((C,), dtype=jnp.float32), 'w_kv': jax.random.normal(ks[3], (C, 2 * C), dtype=jnp.float32) * s, 'b_kv': jnp.zeros((2 * C,), dtype=jnp.float32), 'w_out': jax.random.normal(ks[4], (C, C), dtype=jnp.float32) * s, 'b_out': jnp.zeros((C,), dtype=jnp.float32)}
    _L1_xattn_all = _L1_xattn_setup()
    _L1_xattn_in = {k: v for k, v in _L1_xattn_all.items() if k in ('w_q', 'b_q', 'w_kv', 'b_kv', 'w_out', 'b_out')}
    del _L1_xattn_all

    def _L1_ffn_setup():
        import jax, jax.numpy as jnp
        import numpy as np
        TOP_K = 2
        EPS = 1e-09
        key = jax.random.key(seed)
        ks = jax.random.split(key, 6)
        B, T, D, H, E = (4, 512, 256, 512, 8)
        x = jax.random.normal(ks[0], (B, T, D), dtype=jnp.float32)
        Wg = jax.random.normal(ks[1], (E, D), dtype=jnp.float32) * 0.02
        W1 = jax.random.normal(ks[2], (E, 2 * H, D), dtype=jnp.float32) * 0.02
        b1 = jax.random.normal(ks[3], (E, 2 * H), dtype=jnp.float32) * 0.02
        Wo = jax.random.normal(ks[4], (D, H), dtype=jnp.float32) * 0.02
        bo = jax.random.normal(ks[5], (D,), dtype=jnp.float32) * 0.02
        return {'x': x, 'Wg': Wg, 'W1': W1, 'b1': b1, 'Wo': Wo, 'bo': bo}
    _L1_ffn_all = _L1_ffn_setup()
    _L1_ffn_in = {k: v for k, v in _L1_ffn_all.items() if k in ('Wg', 'W1', 'b1', 'Wo', 'bo')}
    del _L1_ffn_all
    return {'x': x, 'ctx_1024': ctx_1024, 'g_xattn': g_xattn, 'g_ffn': g_ffn, 'L0_ffn_W_r': _L0_ffn_in['W_r'], 'L0_ffn_W_k': _L0_ffn_in['W_k'], 'L0_ffn_W_v': _L0_ffn_in['W_v'], 'L0_ffn_mu_r': _L0_ffn_in['mu_r'], 'L0_ffn_mu_k': _L0_ffn_in['mu_k'], 'L1_xattn_w_q': _L1_xattn_in['w_q'], 'L1_xattn_b_q': _L1_xattn_in['b_q'], 'L1_xattn_w_kv': _L1_xattn_in['w_kv'], 'L1_xattn_b_kv': _L1_xattn_in['b_kv'], 'L1_xattn_w_out': _L1_xattn_in['w_out'], 'L1_xattn_b_out': _L1_xattn_in['b_out'], 'L1_ffn_Wg': _L1_ffn_in['Wg'], 'L1_ffn_W1': _L1_ffn_in['W1'], 'L1_ffn_b1': _L1_ffn_in['b1'], 'L1_ffn_Wo': _L1_ffn_in['Wo'], 'L1_ffn_bo': _L1_ffn_in['bo']}

def reference(x, ctx_1024, g_xattn, g_ffn, L0_ffn_W_r, L0_ffn_W_k, L0_ffn_W_v, L0_ffn_mu_r, L0_ffn_mu_k, L1_xattn_w_q, L1_xattn_b_q, L1_xattn_w_kv, L1_xattn_b_kv, L1_xattn_w_out, L1_xattn_b_out, L1_ffn_Wg, L1_ffn_W1, L1_ffn_b1, L1_ffn_Wo, L1_ffn_bo):
    import jax
    import jax.numpy as jnp

    def _L0_xattn_ref(x, w1, v1, w2):
        import jax, jax.numpy as jnp
        import numpy as np
        E, TPE, H, F = (64, 64, 256, 256)
        h1 = jnp.einsum('eth,efh->etf', x, w1)
        h2 = jnp.einsum('eth,efh->etf', x, v1)
        g = jax.nn.gelu(h1, approximate=False) * h2
        return jnp.einsum('etf,efh->eth', g, w2)

    def _L0_ffn_ref(x, W_r, W_k, W_v, mu_r, mu_k):
        import jax, jax.numpy as jnp
        import numpy as np
        DIM = 256

        def _reference_tuple_inner(x, W_r, W_k, W_v, mu_r, mu_k):
            B, T, C = x.shape
            x_prev = jnp.concatenate([jnp.zeros((B, 1, C), x.dtype), x[:, :-1, :]], axis=1)
            xr = mu_r * x + (1.0 - mu_r) * x_prev
            xk = mu_k * x + (1.0 - mu_k) * x_prev
            r = jax.nn.sigmoid(jnp.einsum('btc,dc->btd', xr, W_r))
            k = jnp.einsum('btc,dc->btd', xk, W_k)
            k_act = jnp.square(jax.nn.relu(k))
            out = r * jnp.einsum('btc,dc->btd', k_act, W_v)
            new_state = x[:, -1, :]
            return (out, new_state)
        return _reference_tuple_inner(x, W_r, W_k, W_v, mu_r, mu_k)[0]

    def _L1_xattn_ref(q, kv, w_q, b_q, w_kv, b_kv, w_out, b_out):
        import jax, jax.numpy as jnp
        import numpy as np
        EMBED_DIM = 256
        NUM_HEADS = 16
        HEAD_DIM = EMBED_DIM // NUM_HEADS
        SCALE = HEAD_DIM ** (-0.5)
        B, Nq, C = q.shape
        _, Nkv, _ = kv.shape
        H, D = (NUM_HEADS, HEAD_DIM)
        qp = (q @ w_q + b_q).reshape(B, Nq, H, D).transpose(0, 2, 1, 3)
        kvp = (kv @ w_kv + b_kv).reshape(B, Nkv, 2, H, D).transpose(2, 0, 3, 1, 4)
        kp, vp = (kvp[0], kvp[1])
        attn = jnp.einsum('bhqd,bhkd->bhqk', qp, kp) * SCALE
        attn = jax.nn.softmax(attn, axis=-1)
        out = jnp.einsum('bhqk,bhkd->bhqd', attn, vp)
        out = out.transpose(0, 2, 1, 3).reshape(B, Nq, C)
        return out @ w_out + b_out

    def _L1_ffn_ref(x, Wg, W1, b1, Wo, bo):
        import jax, jax.numpy as jnp
        import numpy as np
        TOP_K = 2
        EPS = 1e-09
        E = Wg.shape[0]
        gate_logits = jnp.einsum('btd,ed->bte', x, Wg)
        gate_scores = jax.nn.softmax(gate_logits, axis=-1)
        topk_val, topk_idx = jax.lax.top_k(gate_scores, TOP_K)
        topk_val = topk_val / (topk_val.sum(axis=-1, keepdims=True) + EPS)
        comb = (jax.nn.one_hot(topk_idx, E, dtype=x.dtype) * topk_val[..., None]).sum(axis=-2)
        out = jnp.zeros_like(x)
        for e in range(E):
            h = jnp.einsum('btd,hd->bth', x, W1[e]) + b1[e]
            a, b = jnp.split(h, 2, axis=-1)
            g = a * jax.nn.sigmoid(b)
            eo = jnp.einsum('bth,dh->btd', g, Wo) + bo
            out = out + eo * comb[..., e:e + 1]
        return out
    x = x + jnp.tanh(g_xattn[0]) * _L0_xattn_ref(_layernorm(x, axis=-1), ctx_1024, ctx_1024, ctx_1024)
    x = x + jnp.tanh(g_ffn[0]) * _L0_ffn_ref(_layernorm(x, axis=-1), L0_ffn_W_r, L0_ffn_W_k, L0_ffn_W_v, L0_ffn_mu_r, L0_ffn_mu_k)
    x = x + jnp.tanh(g_xattn[1]) * _L1_xattn_ref(_layernorm(x, axis=-1), ctx_1024, L1_xattn_w_q, L1_xattn_b_q, L1_xattn_w_kv, L1_xattn_b_kv, L1_xattn_w_out, L1_xattn_b_out)
    x = x + jnp.tanh(g_ffn[1]) * _L1_ffn_ref(_layernorm(x, axis=-1), L1_ffn_Wg, L1_ffn_W1, L1_ffn_b1, L1_ffn_Wo, L1_ffn_bo)
    return x

_drawn_inputs = setup_inputs


def setup_inputs(seed=0):
    import zlib

    import numpy as np

    out = dict(_drawn_inputs(seed))
    spreads = {'g_ffn': (-1.0, 0.6),
     'L1_xattn_b_q': (0.0, 0.8),
     'L1_xattn_b_kv': (0.0, 0.1),
     'L1_xattn_b_out': (0.0, 0.1)}
    factors = {'L0_ffn_W_r': 4.087,
     'L0_ffn_mu_r': 7.925,
     'L1_xattn_w_q': 8.0,
     'L1_xattn_w_kv': 3.828,
     'L1_ffn_b1': 8.0,
     'L1_ffn_bo': 3.407}
    for name, (base, spread) in spreads.items():
        noise = np.random.default_rng([zlib.crc32(name.encode()), seed]).standard_normal(out[name].shape)
        drawn = base * np.exp(spread * noise) if base else spread * noise
        out[name] = jnp.asarray(drawn.astype(out[name].dtype))
    for name, factor in factors.items():
        out[name] = (out[name] * factor).astype(out[name].dtype)
    return out
```

```python
from contextlib import ExitStack

import numpy as np

import concourse.bass as bass
from concourse import mybir
from concourse.alu_op_type import AluOpType as ALU

F32 = mybir.dt.float32
BF16 = mybir.dt.bfloat16
U32 = mybir.dt.uint32
I32 = mybir.dt.int32
ACT = mybir.ActivationFunctionType
AX_X = mybir.AxisListType.X

P = 128
B, T, D = 8, 256, 256
KT = D // P
TT = T // P
C = 77
H, HD = 16, 16
HB = P // HD
E, TOPK = 8, 2
F = 512
FT = F // P
IT = B // 2
EPS = 1e-5
CAP = B * T + P
TILES = (B * T * TOPK + E * (P - 1)) // P
IDLE = TILES - B * T * TOPK // P
SLOTS = E * CAP + IDLE * P
START = 1
VEC_STEPS = 86


def start(eng, *sems):
    for s in sems:
        for one in s if isinstance(s, list) else [s]:
            eng.sem_inc(one, START)


class Steps:

    def __init__(self, eng, sem, base):
        self.eng, self.sem, self.base, self.n = eng, sem, base, 0

    def done(self, instruction):
        self.n += 1
        instruction.then_inc(self.sem, 1)

    def wait(self):
        self.eng.wait_ge(self.sem, self.base + self.n)


def build(nc, d, out):
    with ExitStack() as ctx:
        def sb(name, shape, dt=F32):
            return ctx.enter_context(nc.sbuf_tensor(name, shape, dt))

        def sem(name):
            return ctx.enter_context(nc.semaphore(name))

        def pair(make, name, *a):
            return [make(f"{name}{u}", *a) for u in range(2)]

        w_r, w_k, w_v, w_q, w_out = (sb(n, [P, KT, D]) for n in ("w_r", "w_k", "w_v", "w_q", "w_out"))
        w_kv = sb("w_kv", [P, KT, 2 * D])
        w_g = sb("w_g", [P, KT, E])
        w_o = sb("w_o", [P, FT, D])
        w_1 = sb("w_1", [P, E, KT, 2 * F])
        b_1 = sb("b_1", [P, E, 2 * F])
        chan = sb("chan", [P, 4, KT])
        rows = sb("rows", [P, 3, D])
        gates = sb("gates", [P, 4])
        tg = sb("tg", [P, 4])
        half_tg = sb("half_tg", [P, 1])
        ident = sb("ident", [P, P])
        tri_ones16 = sb("tri_ones16", [P, 2, P], BF16)
        ident16 = sb("ident16", [P, P], BF16)
        headmask = sb("headmask", [P, HB])
        negsel16 = sb("negsel16", [H, H, C], BF16)
        iotas = sb("iotas", [P, 2, E])
        tile_no = sb("tile_no", [1, TILES + 1])
        half_power = sb("half_power", [P, TT])
        zeros = sb("zeros", [P, D])
        carrier = sb("carrier", [P, 9])
        x = pair(sb, "x", [P, TT, D])
        z = pair(sb, "z", [P, TT, D])
        stats = pair(sb, "stats", [P, TT, 6])
        mv = pair(sb, "mv", [P, TT, 2])
        vare = pair(sb, "vare", [P, TT])
        rstd = pair(sb, "rstd", [P, TT])
        cx = pair(sb, "cx", [C, D])
        cxT = pair(sb, "cxT", [P, KT, C])
        aT = pair(sb, "aT", [P, KT, T])
        aTs = pair(sb, "aTs", [P, KT, T + 1])
        ge = pair(sb, "ge", [C, T])
        gT = pair(sb, "gT", [C, T])
        kT = pair(sb, "kT", [P, KT, C])
        kbd = pair(sb, "kbd", [P, H, C])
        kbd16 = pair(sb, "kbd16", [P, H, C], BF16)
        v = pair(sb, "v", [C, H, HD + 1])
        diff = sb("diff", [P, KT, T])
        xr = pair(sb, "xr", [P, KT, T])
        xk = pair(sb, "xk", [P, KT, T])
        th = pair(sb, "th", [P, TT, D])
        rk = pair(sb, "rk", [P, KT, T])
        qT16 = pair(sb, "qT16", [P, KT, T], BF16)
        mx = pair(sb, "mx", [P, TT, H])
        mx16 = pair(sb, "mx16", [P, TT, H], BF16)
        mT = pair(sb, "mT", [H, T], BF16)
        probs = b_1[0:C, E // 2:E, :].rearrange("p e f -> p (e f)").rearrange("p (c h t) -> p c h t", h=2, t=T)
        rden = pair(sb, "rden", [P, TT, H])
        ka, yb, qT, att, attT = rk, xr, xk, th, aTs
        lg = pair(sb, "lg", [P, TT, E])
        top = pair(sb, "top", [P, TT, 8])
        topi = pair(sb, "topi", [P, TT, 8], U32)
        topf = pair(sb, "topf", [P, TOPK, TT])
        dl = pair(sb, "dl", [P, TT, E + 1])
        el = pair(sb, "el", [P, TT, E + 1])
        zsum = pair(sb, "zsum", [P, TT])
        den = pair(sb, "den", [P, TT])
        wk = pair(sb, "wk", [P, TT, TOPK])
        wsum = pair(sb, "wsum", [P, TT])
        oh = pair(sb, "oh", [P, TOPK, TT, E])
        chosen = pair(sb, "chosen", [P, TT, E], BF16)
        pos = pair(sb, "pos", [P, TT, E])
        ohpos = pair(sb, "ohpos", [P, TOPK, TT, E])
        slotf = pair(sb, "slotf", [P, TOPK * TT])
        slot = pair(sb, "slot", [P, TOPK * TT], U32)
        fill = sb("fill", [P, E])
        fill1 = sb("fill1", [P, E])
        xres = sb("xres", [P, B, TT, D])
        wres = sb("wres", [P, B, TT, TOPK])
        slotres = sb("slotres", [P, B, TOPK * TT])
        expres = sb("expres", [P, B, TOPK * TT])
        packed = sb("packed", [P, B, TOPK * TT], U32)
        filled = sb("filled", [P, E])
        filled_i = sb("filled_i", [P, E], I32)
        fill_i = sb("fill_i", [1, E], I32)
        ntiles = sb("ntiles", [P, E])
        ones_row = sb("ones_row", [P, E])
        cum = sb("cum", [P, E])
        shift = sb("shift", [P, E])
        moved = kbd[0][:, :, :].rearrange("p h c -> p (h c)")[:, 0:B * TOPK * TT * E].rearrange(
            "p (s e) -> p s e", e=E)
        past = sb("past", [1, TILES, E])
        pastn = sb("pastn", [1, TILES, E])
        tile_e = sb("tile_e", [1, TILES])
        tile_c = sb("tile_c", [1, TILES])
        tile_w = sb("tile_w", [1, TILES], I32)
        tile_r = sb("tile_r", [1, TILES], I32)
        sl = [x[u][:, 0, :] for u in range(2)]
        slT = [aT[u][:, :, 0:P] for u in range(2)]
        gate_h = [xr[u][:, :, :].rearrange("p a b -> p (a b)") for u in range(2)]
        val_h = [xk[u][:, :, :].rearrange("p a b -> p (a b)") for u in range(2)]
        sig_h = [rk[u][:, :, :].rearrange("p a b -> p (a b)") for u in range(2)]
        g_h = [th[u][:, :, :].rearrange("p a b -> p (a b)") for u in range(2)]
        g_hT = [aTs[u][:, :, :].rearrange("p a b -> p (a b)")[:, 0:F].rearrange("p (a b) -> p a b", a=FT)
                for u in range(2)]
        o_s = [x[u][:, 1, :] for u in range(2)]
        got = [kbd[u][:, :, :].rearrange("p h c -> p (h c)")[:, 0:TOPK * TT * D].rearrange(
            "p (s d) -> p s d", d=D) for u in range(2)]
        y_out = [xr[u] for u in range(2)]

        bank = [ctx.enter_context(nc.psum_tensor(f"bank{i}", [P, 512], F32)) for i in range(8)]
        tb, mb, ring = bank[0:2], bank[2:4], bank[4:8]

        slots_dram = nc.dram_tensor("slots_dram", (SLOTS, D), F32, kind="Internal").ap()
        outs_dram = nc.dram_tensor("outs_dram", (TILES * P, D), F32, kind="Internal").ap()

        s_small, s_w, s_w1, s_b1 = sem("s_small"), sem("s_w"), sem("s_w1"), sem("s_b1")
        s_const = sem("s_const")
        s_tg = sem("s_tg")
        s_idle = sem("s_idle")
        x_in, cx_in = pair(sem, "x_in"), pair(sem, "cx_in")
        var_ready, rstd_ready = pair(sem, "var_ready"), pair(sem, "rstd_ready")
        z_ready, zT_ps, aT_ready = pair(sem, "z_ready"), pair(sem, "zT_ps"), pair(sem, "aT_ready")
        h_ps, ge_ready, g_ready = pair(sem, "h_ps"), pair(sem, "ge_ready"), pair(sem, "g_ready")
        k_ps, kT_ready, kbd_ready = pair(sem, "k_ps"), pair(sem, "kT_ready"), pair(sem, "kbd_ready")
        o_ps = pair(sem, "o_ps")
        xr_ready, xk_ready = pair(sem, "xr_ready"), pair(sem, "xk_ready")
        r_ps, th_ready, kk_ps, rk_ready, ka_ready = (pair(sem, n) for n in ("r_ps", "th_ready", "kk_ps", "rk_ready", "ka_ready"))
        y_ps, v_ps, v_ready = pair(sem, "y_ps"), pair(sem, "v_ps"), pair(sem, "v_ready")
        x2_done = pair(sem, "x2_done")
        q_ps, q_ready, q16_ready, x2b_ready = pair(sem, "q_ps"), pair(sem, "q_ready"), pair(sem, "q16_ready"), pair(sem, "x2b_ready")
        s_ps, max_done = sem("s_ps"), sem("max_done")
        mx_ready, mT_ps, mT_ready = pair(sem, "mx_ready"), pair(sem, "mT_ps"), pair(sem, "mT_ready")
        st_ps, exp_done, pv_done = sem("st_ps"), sem("exp_done"), sem("pv_done")
        att_ready, attT_ps, attT_ready, out_ps = (pair(sem, n) for n in ("att_ready", "attT_ps", "attT_ready", "out_ps"))
        lg_ps, dl_ready, el_ready, oh_ready, rank_ps, slot_ready = (
            pair(sem, n) for n in ("lg_ps", "dl_ready", "el_ready", "oh_ready", "rank_ps", "slot_ready"))
        sent, z_free = pair(sem, "sent"), pair(sem, "z_free")
        vec_step = sem("vec_step")
        tab_step, tab_ready, pad_done = sem("tab_step"), sem("tab_ready"), sem("pad_done")
        sl_in, slT_ps, slT_ready, hh_ps, gate_ready, sig_ready, gh_ready = (
            pair(sem, n) for n in ("sl_in", "slT_ps", "slT_ready", "hh_ps", "gate_ready", "sig_ready", "gh_ready"))
        val_ready = pair(sem, "val_ready")
        ghT_ps, ghT_ready, os_ps, os_ready, os_out = (
            pair(sem, n) for n in ("ghT_ps", "ghT_ready", "os_ps", "os_ready", "os_out"))
        fidx_ready, fetched, half_y, y_ready, y_out_done = (
            pair(sem, n) for n in ("fidx_ready", "fetched", "half_y", "y_ready", "y_out_done"))
        s_init = sem("s_init")
        carried = pair(sem, "carried")
        block = ctx.enter_context(nc.Block())

        def m_tok(u):
            return mb[u][:, :].rearrange("p (t d) -> p t d", t=TT)

        def t_chan(u):
            return tb[u][:, :].rearrange("p (k t) -> p k t", k=KT)

        def flat(a):
            return a.rearrange("p a b -> p (a b)")


        @block.sync
        def _(sp):
            for t, n in ((ident, "ident"), (gates, "gates"), (chan, "chan"), (rows, "rows"), (w_g, "w_g"),
                         (tri_ones16, "tri_ones"), (ident16, "ident16"), (headmask, "headmask"), (negsel16, "negsel"), (iotas, "iotas"),
                         (tile_no, "tile_no")):
                sp.dma_start(t[:], d[n]).then_inc(s_small, 16)
            start(sp, x_in, cx_in, sl_in, y_out_done)
            with sp.Fori(0, IT) as i:
                for u in range(2):
                    n = 2 * i + u
                    sp.wait_ge(slot_ready[u], START + i)
                    sp.dma_start(x[u][:, :, :], d["x"][bass.ds(n, 1), :, :].rearrange(
                        "n (t p) d -> p (n t) d", p=P)).then_inc(x_in[u], 16)
                    sp.wait_ge(v_ps[u], START + i)
                    sp.wait_ge(o_ps[u], START + i)
                    sp.dma_start(cx[u][:, :], d["ctx"][bass.ds(n, 1), :, :].rearrange(
                        "n c d -> (n c) d")).then_inc(cx_in[u], 16)
                    sp.dma_start(cxT[u][:, :, :], d["ctxT"][bass.ds(n, 1), :, :].rearrange(
                        "n (k p) c -> p (n k) c", p=P)).then_inc(cx_in[u], 16)
            sp.wait_ge(tab_ready, 1)
            for e in range(E):
                at = sp.value_load(fill_i[0:1, e:e + 1], min_val=0, max_val=E * CAP - P)
                sp.dma_start(slots_dram[bass.ds(at, P), :], zeros[:, :]).then_inc(pad_done, 16)
            sp.wait_ge(pad_done, 16 * E)
            sp.wait_ge(s_idle, 16 * IDLE)
            for u in range(2):
                sp.wait_ge(sent[u], 16 * TT * TOPK * IT)

            def load_slots(j, i, u):
                row = sp.value_load(tile_r[0:1, bass.ds(j, 1)], min_val=0, max_val=SLOTS - P)
                sp.wait_ge(slT_ps[u], START + i)
                sp.dma_start(sl[u], slots_dram[bass.ds(row, P), :]).then_inc(sl_in[u], 16)

            with sp.Fori(0, TILES // 2) as i:
                for u in range(2):
                    load_slots(2 * i + u, i, u)
            load_slots(TILES - 1, TILES // 2, 0)

            with sp.Fori(0, IT) as i:
                for u in range(2):
                    sp.wait_ge(y_ready[u], START + i + 1)
                    sp.dma_start(out[bass.ds(2 * i + u, 1), :, :].rearrange("n (t p) d -> p (n t) d", p=P),
                                 y_out[u][:, :, :]).then_inc(y_out_done[u], 16)
            for u in range(2):
                sp.wait_ge(y_out_done[u], START + 16 * IT)

        @block.gpsimd
        def _(pool):
            start(pool, rstd_ready, kbd_ready, ka_ready, q16_ready, x2b_ready, z_free, carried)
            pool.memset(zeros[:, :], 0.0).then_inc(s_init, 1)
            pool.memset(half_power[:, :], -0.5).then_inc(s_init, 1)
            pool.memset(ones_row[:, :], 1.0).then_inc(s_init, 1)
            for u in range(2):
                pool.memset(v[u][:, :, HD:HD + 1], 1.0).then_inc(s_init, 1)
                pool.memset(aTs[u][:, :, 0:1], 0.0).then_inc(s_init, 1)
            pool.wait_ge(s_init, 7)
            pool.wait_ge(s_small, 176)
            for i in range(IDLE):
                pool.dma_start(slots_dram[E * CAP + i * P:E * CAP + (i + 1) * P, :],
                               zeros[:, :]).then_inc(s_idle, 16)

            def inverse_deviation(i, k):
                for u in range(2):
                    n = 4 * i + k + 1
                    pool.wait_ge(var_ready[u], START + n)
                    pool.tensor_tensor(rstd[u][:, :], vare[u][:, :], half_power[:, :], ALU.pow)\
                        .then_inc(rstd_ready[u], 1)

            with pool.Fori(0, IT) as i:
                inverse_deviation(i, 0)
                for u in range(2):
                    pool.wait_ge(kT_ready[u], START + i + 1)
                    pool.wait_ge(st_ps, START + 16 * i)
                    for k in range(KT):
                        for dst in (kbd, kbd16):
                            ins = pool.tensor_tensor(
                                dst[u][:, k * HB:(k + 1) * HB, :],
                                kT[u][:, k, :].unsqueeze(1).to_broadcast([P, HB, C]),
                                headmask[:, :].unsqueeze(2).to_broadcast([P, HB, C]), ALU.mult)
                            ins.then_inc(kbd_ready[u], 1)
                inverse_deviation(i, 1)
                for u in range(2):
                    pool.wait_ge(rk_ready[u], START + i + 1)
                    pool.tensor_tensor(ka[u][:, :, :], rk[u][:, :, :], rk[u][:, :, :], ALU.mult)\
                        .then_inc(ka_ready[u], 1)
                inverse_deviation(i, 2)
                for u in range(2):
                    pool.wait_ge(q_ready[u], START + i + 1)
                    pool.tensor_tensor(carrier[:, 1 + u:2 + u], zeros[:, 0:1], zeros[:, 0:1], ALU.add)
                    pool.tensor_copy(qT16[u][:, :, :], qT[u][:, :, :]).then_inc(q16_ready[u], 1)
                for u in range(2):
                    pool.wait_ge(z_ready[u], START + 4 * i + 3)
                    pool.wait_ge(s_const, 2)
                    for t in range(TT):
                        pool.tensor_tensor(x[u][:, t, :], x[u][:, t, :], rows[:, 1, :], ALU.add)\
                            .then_inc(x2b_ready[u], 1)
                inverse_deviation(i, 3)
                for u in range(2):
                    pool.wait_ge(slot_ready[u], START + i + 1)
                    pool.tensor_tensor(carrier[:, 3 + u:4 + u], zeros[:, 0:1], zeros[:, 0:1], ALU.add)
                    for k in range(TOPK):
                        for t in range(TT):
                            c = k * TT + t
                            pool.indirect_dma_start(
                                out=slots_dram, out_offset=bass.IndirectOffsetOnAxis(ap=slot[u][:, c:c + 1], axis=0),
                                in_=z[u][:, t, :], in_offset=None).then_inc(sent[u], 16)
                for u in range(2):
                    pool.wait_ge(sent[u], 16 * TT * TOPK * (i + 1))
                    pool.tensor_tensor(carrier[:, 7 + u:8 + u], zeros[:, 0:1], zeros[:, 0:1], ALU.add)\
                        .then_inc(z_free[u], 1)

            pool.wait_ge(tab_ready, 1)
            pool.wait_ge(os_out[0], START + 16 * (TILES // 2 + 1))
            pool.wait_ge(os_out[1], START + 16 * (TILES // 2))

            with pool.Fori(0, IT) as i:
                for u in range(2):
                    pool.wait_ge(fidx_ready[u], START + i + 1)
                    pool.wait_ge(y_ready[u], START + i)
                    pool.wait_ge(carried[u], START + i)
                    pool.tensor_tensor(carrier[:, 5 + u:6 + u], zeros[:, 0:1], zeros[:, 0:1], ALU.add)\
                        .then_inc(carried[u], 1)
                    for c in range(TOPK * TT):
                        pool.indirect_dma_start(
                            out=got[u][:, c, :], out_offset=None, in_=outs_dram,
                            in_offset=bass.IndirectOffsetOnAxis(ap=slot[u][:, c:c + 1], axis=0),
                        ).then_inc(fetched[u], 16)

        @block.scalar
        def _(act):
            for t, n in ((w_kv, "w_kv"), (w_r, "w_r"), (w_k, "w_k"), (w_v, "w_v"), (w_q, "w_q"),
                         (w_out, "w_out"), (w_o, "w_o")):
                act.dma_start(t[:], d[n]).then_inc(s_w, 16)
            for e in range(E):
                act.dma_start(w_1[:, e, :, :], d["w_1"][e].rearrange("(k p) f -> p k f", p=P)).then_inc(s_w1, 16)
            act.dma_start(b_1[:, 0:E // 2, :], d["b_1"][:, 0:E // 2, :]).then_inc(s_b1, 16)
            start(act, aT_ready, ge_ready, kT_ready, th_ready, rk_ready, q_ready, mT_ready, exp_done, attT_ready, el_ready,
                  slT_ready, sig_ready, ghT_ready, os_ready, os_out)
            act.wait_ge(s_small, 176)
            act.activation(tg[:, :], gates[:, :], ACT.Tanh).then_inc(s_tg, 1)

            def turn(i, k, u, before):
                dst = aTs[u][:, :, 1:T + 1] if k == 1 else aT[u][:, :, :]
                act.wait_ge(zT_ps[u], START + 4 * i + k + 1)
                before()
                act.activation(dst, t_chan(u), ACT.Copy).then_inc(aT_ready[u], 1)

            with act.Fori(0, IT) as i:
                for u in range(2):
                    turn(i, 0, u, lambda: act.wait_ge(lg_ps[u], START + i))
                for u in range(2):
                    act.wait_ge(h_ps[u], START + i + 1)
                    act.wait_ge(g_ready[u], START + i)
                    act.activation(ge[u][:, :], mb[u][0:C, 0:T], ACT.Gelu).then_inc(ge_ready[u], 1)
                for u in range(2):
                    act.wait_ge(k_ps[u], START + i + 1)
                    act.wait_ge(kbd_ready[u], START + 2 * KT * i)
                    for k in range(KT):
                        ins = act.activation(kT[u][:, k, :], tb[u][:, k * C:(k + 1) * C], ACT.Identity,
                                             bias=chan[:, 3, k:k + 1])
                    ins.then_inc(kT_ready[u], 1)
                for u in range(2):
                    turn(i, 1, u, lambda: act.wait_ge(out_ps[u], START + i))
                for u in range(2):
                    act.wait_ge(r_ps[u], START + i + 1)
                    act.wait_ge(attT_ps[u], START + i)
                    act.activation(flat(th[u][:, :, :]), tb[u][:, :], ACT.Tanh, scale=0.5).then_inc(th_ready[u], 1)
                    act.wait_ge(kk_ps[u], START + i + 1)
                    act.wait_ge(y_ps[u], START + i)
                    act.activation(flat(rk[u][:, :, :]), mb[u][:, :], ACT.Relu).then_inc(rk_ready[u], 1)
                for u in range(2):
                    turn(i, 2, u, lambda: act.wait_ge(h_ps[u], START + i + 1))
                for u in range(2):
                    act.wait_ge(q_ps[u], START + i + 1)
                    for k in range(KT):
                        ins = act.activation(qT[u][:, k, :], mb[u][:, k * T:(k + 1) * T], ACT.Identity,
                                             bias=chan[:, 2, k:k + 1])
                    ins.then_inc(q_ready[u], 1)
                for u in range(2):
                    act.wait_ge(mT_ps[u], START + i + 1)
                    act.activation(mT[u][:, :], tb[u][0:H, 0:T], ACT.Copy).then_inc(mT_ready[u], 1)
                for u in range(2):
                    for c in range(H // 2):
                        act.wait_ge(st_ps, START + 16 * i + 8 * u + c + 1)
                        if u == 0 and c == 0:
                            act.wait_ge(pv_done, START + 16 * i)
                        if u == 1:
                            act.wait_ge(pv_done, START + 16 * i + c + 1)
                        act.activation(flat(probs[:, c, :, :]), ring[c % 4][0:C, :], ACT.Exp,
                                       scale=HD ** -0.5).then_inc(exp_done, 1)
                for u in range(2):
                    act.wait_ge(attT_ps[u], START + i + 1)
                    act.activation(attT[u][:, :, 1:T + 1], t_chan(u), ACT.Copy).then_inc(attT_ready[u], 1)
                for u in range(2):
                    turn(i, 3, u, lambda: act.wait_ge(q_ps[u], START + i + 1))
                for u in range(2):
                    act.wait_ge(dl_ready[u], START + i + 1)
                    act.activation(el[u][:, :, :], dl[u][:, :, :], ACT.Exp).then_inc(el_ready[u], 1)

            act.wait_ge(pv_done, START + 16 * IT)
            act.dma_start(b_1[:, E // 2:E, :], d["b_1"][:, E // 2:E, :]).then_inc(s_b1, 16)

            def take_in(i, u):
                act.wait_ge(slT_ps[u], START + i + 1)
                act.wait_ge(hh_ps[u], START + i)
                act.activation(slT[u], tb[u][:, 0:D].rearrange("p (k t) -> p k t", k=KT), ACT.Copy)\
                    .then_inc(slT_ready[u], 1)

            def gate(i, u):
                act.wait_ge(gate_ready[u], START + i + 1)
                act.wait_ge(gh_ready[u], START + i)
                act.activation(sig_h[u], gate_h[u], ACT.Sigmoid).then_inc(sig_ready[u], 1)

            def bring_out(i, u):
                act.wait_ge(ghT_ps[u], START + i + 1)
                act.wait_ge(os_ps[u], START + i)
                act.activation(g_hT[u], ring[2][:, :].rearrange("p (a b) -> p a b", a=FT), ACT.Copy)\
                    .then_inc(ghT_ready[u], 1)
                act.wait_ge(os_ps[u], START + i + 1)
                act.wait_ge(os_out[u], START + 16 * i)
                act.activation(o_s[u], ring[3][:, 0:D], ACT.Copy).then_inc(os_ready[u], 1)

            def store(j, i, u):
                act.wait_ge(os_ready[u], START + i + 1)
                act.dma_start(outs_dram[bass.ds(P * j, P), :], o_s[u]).then_inc(os_out[u], 16)

            LAST = TILES // 2
            take_in(0, 0)
            take_in(0, 1)
            gate(0, 0)
            take_in(1, 0)
            gate(0, 1)
            bring_out(0, 0)
            with act.Fori(1, LAST) as i:
                take_in(i, 1)
                store(2 * i - 2, i - 1, 0)
                gate(i, 0)
                bring_out(i - 1, 1)
                take_in(i + 1, 0)
                store(2 * i - 1, i - 1, 1)
                gate(i, 1)
                bring_out(i, 0)
            store(2 * LAST - 2, LAST - 1, 0)
            gate(LAST, 0)
            bring_out(LAST - 1, 1)
            store(2 * LAST - 1, LAST - 1, 1)
            bring_out(LAST, 0)
            store(2 * LAST, LAST, 0)

        @block.tensor
        def _(pe):
            start(pe, zT_ps, h_ps, k_ps, o_ps, r_ps, kk_ps, y_ps, v_ps, q_ps, s_ps, mT_ps, st_ps, pv_done, attT_ps, out_ps,
                  lg_ps, rank_ps, slT_ps, hh_ps, ghT_ps, os_ps)
            pe.wait_ge(s_small, 176)
            pe.wait_ge(s_w, 112)
            pe.wait_ge(s_const, 1)

            def turn(i, k, u):
                pe.wait_ge(z_ready[u], START + 4 * i + k + 1)
                for kt in range(KT):
                    for t in range(TT):
                        ins = pe.transpose(t_chan(u)[:, kt, t * P:(t + 1) * P],
                                           z[u][:, t, kt * P:(kt + 1) * P], ident[:, :])
                ins.then_inc(zT_ps[u], 1)

            def by_token(dst, actT, w):
                for t in range(TT):
                    for kt in range(KT):
                        ins = pe.matmul(dst[:, t, :], actT[:, kt, t * P:(t + 1) * P], w[:, kt, :],
                                        start=(kt == 0), stop=(kt == KT - 1))
                return ins

            def by_channel(dst, w, actT, off=0):
                for m in range(KT):
                    for kt in range(KT):
                        ins = pe.matmul(dst[:, m, :], w[:, kt, off + m * P:off + (m + 1) * P], actT[:, kt, :],
                                        start=(kt == 0), stop=(kt == KT - 1))
                return ins

            with pe.Fori(0, IT) as i:
                for u in range(2):
                    pe.wait_ge(aT_ready[u], START + 4 * i)
                    turn(i, 0, u)
                for u in range(2):
                    pe.wait_ge(aT_ready[u], START + 4 * i + 1)
                    pe.wait_ge(cx_in[u], START + 32 * (i + 1))
                    pe.wait_ge(slot_ready[u], START + i)
                    for kt in range(KT):
                        ins = pe.matmul(mb[u][0:C, 0:T], cxT[u][:, kt, :], aT[u][:, kt, :],
                                        start=(kt == 0), stop=(kt == KT - 1))
                    ins.then_inc(h_ps[u], 1)
                for u in range(2):
                    for m in range(KT):
                        for kt in range(KT):
                            ins = pe.matmul(tb[u][:, m * C:(m + 1) * C], w_kv[:, kt, m * P:(m + 1) * P],
                                            cxT[u][:, kt, :], start=(kt == 0), stop=(kt == KT - 1))
                    ins.then_inc(k_ps[u], 1)
                for u in range(2):
                    pe.wait_ge(g_ready[u], START + i + 1)
                    for t in range(TT):
                        ins = pe.matmul(m_tok(u)[:, t, :], gT[u][:, t * P:(t + 1) * P], cx[u][:, :],
                                        start=True, stop=True)
                    ins.then_inc(o_ps[u], 1)
                for u in range(2):
                    pe.wait_ge(kT_ready[u], START + i + 1)
                    turn(i, 1, u)
                for u in range(2):
                    pe.wait_ge(aT_ready[u], START + 4 * i + 2)
                    pe.wait_ge(xr_ready[u], START + i + 1)
                    by_token(tb[u][:, :].rearrange("p (t d) -> p t d", t=TT), xr[u], w_r).then_inc(r_ps[u], 1)
                    pe.wait_ge(xk_ready[u], START + i + 1)
                    by_channel(mb[u][:, :].rearrange("p (k t) -> p k t", k=KT), w_k, xk[u]).then_inc(kk_ps[u], 1)
                for u in range(2):
                    pe.wait_ge(ka_ready[u], START + i + 1)
                    by_token(m_tok(u), ka[u], w_v).then_inc(y_ps[u], 1)
                for u in range(2):
                    pe.wait_ge(x2_done[u], START + i + 1)
                    for kt in range(KT):
                        ins = pe.matmul(mb[u][0:C, 0:D], cxT[u][:, kt, :], w_kv[:, kt, D:2 * D],
                                        start=(kt == 0), stop=(kt == KT - 1))
                    ins.then_inc(v_ps[u], 1)
                for u in range(2):
                    pe.wait_ge(th_ready[u], START + i + 1)
                    turn(i, 2, u)
                for u in range(2):
                    pe.wait_ge(aT_ready[u], START + 4 * i + 3)
                    pe.wait_ge(v_ready[u], START + i + 1)
                    by_channel(mb[u][:, :].rearrange("p (k t) -> p k t", k=KT), w_q, aT[u]).then_inc(q_ps[u], 1)
                for u in range(2):
                    pe.wait_ge(q16_ready[u], START + i + 1)
                    pe.wait_ge(kbd_ready[u], START + 2 * KT * (i + 1))
                    for c in range(8):
                        t, hq = c // 4, c % 4
                        if c >= 4:
                            pe.wait_ge(max_done, START + 16 * i + 8 * u + c - 3)
                        elif u == 1:
                            pe.wait_ge(max_done, START + 16 * i + c + 5)
                        elif c == 0:
                            pe.wait_ge(exp_done, START + 16 * i)
                        pe.matmul(ring[c % 4][:, 0:4 * C], qT16[u][:, hq // 2, t * P:(t + 1) * P],
                                  flat(kbd16[u][:, 4 * hq:4 * hq + 4, :]), start=True, stop=True).then_inc(s_ps, 1)
                for u in range(2):
                    pe.wait_ge(mx_ready[u], START + i + 1)
                    for t in range(TT):
                        ins = pe.matmul(tb[u][0:H, t * P:(t + 1) * P], mx16[u][:, t, :], ident16[:, :],
                                        start=True, stop=True)
                    ins.then_inc(mT_ps[u], 1)

                def weigh(i, u, c):
                    pe.wait_ge(exp_done, START + 16 * i + 8 * u + c + 1)
                    if c == 0:
                        pe.wait_ge(q_ready[u], START + i + 1)
                        pe.wait_ge(mT_ready[u], START + i + 1)
                        pe.wait_ge(v_ready[u], START + i + 1)
                    for h in (2 * c, 2 * c + 1):
                        for t in range(TT):
                            dst = (mb, tb)[t][u]
                            ins = pe.matmul(dst[:, h * (HD + 1):(h + 1) * (HD + 1)],
                                            probs[:, c, h % 2, t * P:(t + 1) * P], v[u][:, h, :],
                                            start=True, stop=True)
                    ins.then_inc(pv_done, 1)

                for u in range(2):
                    pe.wait_ge(mT_ready[u], START + i + 1)
                    for c in range(8):
                        if c >= 4:
                            pe.wait_ge(exp_done, START + 16 * i + 8 * u + c - 3)
                        elif u == 0:
                            pe.wait_ge(max_done, START + 16 * i + 8 + c + 5)
                        else:
                            pe.wait_ge(exp_done, START + 16 * i + c + 5)
                        for h in (2 * c, 2 * c + 1):
                            dst = ring[c % 4][0:C, (h % 2) * T:(h % 2 + 1) * T]
                            pe.matmul(dst, negsel16[:, h, :], mT[u][:, :], start=True, stop=False)
                            ins = pe.matmul(dst, kbd[u][:, h, :], qT[u][:, h // HB, :], start=False, stop=True)
                        ins.then_inc(st_ps, 1)
                        if c >= 2:
                            weigh(i, u, c - 2)
                    weigh(i, u, 6)
                    weigh(i, u, 7)
                for u in range(2):
                    pe.wait_ge(att_ready[u], START + i + 1)
                    for kt in range(KT):
                        for t in range(TT):
                            ins = pe.transpose(t_chan(u)[:, kt, t * P:(t + 1) * P],
                                               att[u][:, t, kt * P:(kt + 1) * P], ident[:, :])
                    ins.then_inc(attT_ps[u], 1)
                for u in range(2):
                    pe.wait_ge(attT_ready[u], START + i + 1)
                    by_token(m_tok(u), attT[u][:, :, 1:T + 1], w_out).then_inc(out_ps[u], 1)
                for u in range(2):
                    turn(i, 3, u)
                for u in range(2):
                    pe.wait_ge(aT_ready[u], START + 4 * i + 4)
                    for t in range(TT):
                        for kt in range(KT):
                            ins = pe.matmul(mb[u][:, t * E:(t + 1) * E], aT[u][:, kt, t * P:(t + 1) * P],
                                            w_g[:, kt, :], start=(kt == 0), stop=(kt == KT - 1))
                    ins.then_inc(lg_ps[u], 1)
                for u in range(2):
                    pe.wait_ge(oh_ready[u], START + i + 1)
                    for m in range(2):
                        ins = pe.matmul(mb[u][:, (1 + m) * TT * E:(2 + m) * TT * E], tri_ones16[:, m, :],
                                        flat(chosen[u][:, :, :]), start=True, stop=True)
                    ins.then_inc(rank_ps[u], 1)

            pe.wait_ge(tab_ready, 1)
            pe.wait_ge(s_w1, 16 * E)

            def take_in(i, u):
                pe.wait_ge(sl_in[u], START + 16 * (i + 1))
                pe.wait_ge(slT_ready[u], START + i)
                for kt in range(KT):
                    ins = pe.transpose(tb[u][:, kt * P:(kt + 1) * P], sl[u][:, kt * P:(kt + 1) * P], ident[:, :])
                ins.then_inc(slT_ps[u], 1)

            hid = [[mb[0], mb[1]], [ring[0], ring[1]]]

            def hidden(j, i, u):
                e = pe.value_load(tile_w[0:1, bass.ds(j, 1)], min_val=0, max_val=E - 1)
                pe.wait_ge(slT_ready[u], START + i + 1)
                pe.wait_ge(gh_ready[u], START + i)
                for m in (1, 0):
                    for kt in range(KT):
                        ins = pe.matmul(hid[u][m][:, :], slT[u][:, kt, :],
                                        w_1[:, bass.ds(e, 1), kt, m * F:(m + 1) * F].rearrange("p e f -> p (e f)"),
                                        start=(kt == 0), stop=(kt == KT - 1))
                    ins.then_inc(hh_ps[u], 1)

            def back(i, u, last_i):
                pe.wait_ge(gh_ready[u], START + i + 1)
                pe.wait_ge(ghT_ready[1 - u], START + last_i)
                for a in range(FT):
                    ins = pe.transpose(ring[2][:, a * P:(a + 1) * P], g_h[u][:, a * P:(a + 1) * P], ident[:, :])
                ins.then_inc(ghT_ps[u], 1)
                pe.wait_ge(ghT_ready[u], START + i + 1)
                pe.wait_ge(os_ready[1 - u], START + last_i)
                for a in range(FT):
                    ins = pe.matmul(ring[3][:, 0:D], g_hT[u][:, a, :], w_o[:, a, :],
                                    start=(a == 0), stop=(a == FT - 1))
                ins.then_inc(os_ps[u], 1)

            take_in(0, 0)
            hidden(0, 0, 0)
            take_in(0, 1)
            hidden(1, 0, 1)
            take_in(1, 0)
            back(0, 0, 0)
            with pe.Fori(1, TILES // 2) as i:
                hidden(2 * i, i, 0)
                take_in(i, 1)
                back(i - 1, 1, i)
                hidden(2 * i + 1, i, 1)
                take_in(i + 1, 0)
                back(i, 0, i)
            hidden(TILES - 1, TILES // 2, 0)
            back(TILES // 2 - 1, 1, TILES // 2)
            back(TILES // 2, 0, TILES // 2)

        @block.vector
        def _(dve):
            start(dve, var_ready, z_ready, g_ready, xr_ready, xk_ready, v_ready, x2_done, max_done, mx_ready, att_ready, dl_ready,
                  oh_ready, slot_ready, gate_ready, gh_ready, val_ready, fidx_ready, half_y, y_ready)
            dve.wait_ge(s_init, 7)
            dve.wait_ge(s_small, 176)
            dve.tensor_copy(fill[:, :], iotas[:, 1, :]).then_inc(s_const, 1)
            dve.wait_ge(s_tg, 1)
            dve.tensor_scalar(rows[:, 1, :], rows[:, 1, :], tg[:, 2:3], None, ALU.mult)
            dve.tensor_scalar(rows[:, 2, :], rows[:, 2, :], tg[:, 3:4], None, ALU.mult)
            dve.tensor_scalar(half_tg[:, :], tg[:, 1:2], 0.5, None, ALU.mult).then_inc(s_const, 1)
            dve.wait_ge(s_const, 2)

            with dve.Fori(0, IT) as i:
                c = Steps(dve, vec_step, VEC_STEPS * i)

                def statistics(k, u):
                    for t in range(TT):
                        c.done(dve.bn_stats(stats[u][:, t, :], x[u][:, t, :]))
                    c.wait()
                    dve.memset(carrier[:, 0:1], 0.0)
                    for t in range(TT):
                        c.done(dve.bn_aggr(mv[u][:, t, :], stats[u][:, t, :]))
                    c.wait()
                    dve.tensor_scalar(vare[u][:, :], mv[u][:, :, 1], EPS, None, ALU.add).then_inc(var_ready[u], 1)

                def normalise(k, u):
                    dve.wait_ge(rstd_ready[u], START + 4 * i + k + 1)
                    dve.wait_ge(zT_ps[u], START + 4 * i + k)
                    if k == 0:
                        dve.wait_ge(z_free[u], START + i)
                    for t in range(TT):
                        ins = dve.tensor_scalar(z[u][:, t, :], x[u][:, t, :], mv[u][:, t, 0:1], rstd[u][:, t:t + 1],
                                                ALU.subtract, ALU.mult)
                    ins.then_inc(z_ready[u], 1)

                for u in range(2):
                    dve.wait_ge(x_in[u], START + 16 * (i + 1))
                    statistics(0, u)
                for u in range(2):
                    normalise(0, u)
                for u in range(2):
                    dve.wait_ge(ge_ready[u], START + i + 1)
                    dve.wait_ge(o_ps[u], START + i)
                    dve.tensor_tensor(gT[u][:, :], ge[u][:, :], mb[u][0:C, 0:T], ALU.mult).then_inc(g_ready[u], 1)
                for u in range(2):
                    dve.wait_ge(o_ps[u], START + i + 1)
                    c.done(dve.scalar_tensor_tensor(flat(x[u][:, :, :]), mb[u][:, :], tg[:, 0:1], flat(x[u][:, :, :]),
                                                    ALU.mult, ALU.add))
                    c.wait()
                    statistics(1, u)
                for u in range(2):
                    normalise(1, u)
                for u in range(2):
                    dve.wait_ge(aT_ready[u], START + 4 * i + 2)
                    dve.wait_ge(xk_ready[1 - u], START + i + u)
                    cur, prev = aTs[u][:, :, 1:T + 1], aTs[u][:, :, 0:T]
                    c.done(dve.tensor_tensor(diff[:, :, :], cur, prev, ALU.subtract))
                    c.wait()
                    dve.wait_ge(st_ps, START + 16 * i)
                    dve.wait_ge(q16_ready[u], START + i)
                    for dst, m, s in ((xr, 0, xr_ready), (xk, 1, xk_ready)):
                        for k in range(KT):
                            ins = dve.scalar_tensor_tensor(dst[u][:, k, :], diff[:, k, :], chan[:, m, k:k + 1],
                                                           prev[:, k, :], ALU.mult, ALU.add)
                        ins.then_inc(s[u], 1)
                for u in range(2):
                    dve.wait_ge(y_ps[u], START + i + 1)
                    dve.wait_ge(th_ready[u], START + i + 1)
                    c.done(dve.scalar_tensor_tensor(flat(yb[u][:, :, :]), flat(th[u][:, :, :]), 1.0, mb[u][:, :],
                                                    ALU.add, ALU.mult))
                    c.wait()
                    dve.scalar_tensor_tensor(flat(x[u][:, :, :]), flat(yb[u][:, :, :]), half_tg[:, 0:1],
                                             flat(x[u][:, :, :]), ALU.mult, ALU.add).then_inc(x2_done[u], 1)
                    dve.wait_ge(x2_done[u], START + i + 1)
                    statistics(2, u)
                for u in range(2):
                    normalise(2, u)
                for u in range(2):
                    dve.wait_ge(v_ps[u], START + i + 1)
                    dve.wait_ge(pv_done, START + 16 * i)
                    dve.tensor_tensor(v[u][:, :, 0:HD], mb[u][0:C, 0:D].rearrange("p (h c) -> p h c", h=H),
                                      rows[0:C, 0, :].rearrange("p (h c) -> p h c", h=H), ALU.add)\
                        .then_inc(v_ready[u], 1)
                for u in range(2):
                    for n in range(8):
                        t, hq = n // 4, n % 4
                        dve.wait_ge(s_ps, START + 16 * i + 8 * u + n + 1)
                        dve.tensor_reduce(mx[u][:, t, 4 * hq:4 * hq + 4],
                                          ring[n % 4][:, 0:4 * C].rearrange("p (h c) -> p h c", h=4),
                                          AX_X, ALU.max).then_inc(max_done, 1)
                    dve.wait_ge(max_done, START + 16 * i + 8 * u + 8)
                    dve.wait_ge(mT_ps[u], START + i)
                    dve.tensor_copy(flat(mx16[u][:, :, :]), flat(mx[u][:, :, :])).then_inc(mx_ready[u], 1)
                for u in range(2):
                    dve.wait_ge(pv_done, START + 16 * i + 8 * u + 8)
                    for t in range(TT):
                        ps = (mb, tb)[t][u][:, 0:H * (HD + 1)].rearrange("p (h c) -> p h c", h=H)
                        c.done(dve.reciprocal(rden[u][:, t, :], ps[:, :, HD]))
                    c.wait()
                    for t in range(TT):
                        ps = (mb, tb)[t][u][:, 0:H * (HD + 1)].rearrange("p (h c) -> p h c", h=H)
                        ins = dve.tensor_tensor(att[u][:, t, :].rearrange("p (h c) -> p h c", h=H), ps[:, :, 0:HD],
                                                rden[u][:, t, :].unsqueeze(2).to_broadcast([P, H, HD]), ALU.mult)
                    ins.then_inc(att_ready[u], 1)
                for u in range(2):
                    dve.wait_ge(out_ps[u], START + i + 1)
                    dve.wait_ge(x2b_ready[u], START + TT * (i + 1))
                    c.done(dve.scalar_tensor_tensor(flat(x[u][:, :, :]), mb[u][:, :], tg[:, 2:3], flat(x[u][:, :, :]),
                                                    ALU.mult, ALU.add))
                    c.wait()
                    statistics(3, u)
                for u in range(2):
                    normalise(3, u)

                for u in range(2):
                    dve.wait_ge(lg_ps[u], START + i + 1)
                    c.done(dve.tensor_copy(flat(lg[u][:, :, :]), mb[u][:, 0:TT * E]))
                    c.wait()
                    dve.memset(carrier[:, 0:1], 0.0)
                    for t in range(TT):
                        c.done(dve.max(top[u][:, t, :], lg[u][:, t, :]))
                    c.wait()
                    for t in range(TT):
                        dve.tensor_scalar(dl[u][:, t, 0:E], lg[u][:, t, :], top[u][:, t, 0:1], None, ALU.subtract)
                        dve.tensor_scalar(dl[u][:, t, E:E + 1], top[u][:, t, 1:2], top[u][:, t, 0:1], None,
                                          ALU.subtract).then_inc(dl_ready[u], 1) if t == TT - 1 else \
                            dve.tensor_scalar(dl[u][:, t, E:E + 1], top[u][:, t, 1:2], top[u][:, t, 0:1], None,
                                              ALU.subtract)
                        c.done(dve.max_index(topi[u][:, t, :], top[u][:, t, :], lg[u][:, t, :]))
                    c.wait()
                    c.done(dve.tensor_copy(topf[u][:, :, :], topi[u][:, :, 0:TOPK].rearrange("p t k -> p k t")))
                    c.wait()
                    for k in range(TOPK):
                        for t in range(TT):
                            c.done(dve.tensor_scalar(oh[u][:, k, t, :], iotas[:, 0, :], topf[u][:, k, t:t + 1], None,
                                                     ALU.is_equal))
                    c.wait()
                    dve.tensor_tensor(chosen[u][:, :, :], oh[u][:, 0, :, :], oh[u][:, 1, :, :], ALU.add)\
                        .then_inc(oh_ready[u], 1)
                for u in range(2):
                    dve.wait_ge(el_ready[u], START + i + 1)
                    c.done(dve.tensor_reduce(zsum[u][:, :], el[u][:, :, 0:E], AX_X, ALU.add))
                    c.wait()
                    c.done(dve.scalar_tensor_tensor(den[u][:, :], zsum[u][:, :], 1e-9, el[u][:, :, E], ALU.mult, ALU.add))
                    c.wait()
                    c.done(dve.tensor_scalar(zsum[u][:, :], den[u][:, :], 1.0, None, ALU.add))
                    c.wait()
                    c.done(dve.reciprocal(den[u][:, :], zsum[u][:, :]))
                    c.wait()
                    dve.tensor_scalar(wk[u][:, :, 0], den[u][:, :], tg[:, 3:4], None, ALU.mult)
                    c.done(dve.scalar_tensor_tensor(wk[u][:, :, 1], den[u][:, :], tg[:, 3:4], el[u][:, :, E],
                                                    ALU.mult, ALU.mult))
                    c.done(dve.scalar_tensor_tensor(wsum[u][:, :], el[u][:, :, E], 1.0, den[u][:, :], ALU.add, ALU.mult))
                    c.wait()
                    dve.tensor_copy(wres[:, bass.ds(2 * i + u, 1), :, :].rearrange("p n t k -> p (n t k)"),
                                    flat(wk[u][:, :, :]))
                    dve.wait_ge(rank_ps[u], START + i + 1)
                    rank = mb[u][:, TT * E:2 * TT * E].rearrange("p (t e) -> p t e", t=TT)
                    count = mb[u][:, 2 * TT * E:3 * TT * E].rearrange("p (t e) -> p t e", t=TT)
                    dve.tensor_tensor(pos[u][:, 0, :], fill[:, :], rank[:, 0, :], ALU.add)
                    c.done(dve.tensor_tensor(fill1[:, :], fill[:, :], count[:, 0, :], ALU.add))
                    c.wait()
                    dve.tensor_tensor(pos[u][:, 1, :], fill1[:, :], rank[:, 1, :], ALU.add)
                    c.done(dve.tensor_tensor(fill[:, :], fill1[:, :], count[:, 1, :], ALU.add))
                    c.wait()
                    for k in range(TOPK):
                        c.done(dve.tensor_tensor(ohpos[u][:, k, :, :], oh[u][:, k, :, :], pos[u][:, :, :], ALU.mult))
                    c.wait()
                    dve.wait_ge(z_free[u], START + i)
                    c.done(dve.tensor_reduce(slotf[u][:, :], ohpos[u][:, :, :, :].rearrange("p k t e -> p (k t) e"),
                                             AX_X, ALU.add))
                    c.wait()
                    dve.tensor_copy(slotres[:, bass.ds(2 * i + u, 1), :].rearrange("p n s -> p (n s)"), slotf[u][:, :])
                    dve.tensor_copy(expres[:, bass.ds(2 * i + u, 1), :].rearrange("p n s -> p (n s)"),
                                    flat(topf[u][:, :, :]))
                    for t in range(TT):
                        dve.scalar_tensor_tensor(
                            xres[:, bass.ds(2 * i + u, 1), t, :].rearrange("p n d -> p (n d)"), rows[:, 2, :],
                            wsum[u][:, t:t + 1], x[u][:, t, :], ALU.mult, ALU.add)
                    dve.tensor_copy(slot[u][:, :], slotf[u][:, :]).then_inc(slot_ready[u], 1)
                assert c.n == VEC_STEPS, c.n

            c = Steps(dve, tab_step, 0)
            c.done(dve.tensor_copy(fill_i[:, :], fill[0:1, :]))
            c.done(dve.tensor_tensor(filled[:, :], fill[:, :], iotas[:, 1, :], ALU.subtract))
            c.wait()
            c.done(dve.tensor_scalar(filled_i[:, :], filled[:, :], float(P - 1), None, ALU.add))
            c.wait()
            c.done(dve.tensor_scalar(filled_i[:, :], filled_i[:, :], 7, None, ALU.arith_shift_right))
            c.wait()
            c.done(dve.tensor_copy(ntiles[:, :], filled_i[:, :]))
            c.wait()
            c.done(dve.tensor_tensor_scan(cum[:, :], ones_row[:, :], ntiles[:, :], 0.0, ALU.mult, ALU.add))
            c.wait()
            wide = [1, TILES, E]
            c.done(dve.tensor_tensor(past[:, :, :], cum[0:1, :].unsqueeze(1).to_broadcast(wide),
                                     tile_no[:, 0:TILES].unsqueeze(2).to_broadcast(wide), ALU.is_le))
            c.wait()
            c.done(dve.tensor_tensor(pastn[:, :, :], past[:, :, :], ntiles[0:1, :].unsqueeze(1).to_broadcast(wide), ALU.mult))
            c.done(dve.tensor_reduce(tile_e[:, :], past[:, :, :], AX_X, ALU.add))
            c.wait()
            c.done(dve.tensor_reduce(tile_c[:, :], pastn[:, :, :], AX_X, ALU.add))
            c.done(dve.tensor_scalar(tile_w[:, :], tile_e[:, :], float(E - 1), None, ALU.min))
            c.wait()
            c.done(dve.tensor_tensor(tile_c[:, :], tile_no[:, 0:TILES], tile_c[:, :], ALU.subtract))
            c.done(dve.tensor_scalar(tile_e[:, :], tile_e[:, :], float(CAP), None, ALU.mult))
            c.wait()
            c.done(dve.scalar_tensor_tensor(tile_r[:, :], tile_c[:, :], float(P), tile_e[:, :], ALU.mult, ALU.add))
            c.wait()
            dve.tensor_copy(filled[:, :], ntiles[:, :]).then_inc(tab_ready, 1)

            c.wait()
            c.done(dve.tensor_tensor(shift[:, :], cum[:, :], ntiles[:, :], ALU.subtract))
            c.wait()
            c.done(dve.scalar_tensor_tensor(shift[:, :], shift[:, :], float(P), iotas[:, 1, :], ALU.mult, ALU.subtract))
            wide = [P, B * TOPK * TT, E]
            c.done(dve.tensor_tensor(moved, flat(expres[:, :, :]).unsqueeze(2).to_broadcast(wide),
                                     iotas[:, 0, :].unsqueeze(1).to_broadcast(wide), ALU.is_equal))
            c.wait()
            c.done(dve.tensor_tensor(moved, moved, shift[:, :].unsqueeze(1).to_broadcast(wide), ALU.mult))
            c.wait()
            c.done(dve.tensor_reduce(flat(expres[:, :, :]), moved, AX_X, ALU.add))
            c.wait()
            c.done(dve.tensor_tensor(flat(packed[:, :, :]), flat(expres[:, :, :]), flat(slotres[:, :, :]), ALU.add))
            c.wait()

            hid = [[mb[0], mb[1]], [ring[0], ring[1]]]
            dve.wait_ge(s_b1, 32)
            dve.wait_ge(tab_ready, 1)

            def glu(j, i, u):
                e = dve.value_load(tile_w[0:1, bass.ds(j, 1)], min_val=0, max_val=E - 1)

                def bias(m):
                    return b_1[:, bass.ds(e, 1), m * F:(m + 1) * F].rearrange("p e f -> p (e f)")

                dve.wait_ge(hh_ps[u], START + 2 * i + 1)
                dve.wait_ge(sig_ready[u], START + i)
                dve.tensor_tensor(gate_h[u], hid[u][1][:, :], bias(1), ALU.add).then_inc(gate_ready[u], 1)
                dve.wait_ge(hh_ps[u], START + 2 * i + 2)
                dve.tensor_tensor(val_h[u], hid[u][0][:, :], bias(0), ALU.add).then_inc(val_ready[u], 1)
                dve.wait_ge(val_ready[u], START + i + 1)
                dve.wait_ge(sig_ready[u], START + i + 1)
                dve.wait_ge(ghT_ps[u], START + i)
                dve.tensor_tensor(g_h[u], val_h[u], sig_h[u], ALU.mult).then_inc(gh_ready[u], 1)

            with dve.Fori(0, TILES // 2) as i:
                for u in range(2):
                    glu(2 * i + u, i, u)
            glu(TILES - 1, TILES // 2, 0)

            def indices(i, u):
                dve.tensor_copy(slot[u][:, :], packed[:, bass.ds(2 * i + u, 1), :].rearrange(
                    "p n s -> p (n s)")).then_inc(fidx_ready[u], 1)

            def combine(i, u, more):
                dve.wait_ge(fetched[u], 16 * TOPK * TT * (i + 1))
                if more:
                    indices(i + 1, u)
                dve.wait_ge(y_out_done[u], START + 16 * i)
                for k in range(TOPK):
                    for t in range(TT):
                        base = (xres[:, bass.ds(2 * i + u, 1), t, :].rearrange("p n d -> p (n d)") if k == 0
                                else y_out[u][:, t, :])
                        ins = dve.scalar_tensor_tensor(
                            y_out[u][:, t, :], got[u][:, k * TT + t, :],
                            wres[:, bass.ds(2 * i + u, 1), t, k:k + 1].rearrange("p n k -> p (n k)"), base,
                            ALU.mult, ALU.add)
                    if k == 0:
                        ins.then_inc(half_y[u], 1)
                        dve.wait_ge(half_y[u], START + i + 1)
                ins.then_inc(y_ready[u], 1)

            for u in range(2):
                indices(0, u)
            with dve.Fori(0, IT - 1) as i:
                for u in range(2):
                    combine(i, u, True)
            for u in range(2):
                combine(IT - 1, u, False)


def kernel(x, ctx_1024, g_xattn, g_ffn, L0_ffn_W_r, L0_ffn_W_k, L0_ffn_W_v, L0_ffn_mu_r, L0_ffn_mu_k,
           L1_xattn_w_q, L1_xattn_b_q, L1_xattn_w_kv, L1_xattn_b_kv, L1_xattn_w_out, L1_xattn_b_out,
           L1_ffn_Wg, L1_ffn_W1, L1_ffn_b1, L1_ffn_Wo, L1_ffn_bo):
    import ml_dtypes
    import concourse.bacc as bacc
    from concourse.bass_utils import run_bass_kernel_spmd

    def blocks(w):
        w = np.asarray(w)
        return np.ascontiguousarray(w.reshape(-1, P, w.shape[1]).transpose(1, 0, 2))

    def every(a):
        a = np.asarray(a)
        return np.ascontiguousarray(np.broadcast_to(a[None], (P,) + a.shape))

    def per_channel(a):
        return np.asarray(a).reshape(KT, P).T

    f32, bf16 = np.float32, ml_dtypes.bfloat16
    tri = np.triu(np.ones((P, P), f32), 1)
    negsel = np.zeros((H, H, C), f32)
    negsel[np.arange(H), np.arange(H)] = -1.0
    arrays = {
        "x": np.asarray(x),
        "ctx": np.asarray(ctx_1024),
        "ctxT": np.ascontiguousarray(np.asarray(ctx_1024).transpose(0, 2, 1)),
        "gates": every(np.stack([np.asarray(g)[l] for l in range(2) for g in (g_xattn, g_ffn)])),
        "w_r": blocks(np.asarray(L0_ffn_W_r).T),
        "w_k": blocks(np.asarray(L0_ffn_W_k).T),
        "w_v": blocks(np.asarray(L0_ffn_W_v).T),
        "w_q": blocks(L1_xattn_w_q),
        "w_kv": blocks(L1_xattn_w_kv),
        "w_out": blocks(L1_xattn_w_out),
        "w_g": blocks(np.asarray(L1_ffn_Wg).T),
        "w_o": blocks(np.asarray(L1_ffn_Wo).T),
        "w_1": np.ascontiguousarray(np.asarray(L1_ffn_W1).transpose(0, 2, 1)),
        "b_1": every(L1_ffn_b1),
        "chan": np.ascontiguousarray(np.stack(
            [per_channel(a) for a in (L0_ffn_mu_r, L0_ffn_mu_k, L1_xattn_b_q, np.asarray(L1_xattn_b_kv)[:D])], 1)),
        "rows": every(np.stack([np.asarray(L1_xattn_b_kv)[D:], np.asarray(L1_xattn_b_out), np.asarray(L1_ffn_bo)])),
        "ident": np.eye(P, dtype=f32),
        "ident16": np.eye(P, dtype=f32).astype(bf16),
        "tri_ones": np.ascontiguousarray(np.stack([tri, np.ones((P, P), f32)], 1)).astype(bf16),
        "headmask": (np.arange(P)[:, None] // HD == np.arange(HB)[None]).astype(f32),
        "negsel": negsel.astype(bf16),
        "iotas": every(np.stack([np.arange(E), np.arange(E) * CAP]).astype(f32)),
        "tile_no": np.arange(TILES + 1, dtype=f32)[None],
    }
    nc = bacc.Bacc("TRN2", target_bir_lowering=False, num_devices=1)
    feed, d = {}, {}
    for name, a in arrays.items():
        feed[f"in_{name}"] = a
        d[name] = nc.dram_tensor(f"in_{name}", a.shape, mybir.dt.from_np(a.dtype), kind="ExternalInput").ap()
    out = nc.dram_tensor("out_0_dram", (B, T, D), F32, kind="ExternalOutput").ap()
    build(nc, d, out)
    return run_bass_kernel_spmd(nc, [feed], core_ids=[0]).results[0]["out_0_dram"]
```

```python
from contextlib import ExitStack

import numpy as np

import concourse.bass as bass
from concourse import mybir
from concourse.alu_op_type import AluOpType as ALU

F32 = mybir.dt.float32
BF16 = mybir.dt.bfloat16
U32 = mybir.dt.uint32
I32 = mybir.dt.int32
ACT = mybir.ActivationFunctionType
AX_X = mybir.AxisListType.X

P = 128
B, T, D = 8, 256, 256
KT = D // P
TT = T // P
C = 77
H, HD = 16, 16
HB = P // HD
E, TOPK = 8, 2
F = 512
FT = F // P
IT = B // 2
EPS = 1e-5
CAP = B * T + P
TILES = (B * T * TOPK + E * (P - 1)) // P
IDLE = TILES - B * T * TOPK // P
SLOTS = E * CAP + IDLE * P
START = 1
VEC_STEPS = 84


def start(eng, *sems):
    for s in sems:
        for one in s if isinstance(s, list) else [s]:
            eng.sem_inc(one, START)


class Steps:

    def __init__(self, eng, sem, base):
        self.eng, self.sem, self.base, self.n = eng, sem, base, 0

    def done(self, instruction):
        self.n += 1
        instruction.then_inc(self.sem, 1)

    def wait(self):
        self.eng.wait_ge(self.sem, self.base + self.n)


def build(nc, d, out):
    with ExitStack() as ctx:
        def sb(name, shape, dt=F32):
            return ctx.enter_context(nc.sbuf_tensor(name, shape, dt))

        def sem(name):
            return ctx.enter_context(nc.semaphore(name))

        def pair(make, name, *a):
            return [make(f"{name}{u}", *a) for u in range(2)]

        w_r, w_k, w_v, w_q, w_out = (sb(n, [P, KT, D]) for n in ("w_r", "w_k", "w_v", "w_q", "w_out"))
        w_kv = sb("w_kv", [P, KT, 2 * D])
        w_g = sb("w_g", [P, KT, E])
        w_o = sb("w_o", [P, FT, D])
        w_1 = sb("w_1", [P, E, KT, 2 * F])
        b_1 = sb("b_1", [P, E, 2 * F])
        chan = sb("chan", [P, 4, KT])
        rows = sb("rows", [P, 3, D])
        gates = sb("gates", [P, 4])
        tg = sb("tg", [P, 4])
        half_tg = sb("half_tg", [P, 1])
        ident = sb("ident", [P, P])
        tri_ones16 = sb("tri_ones16", [P, 2, P], BF16)
        ident16 = sb("ident16", [P, P], BF16)
        headmask = sb("headmask", [P, HB])
        negsel16 = sb("negsel16", [H, H, C], BF16)
        iotas = sb("iotas", [P, 2, E])
        tile_no = sb("tile_no", [1, TILES + 1])
        half_power = sb("half_power", [P, TT])
        zeros = sb("zeros", [P, D])
        carrier = sb("carrier", [P, 9])
        x = pair(sb, "x", [P, TT, D])
        z = pair(sb, "z", [P, TT, D])
        stats = pair(sb, "stats", [P, TT, 6])
        mv = pair(sb, "mv", [P, TT, 2])
        vare = pair(sb, "vare", [P, TT])
        rstd = pair(sb, "rstd", [P, TT])
        cx = pair(sb, "cx", [C, D])
        cxT = pair(sb, "cxT", [P, KT, C])
        aT = pair(sb, "aT", [P, KT, T])
        aTs = pair(sb, "aTs", [P, KT, T + 1])
        lower = b_1[:, 0:E // 2, :].rearrange("p e f -> p (e f)")
        diff = lower[:, 0:KT * T].rearrange("p (k t) -> p k t", k=KT)
        ge = [lower[0:C, KT * T + u * T:KT * T + (u + 1) * T] for u in range(2)]
        gT = [lower[0:C, (KT + 2) * T + u * T:(KT + 2) * T + (u + 1) * T] for u in range(2)]
        kT = pair(sb, "kT", [P, KT, C])
        kbd = pair(sb, "kbd", [P, H, C])
        kbd16 = pair(sb, "kbd16", [P, H, C], BF16)
        v = pair(sb, "v", [C, H, HD + 1])
        xr = pair(sb, "xr", [P, KT, T])
        xk = pair(sb, "xk", [P, KT, T])
        th = pair(sb, "th", [P, TT, D])
        ka = pair(sb, "ka", [P, KT, T])
        qT16 = pair(sb, "qT16", [P, KT, T], BF16)
        mx = pair(sb, "mx", [P, TT, H])
        mx16 = pair(sb, "mx16", [P, TT, H], BF16)
        mT = pair(sb, "mT", [H, T], BF16)
        probs = b_1[0:C, E // 2:E, :].rearrange("p e f -> p (e f)").rearrange("p (c h t) -> p c h t", h=2, t=T)
        rden = pair(sb, "rden", [P, TT, H])
        yb, qT, att, attT = xr, xk, th, aTs
        z3 = pair(sb, "z3", [P, TT, D])
        stats3 = pair(sb, "stats3", [P, TT, 6])
        mv3 = pair(sb, "mv3", [P, TT, 2])
        vare3 = pair(sb, "vare3", [P, TT])
        rstd3 = pair(sb, "rstd3", [P, TT])
        lg = pair(sb, "lg", [P, TT, E])
        top = pair(sb, "top", [P, TT, 8])
        topi = pair(sb, "topi", [P, TT, 8], U32)
        topf = pair(sb, "topf", [P, TOPK, TT])
        dl = pair(sb, "dl", [P, TT, E + 1])
        el = pair(sb, "el", [P, TT, E + 1])
        zsum = pair(sb, "zsum", [P, TT])
        den = pair(sb, "den", [P, TT])
        wk = pair(sb, "wk", [P, TT, TOPK])
        wsum = pair(sb, "wsum", [P, TT])
        oh = pair(sb, "oh", [P, TOPK, TT, E])
        chosen = pair(sb, "chosen", [P, TT, E], BF16)
        pos = pair(sb, "pos", [P, TT, E])
        ohpos = pair(sb, "ohpos", [P, TOPK, TT, E])
        slotf = pair(sb, "slotf", [P, TOPK * TT])
        ranks = pair(sb, "ranks", [P, 2, TT, E])
        slot = pair(sb, "slot", [P, TOPK * TT], U32)
        fill = sb("fill", [P, E])
        fill1 = sb("fill1", [P, E])
        xres = sb("xres", [P, B, TT, D])
        wres = sb("wres", [P, B, TT, TOPK])
        slotres = sb("slotres", [P, B, TOPK * TT])
        expres = sb("expres", [P, B, TOPK * TT])
        packed = sb("packed", [P, B, TOPK * TT], U32)
        filled = sb("filled", [P, E])
        filled_i = sb("filled_i", [P, E], I32)
        fill_i = sb("fill_i", [1, E], I32)
        ntiles = sb("ntiles", [P, E])
        ones_row = sb("ones_row", [P, E])
        cum = sb("cum", [P, E])
        shift = sb("shift", [P, E])
        moved = kbd[0][:, :, :].rearrange("p h c -> p (h c)")[:, 0:B * TOPK * TT * E].rearrange(
            "p (s e) -> p s e", e=E)
        past = sb("past", [1, TILES, E])
        pastn = sb("pastn", [1, TILES, E])
        tile_e = sb("tile_e", [1, TILES])
        tile_c = sb("tile_c", [1, TILES])
        tile_w = sb("tile_w", [1, TILES], I32)
        tile_r = sb("tile_r", [1, TILES], I32)
        sl = [x[u][:, 0, :] for u in range(2)]
        slT = [aT[u][:, :, 0:P] for u in range(2)]
        gate_h = [xr[u][:, :, :].rearrange("p a b -> p (a b)") for u in range(2)]
        val_h = [xk[u][:, :, :].rearrange("p a b -> p (a b)") for u in range(2)]
        sig_h = [ka[u][:, :, :].rearrange("p a b -> p (a b)") for u in range(2)]
        g_h = [th[u][:, :, :].rearrange("p a b -> p (a b)") for u in range(2)]
        g_hT = [aTs[u][:, :, :].rearrange("p a b -> p (a b)")[:, 0:F].rearrange("p (a b) -> p a b", a=FT)
                for u in range(2)]
        o_s = [x[u][:, 1, :] for u in range(2)]
        got = [kbd[u][:, :, :].rearrange("p h c -> p (h c)")[:, 0:TOPK * TT * D].rearrange(
            "p (s d) -> p s d", d=D) for u in range(2)]
        y_out = [xr[u] for u in range(2)]

        bank = [ctx.enter_context(nc.psum_tensor(f"bank{i}", [P, 512], F32)) for i in range(8)]
        tb, mb, ring = bank[0:2], bank[2:4], bank[4:8]

        slots_dram = nc.dram_tensor("slots_dram", (SLOTS, D), F32, kind="Internal").ap()
        outs_dram = nc.dram_tensor("outs_dram", (TILES * P, D), F32, kind="Internal").ap()

        s_first, s_small, s_w, s_w1, s_b1 = (sem(n) for n in ("s_first", "s_small", "s_w", "s_w1", "s_b1"))
        s_const = sem("s_const")
        s_tg = sem("s_tg")
        s_idle = sem("s_idle")
        x_in, cx_in = pair(sem, "x_in"), pair(sem, "cx_in")
        var_ready, rstd_ready = pair(sem, "var_ready"), pair(sem, "rstd_ready")
        z_ready, zT_ps, aT_ready = pair(sem, "z_ready"), pair(sem, "zT_ps"), pair(sem, "aT_ready")
        h_ps, ge_ready, g_ready = pair(sem, "h_ps"), pair(sem, "ge_ready"), pair(sem, "g_ready")
        k_ps, kT_ready, kbd_ready = pair(sem, "k_ps"), pair(sem, "kT_ready"), pair(sem, "kbd_ready")
        o_ps = pair(sem, "o_ps")
        xr_ready, xk_ready = pair(sem, "xr_ready"), pair(sem, "xk_ready")
        r_ps, th_ready, kk_ps, rk_ready, ka_ready = (
            pair(sem, n) for n in ("r_ps", "th_ready", "kk_ps", "rk_ready", "ka_ready"))
        y_ps, v_ps, v_ready = pair(sem, "y_ps"), pair(sem, "v_ps"), pair(sem, "v_ready")
        x2_done = pair(sem, "x2_done")
        q_ps, q_ready, q16_ready, kbd16_ready = (pair(sem, n) for n in ("q_ps", "q_ready", "q16_ready", "kbd16_ready"))
        s_ps, max_done = sem("s_ps"), sem("max_done")
        mx_ready, mT_ps, mT_ready = pair(sem, "mx_ready"), pair(sem, "mT_ps"), pair(sem, "mT_ready")
        st_ps, exp_done, pv_done = sem("st_ps"), sem("exp_done"), sem("pv_done")
        att_ready, attT_ps, attT_ready, out_ps = (pair(sem, n) for n in ("att_ready", "attT_ps", "attT_ready", "out_ps"))
        var3_ready, rstd3_ready, z3_ready, z3T_ps, aT3_ready = (
            pair(sem, n) for n in ("var3_ready", "rstd3_ready", "z3_ready", "z3T_ps", "aT3_ready"))
        lg_ps, dl_ready, el_ready, oh_ready, rank_ps, slot_ready = (
            pair(sem, n) for n in ("lg_ps", "dl_ready", "el_ready", "oh_ready", "rank_ps", "slot_ready"))
        rank_taken = pair(sem, "rank_taken")
        sent, z3_free = pair(sem, "sent"), pair(sem, "z3_free")
        vec_step = sem("vec_step")
        tab_step, tab_ready, pad_done = sem("tab_step"), sem("tab_ready"), sem("pad_done")
        sl_in, slT_ps, slT_ready, hh_ps, gate_ready, sig_ready, gh_ready = (
            pair(sem, n) for n in ("sl_in", "slT_ps", "slT_ready", "hh_ps", "gate_ready", "sig_ready", "gh_ready"))
        val_ready = pair(sem, "val_ready")
        ghT_ps, ghT_ready, os_ps, os_ready, os_out = (
            pair(sem, n) for n in ("ghT_ps", "ghT_ready", "os_ps", "os_ready", "os_out"))
        fidx_ready, fetched, half_y, y_ready, y_out_done = (
            pair(sem, n) for n in ("fidx_ready", "fetched", "half_y", "y_ready", "y_out_done"))
        s_init = sem("s_init")
        carried = pair(sem, "carried")
        block = ctx.enter_context(nc.Block())

        def m_tok(u):
            return mb[u][:, :].rearrange("p (t d) -> p t d", t=TT)

        def t_chan(u):
            return tb[u][:, :].rearrange("p (k t) -> p k t", k=KT)

        def flat(a):
            return a.rearrange("p a b -> p (a b)")


        @block.sync
        def _(sp):
            def load_x(n, u):
                sp.dma_start(x[u][:, :, :], d["x"][bass.ds(n, 1), :, :].rearrange(
                    "n (t p) d -> p (n t) d", p=P)).then_inc(x_in[u], 16)

            def load_context(n, u):
                sp.dma_start(cxT[u][:, :, :], d["ctxT"][bass.ds(n, 1), :, :].rearrange(
                    "n (k p) c -> p (n k) c", p=P)).then_inc(cx_in[u], 16)
                sp.dma_start(cx[u][:, :], d["ctx"][bass.ds(n, 1), :, :].rearrange(
                    "n c d -> (n c) d")).then_inc(cx_in[u], 16)

            def load_expert(e):
                sp.dma_start(w_1[:, bass.ds(e, 1), :, :].rearrange("p e k f -> p (e k) f"),
                             d["w_1"][bass.ds(e, 1), :, :].rearrange("e (k p) f -> p (e k) f", p=P)).then_inc(s_w1, 16)

            start(sp, x_in, cx_in, sl_in, y_out_done)
            for u in range(2):
                load_x(u, u)
            for u in range(2):
                load_context(u, u)
            for t, n in ((rows, "rows"), (headmask, "headmask"), (w_g, "w_g"), (ident16, "ident16"),
                         (negsel16, "negsel"), (tri_ones16, "tri_ones"), (iotas, "iotas"), (tile_no, "tile_no")):
                sp.dma_start(t[:], d[n]).then_inc(s_small, 16)
            with sp.Fori(0, IT - 1) as i:
                for u in range(2):
                    sp.wait_ge(x2_done[u], START + i + 1)
                    load_x(2 * i + 2 + u, u)
                for u in range(2):
                    sp.wait_ge(v_ps[u], START + i + 1)
                    sp.wait_ge(o_ps[u], START + i + 1)
                    load_context(2 * i + 2 + u, u)
                for j in range(2):
                    load_expert(2 * i + j)
            for e in range(2 * (IT - 1), E):
                load_expert(e)
            for u in range(2):
                sp.wait_ge(xk_ready[u], START + IT)
                sp.wait_ge(o_ps[u], START + IT)
            sp.dma_start(b_1[:, 0:E // 2, :], d["b_1"][:, 0:E // 2, :]).then_inc(s_b1, 16)
            sp.wait_ge(pv_done, START + 16 * IT)
            sp.dma_start(b_1[:, E // 2:E, :], d["b_1"][:, E // 2:E, :]).then_inc(s_b1, 16)
            sp.wait_ge(tab_ready, 1)
            for e in range(E):
                at = sp.value_load(fill_i[0:1, e:e + 1], min_val=0, max_val=E * CAP - P)
                sp.dma_start(slots_dram[bass.ds(at, P), :], zeros[:, :]).then_inc(pad_done, 16)
            sp.wait_ge(pad_done, 16 * E)
            sp.wait_ge(s_idle, 16 * IDLE)
            for u in range(2):
                sp.wait_ge(sent[u], 16 * TT * TOPK * IT)

            def load_slots(j, i, u):
                row = sp.value_load(tile_r[0:1, bass.ds(j, 1)], min_val=0, max_val=SLOTS - P)
                sp.wait_ge(slT_ps[u], START + i)
                sp.dma_start(sl[u], slots_dram[bass.ds(row, P), :]).then_inc(sl_in[u], 16)

            with sp.Fori(0, TILES // 2) as i:
                for u in range(2):
                    load_slots(2 * i + u, i, u)
            load_slots(TILES - 1, TILES // 2, 0)

            with sp.Fori(0, IT) as i:
                for u in range(2):
                    sp.wait_ge(y_ready[u], START + i + 1)
                    sp.dma_start(out[bass.ds(2 * i + u, 1), :, :].rearrange("n (t p) d -> p (n t) d", p=P),
                                 y_out[u][:, :, :]).then_inc(y_out_done[u], 16)
            for u in range(2):
                sp.wait_ge(y_out_done[u], START + 16 * IT)

        @block.gpsimd
        def _(pool):
            start(pool, rstd_ready, kbd_ready, kbd16_ready, rstd3_ready, z3_free, carried)
            pool.memset(half_power[:, :], -0.5).then_inc(s_init, 1)
            for u in range(2):
                pool.memset(aTs[u][:, :, 0:1], 0.0).then_inc(s_init, 1)
                pool.memset(v[u][:, :, HD:HD + 1], 1.0).then_inc(s_init, 1)
            pool.memset(ones_row[:, :], 1.0).then_inc(s_init, 1)
            pool.memset(zeros[:, :], 0.0).then_inc(s_init, 1)
            pool.wait_ge(s_init, 7)

            def inverse_deviation(i, k):
                for u in range(2):
                    pool.wait_ge(var_ready[u], START + 3 * i + k + 1)
                    pool.tensor_tensor(rstd[u][:, :], vare[u][:, :], half_power[:, :], ALU.pow)\
                        .then_inc(rstd_ready[u], 1)

            def keys(i):
                for dst, ready, used in ((kbd16, kbd16_ready, s_ps), (kbd, kbd_ready, st_ps)):
                    for u in range(2):
                        pool.wait_ge(kT_ready[u], START + i + 1)
                        pool.wait_ge(used, START + 16 * i)
                        for k in range(KT):
                            pool.tensor_tensor(
                                dst[u][:, k * HB:(k + 1) * HB, :],
                                kT[u][:, k, :].unsqueeze(1).to_broadcast([P, HB, C]),
                                headmask[:, :].unsqueeze(2).to_broadcast([P, HB, C]), ALU.mult).then_inc(ready[u], 1)

            def turn(i, more):
                if more:
                    inverse_deviation(i + 1, 0)
                for u in range(2):
                    pool.wait_ge(var3_ready[u], START + i + 1)
                    pool.tensor_tensor(rstd3[u][:, :], vare3[u][:, :], half_power[:, :], ALU.pow)\
                        .then_inc(rstd3_ready[u], 1)
                if more:
                    inverse_deviation(i + 1, 1)
                    keys(i + 1)
                    inverse_deviation(i + 1, 2)
                for u in range(2):
                    pool.wait_ge(slot_ready[u], START + i + 1)
                    pool.tensor_tensor(carrier[:, 3 + u:4 + u], zeros[:, 0:1], zeros[:, 0:1], ALU.add)
                    for k in range(TOPK):
                        for t in range(TT):
                            c = k * TT + t
                            pool.indirect_dma_start(
                                out=slots_dram, out_offset=bass.IndirectOffsetOnAxis(ap=slot[u][:, c:c + 1], axis=0),
                                in_=z3[u][:, t, :], in_offset=None).then_inc(sent[u], 16)
                for u in range(2):
                    pool.wait_ge(sent[u], 16 * TT * TOPK * (i + 1))
                    pool.tensor_tensor(carrier[:, 7 + u:8 + u], zeros[:, 0:1], zeros[:, 0:1], ALU.add)\
                        .then_inc(z3_free[u], 1)

            inverse_deviation(0, 0)
            inverse_deviation(0, 1)
            pool.wait_ge(s_small, 128)
            keys(0)
            inverse_deviation(0, 2)
            for i in range(IDLE):
                pool.dma_start(slots_dram[E * CAP + i * P:E * CAP + (i + 1) * P, :],
                               zeros[:, :]).then_inc(s_idle, 16)
            with pool.Fori(0, IT - 1) as i:
                turn(i, True)
            turn(IT - 1, False)

            pool.wait_ge(tab_ready, 1)
            pool.wait_ge(os_out[0], START + 16 * (TILES // 2 + 1))
            pool.wait_ge(os_out[1], START + 16 * (TILES // 2))

            with pool.Fori(0, IT) as i:
                for u in range(2):
                    pool.wait_ge(fidx_ready[u], START + i + 1)
                    pool.wait_ge(y_ready[u], START + i)
                    pool.wait_ge(carried[u], START + i)
                    pool.tensor_tensor(carrier[:, 5 + u:6 + u], zeros[:, 0:1], zeros[:, 0:1], ALU.add)\
                        .then_inc(carried[u], 1)
                    for c in range(TOPK * TT):
                        pool.indirect_dma_start(
                            out=got[u][:, c, :], out_offset=None, in_=outs_dram,
                            in_offset=bass.IndirectOffsetOnAxis(ap=slot[u][:, c:c + 1], axis=0),
                        ).then_inc(fetched[u], 16)

        @block.scalar
        def _(act):
            for t, n in ((ident, "ident"), (w_kv, "w_kv"), (gates, "gates"), (chan, "chan")):
                act.dma_start(t[:], d[n]).then_inc(s_first, 16)
            for t, n in ((w_r, "w_r"), (w_k, "w_k"), (w_v, "w_v"), (w_q, "w_q"), (w_out, "w_out"), (w_o, "w_o")):
                act.dma_start(t[:], d[n]).then_inc(s_w, 16)
            start(act, aT_ready, ge_ready, kT_ready, th_ready, rk_ready, ka_ready, q16_ready, q_ready, mT_ready, exp_done, attT_ready, aT3_ready,
                  el_ready, slT_ready, sig_ready, ghT_ready, os_ready, os_out)
            act.wait_ge(s_first, 64)
            act.activation(tg[:, :], gates[:, :], ACT.Tanh).then_inc(s_tg, 1)

            def transposed(i, k, u, before):
                dst = aTs[u][:, :, 1:T + 1] if k == 1 else aT[u][:, :, :]
                act.wait_ge(zT_ps[u], START + 3 * i + k + 1)
                before()
                act.activation(dst, t_chan(u), ACT.Copy).then_inc(aT_ready[u], 1)

            def layer0_context(i):
                for u in range(2):
                    transposed(i, 0, u, lambda: act.wait_ge(q_ps[u], START + i))
                for u in range(2):
                    act.wait_ge(h_ps[u], START + i + 1)
                    act.wait_ge(g_ready[u], START + i)
                    act.activation(ge[u], mb[u][0:C, 0:T], ACT.Gelu).then_inc(ge_ready[u], 1)
                for u in range(2):
                    act.wait_ge(k_ps[u], START + i + 1)
                    act.wait_ge(kbd16_ready[u], START + KT * i)
                    act.wait_ge(kbd_ready[u], START + KT * i)
                    for k in range(KT):
                        ins = act.activation(kT[u][:, k, :], tb[u][:, k * C:(k + 1) * C], ACT.Identity,
                                             bias=chan[:, 3, k:k + 1])
                    ins.then_inc(kT_ready[u], 1)

            def layer0_mix(i, router):
                for u in range(2):
                    transposed(i, 1, u, lambda: act.wait_ge(lg_ps[u], START + i))
                for u in range(2):
                    act.wait_ge(r_ps[u], START + i + 1)
                    act.wait_ge(attT_ps[u], START + i)
                    act.activation(flat(th[u][:, :, :]), tb[u][:, :], ACT.Tanh, scale=0.5).then_inc(th_ready[u], 1)
                    act.wait_ge(kk_ps[u], START + i + 1)
                    act.wait_ge(y_ps[u], START + i)
                    act.activation(flat(ka[u][:, :, :]), mb[u][:, :], ACT.Relu).then_inc(rk_ready[u], 1)
                    act.wait_ge(rk_ready[u], START + i + 1)
                    act.activation(flat(ka[u][:, :, :]), flat(ka[u][:, :, :]), ACT.Square).then_inc(ka_ready[u], 1)
                router()

            def queries(i):
                for u in range(2):
                    transposed(i, 2, u, lambda: act.wait_ge(h_ps[u], START + i + 1))
                    act.wait_ge(q_ps[u], START + i + 1)
                    act.wait_ge(s_ps, START + 16 * i)
                    for dst, ready in ((qT16, q16_ready), (qT, q_ready)):
                        for k in range(KT):
                            ins = act.activation(dst[u][:, k, :], mb[u][:, k * T:(k + 1) * T], ACT.Identity,
                                                 bias=chan[:, 2, k:k + 1])
                        ins.then_inc(ready[u], 1)

            def maxima(i, u):
                act.wait_ge(mT_ps[u], START + i + 1)
                act.activation(mT[u][:, :], tb[u][0:H, 0:T], ACT.Copy).then_inc(mT_ready[u], 1)

            def router(i):
                for u in range(2):
                    act.wait_ge(dl_ready[u], START + i + 1)
                    act.activation(el[u][:, :, :], dl[u][:, :, :], ACT.Exp).then_inc(el_ready[u], 1)

            def turn(i, more):
                maxima(i, 0)
                for u in range(2):
                    for c in range(H // 2):
                        if u == 0 and c == 2:
                            maxima(i, 1)
                        act.wait_ge(st_ps, START + 16 * i + 8 * u + c + 1)
                        if u == 0 and c == 0:
                            act.wait_ge(pv_done, START + 16 * i)
                        if u == 1:
                            act.wait_ge(pv_done, START + 16 * i + c + 1)
                        act.activation(flat(probs[:, c, :, :]), ring[c % 4][0:C, :], ACT.Exp,
                                       scale=HD ** -0.5).then_inc(exp_done, 1)
                for u in range(2):
                    act.wait_ge(attT_ps[u], START + i + 1)
                    act.activation(attT[u][:, :, 1:T + 1], t_chan(u), ACT.Copy).then_inc(attT_ready[u], 1)
                if more:
                    layer0_context(i + 1)
                for u in range(2):
                    act.wait_ge(z3T_ps[u], START + i + 1)
                    act.wait_ge(out_ps[u], START + i + 1)
                    act.activation(aTs[u][:, :, 1:T + 1], ring[2 + u][:, :].rearrange("p (k t) -> p k t", k=KT),
                                   ACT.Copy).then_inc(aT3_ready[u], 1)
                if more:
                    layer0_mix(i + 1, lambda: router(i))
                    queries(i + 1)
                else:
                    router(i)

            layer0_context(0)
            layer0_mix(0, lambda: None)
            queries(0)
            with act.Fori(0, IT - 1) as i:
                turn(i, True)
            turn(IT - 1, False)

            def take_in(i, u):
                act.wait_ge(slT_ps[u], START + i + 1)
                act.wait_ge(hh_ps[u], START + i)
                act.activation(slT[u], tb[u][:, 0:D].rearrange("p (k t) -> p k t", k=KT), ACT.Copy)\
                    .then_inc(slT_ready[u], 1)

            def gate(i, u):
                act.wait_ge(gate_ready[u], START + i + 1)
                act.wait_ge(gh_ready[u], START + i)
                act.activation(sig_h[u], gate_h[u], ACT.Sigmoid).then_inc(sig_ready[u], 1)

            def bring_back(i, u):
                act.wait_ge(ghT_ps[u], START + i + 1)
                act.wait_ge(os_ps[u], START + i)
                act.activation(g_hT[u], ring[2][:, :].rearrange("p (a b) -> p a b", a=FT), ACT.Copy)\
                    .then_inc(ghT_ready[u], 1)

            def bring_out(j, i, u):
                act.wait_ge(os_ps[u], START + i + 1)
                act.wait_ge(os_out[u], START + 16 * i)
                act.activation(o_s[u], ring[3][:, 0:D], ACT.Copy).then_inc(os_ready[u], 1)
                act.wait_ge(os_ready[u], START + i + 1)
                act.dma_start(outs_dram[bass.ds(P * j, P), :], o_s[u]).then_inc(os_out[u], 16)

            LAST = TILES // 2
            take_in(0, 0)
            gate(0, 0)
            take_in(0, 1)
            gate(0, 1)
            take_in(1, 0)
            bring_back(0, 0)
            with act.Fori(1, LAST) as i:
                gate(i, 0)
                take_in(i, 1)
                bring_back(i - 1, 1)
                bring_out(2 * i - 2, i - 1, 0)
                gate(i, 1)
                take_in(i + 1, 0)
                bring_back(i, 0)
                bring_out(2 * i - 1, i - 1, 1)
            gate(LAST, 0)
            bring_back(LAST - 1, 1)
            bring_out(2 * LAST - 2, LAST - 1, 0)
            bring_back(LAST, 0)
            bring_out(2 * LAST - 1, LAST - 1, 1)
            bring_out(2 * LAST, LAST, 0)

        @block.tensor
        def _(pe):
            start(pe, zT_ps, h_ps, k_ps, o_ps, r_ps, kk_ps, y_ps, v_ps, q_ps, s_ps, mT_ps, st_ps, pv_done, attT_ps, out_ps,
                  z3T_ps, lg_ps, rank_ps, slT_ps, hh_ps, ghT_ps, os_ps)
            pe.wait_ge(s_first, 64)

            def transposes(dst, src):
                for kt in range(KT):
                    for t in range(TT):
                        ins = pe.transpose(dst[:, kt, t * P:(t + 1) * P], src[:, t, kt * P:(kt + 1) * P], ident[:, :])
                return ins

            def transpose(i, k, u):
                pe.wait_ge(z_ready[u], START + 3 * i + k + 1)
                transposes(t_chan(u), z[u]).then_inc(zT_ps[u], 1)

            def by_token(dst, actT, w):
                for t in range(TT):
                    for kt in range(KT):
                        ins = pe.matmul(dst[:, t, :], actT[:, kt, t * P:(t + 1) * P], w[:, kt, :],
                                        start=(kt == 0), stop=(kt == KT - 1))
                return ins

            def by_channel(dst, w, actT, off=0):
                for m in range(KT):
                    for kt in range(KT):
                        ins = pe.matmul(dst[:, m, :], w[:, kt, off + m * P:off + (m + 1) * P], actT[:, kt, :],
                                        start=(kt == 0), stop=(kt == KT - 1))
                return ins

            def layer0_hidden(i):
                for u in range(2):
                    pe.wait_ge(aT_ready[u], START + 3 * i + 1)
                    pe.wait_ge(cx_in[u], START + 32 * (i + 1))
                    pe.wait_ge(var3_ready[u], START + i)
                    for kt in range(KT):
                        ins = pe.matmul(mb[u][0:C, 0:T], cxT[u][:, kt, :], aT[u][:, kt, :],
                                        start=(kt == 0), stop=(kt == KT - 1))
                    ins.then_inc(h_ps[u], 1)
                    for m in range(KT):
                        for kt in range(KT):
                            ins = pe.matmul(tb[u][:, m * C:(m + 1) * C], w_kv[:, kt, m * P:(m + 1) * P],
                                            cxT[u][:, kt, :], start=(kt == 0), stop=(kt == KT - 1))
                    ins.then_inc(k_ps[u], 1)

            def layer0_context(i):
                for u in range(2):
                    pe.wait_ge(g_ready[u], START + i + 1)
                    for t in range(TT):
                        ins = pe.matmul(m_tok(u)[:, t, :], gT[u][:, t * P:(t + 1) * P], cx[u][:, :],
                                        start=True, stop=True)
                    ins.then_inc(o_ps[u], 1)

            def layer0_mix(i, router):
                for u in range(2):
                    pe.wait_ge(kT_ready[u], START + i + 1)
                    transpose(i, 1, u)

                def receptance(u):
                    pe.wait_ge(aT_ready[u], START + 3 * i + 2)
                    pe.wait_ge(xr_ready[u], START + i + 1)
                    by_token(tb[u][:, :].rearrange("p (t d) -> p t d", t=TT), xr[u], w_r).then_inc(r_ps[u], 1)

                def key(u):
                    pe.wait_ge(xk_ready[u], START + i + 1)
                    by_channel(mb[u][:, :].rearrange("p (k t) -> p k t", k=KT), w_k, xk[u]).then_inc(kk_ps[u], 1)

                def value(u):
                    pe.wait_ge(ka_ready[u], START + i + 1)
                    by_token(m_tok(u), ka[u], w_v).then_inc(y_ps[u], 1)

                receptance(0)
                key(0)
                receptance(1)
                value(0)
                key(1)
                for u in range(2):
                    pe.wait_ge(aT3_ready[u], START + i)
                    for kt in range(KT):
                        ins = pe.matmul(ring[2 + u][0:C, 0:D], cxT[u][:, kt, :], w_kv[:, kt, D:2 * D],
                                        start=(kt == 0), stop=(kt == KT - 1))
                    ins.then_inc(v_ps[u], 1)
                value(1)
                router()

            def queries(i):
                def project(u):
                    pe.wait_ge(aT_ready[u], START + 3 * i + 3)
                    by_channel(mb[u][:, :].rearrange("p (k t) -> p k t", k=KT), w_q, aT[u]).then_inc(q_ps[u], 1)

                def scores(u, chunks):
                    pe.wait_ge(q16_ready[u], START + i + 1)
                    pe.wait_ge(kbd16_ready[u], START + KT * (i + 1))
                    for c in chunks:
                        t, hq = c // 4, c % 4
                        if c >= 4:
                            pe.wait_ge(max_done, START + 16 * i + 8 * u + c - 3)
                        elif u == 1:
                            pe.wait_ge(max_done, START + 16 * i + c + 5)
                        elif c == 0:
                            pe.wait_ge(exp_done, START + 16 * i)
                            for b in range(2):
                                pe.wait_ge(rank_taken[b], START + i)
                                pe.wait_ge(v_ready[b], START + i + 1)
                        pe.matmul(ring[c % 4][:, 0:4 * C], qT16[u][:, hq // 2, t * P:(t + 1) * P],
                                  flat(kbd16[u][:, 4 * hq:4 * hq + 4, :]), start=True, stop=True).then_inc(s_ps, 1)

                pe.wait_ge(th_ready[0], START + i + 1)
                transpose(i, 2, 0)
                project(0)
                pe.wait_ge(th_ready[1], START + i + 1)
                transpose(i, 2, 1)
                scores(0, range(0, 4))
                project(1)
                scores(0, range(4, 8))
                scores(1, range(0, 8))

            def maxima(i, u):
                pe.wait_ge(mx_ready[u], START + i + 1)
                for t in range(TT):
                    ins = pe.matmul(tb[u][0:H, t * P:(t + 1) * P], mx16[u][:, t, :], ident16[:, :],
                                    start=True, stop=True)
                ins.then_inc(mT_ps[u], 1)

            def weigh(i, u, c):
                pe.wait_ge(exp_done, START + 16 * i + 8 * u + c + 1)
                if c == 0:
                    pe.wait_ge(q_ready[u], START + i + 1)
                    pe.wait_ge(mT_ready[u], START + i + 1)
                for h in (2 * c, 2 * c + 1):
                    for t in range(TT):
                        dst = (mb, tb)[t][u]
                        ins = pe.matmul(dst[:, h * (HD + 1):(h + 1) * (HD + 1)],
                                        probs[:, c, h % 2, t * P:(t + 1) * P], v[u][:, h, :],
                                        start=True, stop=True)
                ins.then_inc(pv_done, 1)

            def ranks_of(i):
                for u in range(2):
                    pe.wait_ge(oh_ready[u], START + i + 1)
                    for m in range(2):
                        ins = pe.matmul(ring[u][:, (1 + m) * TT * E:(2 + m) * TT * E], tri_ones16[:, m, :],
                                        flat(chosen[u][:, :, :]), start=True, stop=True)
                    ins.then_inc(rank_ps[u], 1)

            def turn(i, more):
                maxima(i, 0)
                for u in range(2):
                    pe.wait_ge(q_ready[u], START + i + 1)
                    pe.wait_ge(kbd_ready[u], START + KT * (i + 1))
                    pe.wait_ge(mT_ready[u], START + i + 1)
                    for c in range(8):
                        if c >= 4:
                            pe.wait_ge(exp_done, START + 16 * i + 8 * u + c - 3)
                        elif u == 0:
                            pe.wait_ge(max_done, START + 16 * i + 8 + c + 5)
                        else:
                            pe.wait_ge(exp_done, START + 16 * i + c + 5)
                        if u == 0 and c == 2:
                            maxima(i, 1)
                        for h in (2 * c, 2 * c + 1):
                            dst = ring[c % 4][0:C, (h % 2) * T:(h % 2 + 1) * T]
                            pe.matmul(dst, negsel16[:, h, :], mT[u][:, :], start=True, stop=False)
                            ins = pe.matmul(dst, kbd[u][:, h, :], qT[u][:, h // HB, :], start=False, stop=True)
                        ins.then_inc(st_ps, 1)
                        if c >= 2:
                            weigh(i, u, c - 2)
                    weigh(i, u, 6)
                    weigh(i, u, 7)
                for u in range(2):
                    pe.wait_ge(att_ready[u], START + i + 1)
                    transposes(t_chan(u), att[u]).then_inc(attT_ps[u], 1)
                for u in range(2):
                    pe.wait_ge(attT_ready[u], START + i + 1)
                    by_token(m_tok(u), attT[u][:, :, 1:T + 1], w_out).then_inc(out_ps[u], 1)
                    if more:
                        transpose(i + 1, 0, u)
                if more:
                    layer0_hidden(i + 1)
                for u in range(2):
                    pe.wait_ge(z3_ready[u], START + i + 1)
                    transposes(ring[2 + u][:, :].rearrange("p (k t) -> p k t", k=KT), z3[u]).then_inc(z3T_ps[u], 1)
                if more:
                    layer0_context(i + 1)
                for u in range(2):
                    pe.wait_ge(aT3_ready[u], START + i + 1)
                    for t in range(TT):
                        for kt in range(KT):
                            ins = pe.matmul(ring[u][:, t * E:(t + 1) * E], aTs[u][:, kt, 1 + t * P:1 + (t + 1) * P],
                                            w_g[:, kt, :], start=(kt == 0), stop=(kt == KT - 1))
                    ins.then_inc(lg_ps[u], 1)
                if more:
                    layer0_mix(i + 1, lambda: ranks_of(i))
                    queries(i + 1)
                else:
                    ranks_of(i)

            for u in range(2):
                transpose(0, 0, u)
            layer0_hidden(0)
            layer0_context(0)
            pe.wait_ge(s_w, 96)
            pe.wait_ge(s_small, 128)
            layer0_mix(0, lambda: None)
            queries(0)
            with pe.Fori(0, IT - 1) as i:
                turn(i, True)
            turn(IT - 1, False)

            pe.wait_ge(tab_ready, 1)
            pe.wait_ge(s_w1, 16 * E)

            def take_in(i, u):
                pe.wait_ge(sl_in[u], START + 16 * (i + 1))
                pe.wait_ge(slT_ready[u], START + i)
                for kt in range(KT):
                    ins = pe.transpose(tb[u][:, kt * P:(kt + 1) * P], sl[u][:, kt * P:(kt + 1) * P], ident[:, :])
                ins.then_inc(slT_ps[u], 1)

            hid = [[mb[0], mb[1]], [ring[0], ring[1]]]

            def hidden(j, i, u):
                e = pe.value_load(tile_w[0:1, bass.ds(j, 1)], min_val=0, max_val=E - 1)
                pe.wait_ge(slT_ready[u], START + i + 1)
                pe.wait_ge(gh_ready[u], START + i)
                for m in (1, 0):
                    for kt in range(KT):
                        ins = pe.matmul(hid[u][m][:, :], slT[u][:, kt, :],
                                        w_1[:, bass.ds(e, 1), kt, m * F:(m + 1) * F].rearrange("p e f -> p (e f)"),
                                        start=(kt == 0), stop=(kt == KT - 1))
                    ins.then_inc(hh_ps[u], 1)

            def back(i, u):
                pe.wait_ge(gh_ready[u], START + i + 1)
                pe.wait_ge(ghT_ready[1 - u], START + i + u)
                for a in range(FT):
                    ins = pe.transpose(ring[2][:, a * P:(a + 1) * P], g_h[u][:, a * P:(a + 1) * P], ident[:, :])
                ins.then_inc(ghT_ps[u], 1)

            def result(i, u):
                pe.wait_ge(ghT_ready[u], START + i + 1)
                pe.wait_ge(os_ready[1 - u], START + i + u)
                for a in range(FT):
                    ins = pe.matmul(ring[3][:, 0:D], g_hT[u][:, a, :], w_o[:, a, :],
                                    start=(a == 0), stop=(a == FT - 1))
                ins.then_inc(os_ps[u], 1)

            LAST = TILES // 2
            take_in(0, 0)
            hidden(0, 0, 0)
            take_in(0, 1)
            hidden(1, 0, 1)
            take_in(1, 0)
            back(0, 0)
            with pe.Fori(1, LAST) as i:
                hidden(2 * i, i, 0)
                take_in(i, 1)
                back(i - 1, 1)
                result(i - 1, 0)
                hidden(2 * i + 1, i, 1)
                take_in(i + 1, 0)
                back(i, 0)
                result(i - 1, 1)
            hidden(2 * LAST, LAST, 0)
            back(LAST - 1, 1)
            result(LAST - 1, 0)
            back(LAST, 0)
            result(LAST - 1, 1)
            result(LAST, 0)

        @block.vector
        def _(dve):
            start(dve, var_ready, z_ready, g_ready, xr_ready, xk_ready, v_ready, x2_done, max_done, mx_ready, att_ready,
                  dl_ready, var3_ready, z3_ready, rank_taken,
                  oh_ready, slot_ready, gate_ready, gh_ready, val_ready, fidx_ready, half_y, y_ready)
            dve.wait_ge(s_init, 7)
            dve.wait_ge(s_first, 64)
            dve.wait_ge(s_tg, 1)
            dve.tensor_scalar(half_tg[:, :], tg[:, 1:2], 0.5, None, ALU.mult).then_inc(s_const, 1)

            def residual(i, u):
                return xres[:, bass.ds(2 * i + u, 1), :, :].rearrange("p n t d -> p (n t) d")

            def statistics(c, src, buffers, ready):
                stats_u, mv_u, vare_u = buffers
                dve.memset(carrier[:, 0:1], 0.0)
                for t in range(TT):
                    c.done(dve.bn_stats(stats_u[:, t, :], src[:, t, :]))
                c.wait()
                dve.memset(carrier[:, 0:1], 0.0)
                for t in range(TT):
                    c.done(dve.bn_aggr(mv_u[:, t, :], stats_u[:, t, :]))
                c.wait()
                dve.tensor_scalar(vare_u[:, :], mv_u[:, :, 1], EPS, None, ALU.add).then_inc(ready, 1)

            def moments(u):
                return stats[u], mv[u], vare[u]

            def normalise(i, k, u, src):
                dve.wait_ge(rstd_ready[u], START + 3 * i + k + 1)
                dve.wait_ge(zT_ps[u], START + 3 * i + k)
                for t in range(TT):
                    ins = dve.tensor_scalar(z[u][:, t, :], src[:, t, :], mv[u][:, t, 0:1], rstd[u][:, t:t + 1],
                                            ALU.subtract, ALU.mult)
                ins.then_inc(z_ready[u], 1)

            def layer0_enter(i, c):
                for u in range(2):
                    dve.wait_ge(x_in[u], START + 16 * (i + 1))
                    statistics(c, x[u], moments(u), var_ready[u])
                for u in range(2):
                    normalise(i, 0, u, x[u])

            def layer0_gate(i, c):
                for u in range(2):
                    dve.wait_ge(ge_ready[u], START + i + 1)
                    dve.wait_ge(o_ps[u], START + i)
                    dve.tensor_tensor(gT[u], ge[u], mb[u][0:C, 0:T], ALU.mult).then_inc(g_ready[u], 1)

            def layer0_context(i, c):
                for u in range(2):
                    dve.wait_ge(o_ps[u], START + i + 1)
                    c.done(dve.scalar_tensor_tensor(flat(x[u][:, :, :]), mb[u][:, :], tg[:, 0:1], flat(x[u][:, :, :]),
                                                    ALU.mult, ALU.add))
                    c.wait()
                    statistics(c, x[u], moments(u), var_ready[u])
                for u in range(2):
                    normalise(i, 1, u, x[u])

            def layer0_shift(i, c):
                for u in range(2):
                    dve.wait_ge(aT_ready[u], START + 3 * i + 2)
                    dve.wait_ge(xk_ready[1 - u], START + i + u)
                    cur, prev = aTs[u][:, :, 1:T + 1], aTs[u][:, :, 0:T]
                    c.done(dve.tensor_tensor(diff[:, :, :], cur, prev, ALU.subtract))
                    c.wait()
                    dve.wait_ge(st_ps, START + 16 * i)
                    for dst, m, s in ((xr, 0, xr_ready), (xk, 1, xk_ready)):
                        for k in range(KT):
                            ins = dve.scalar_tensor_tensor(dst[u][:, k, :], diff[:, k, :], chan[:, m, k:k + 1],
                                                           prev[:, k, :], ALU.mult, ALU.add)
                        ins.then_inc(s[u], 1)

            def weights(i, c):
                for u in range(2):
                    dve.wait_ge(el_ready[u], START + i + 1)
                    c.done(dve.tensor_reduce(zsum[u][:, :], el[u][:, :, 0:E], AX_X, ALU.add))
                    c.wait()
                    c.done(dve.scalar_tensor_tensor(den[u][:, :], zsum[u][:, :], 1e-9, el[u][:, :, E], ALU.mult, ALU.add))
                    c.wait()
                    c.done(dve.tensor_scalar(zsum[u][:, :], den[u][:, :], 1.0, None, ALU.add))
                    c.wait()
                    c.done(dve.reciprocal(den[u][:, :], zsum[u][:, :]))
                    c.wait()
                    dve.tensor_scalar(wk[u][:, :, 0], den[u][:, :], tg[:, 3:4], None, ALU.mult)
                    c.done(dve.scalar_tensor_tensor(wk[u][:, :, 1], den[u][:, :], tg[:, 3:4], el[u][:, :, E],
                                                    ALU.mult, ALU.mult))
                    c.done(dve.scalar_tensor_tensor(wsum[u][:, :], el[u][:, :, E], 1.0, den[u][:, :], ALU.add, ALU.mult))
                    c.wait()
                    dve.tensor_copy(wres[:, bass.ds(2 * i + u, 1), :, :].rearrange("p n t k -> p (n t k)"),
                                    flat(wk[u][:, :, :]))
                    for t in range(TT):
                        dve.scalar_tensor_tensor(
                            xres[:, bass.ds(2 * i + u, 1), t, :].rearrange("p n d -> p (n d)"), rows[:, 2, :],
                            wsum[u][:, t:t + 1], residual(i, u)[:, t, :], ALU.mult, ALU.add)

            def choose(i, c):
                for u in range(2):
                    dve.wait_ge(lg_ps[u], START + i + 1)
                    c.done(dve.tensor_copy(flat(lg[u][:, :, :]), ring[u][:, 0:TT * E]))
                    c.wait()
                    dve.memset(carrier[:, 0:1], 0.0)
                    for t in range(TT):
                        c.done(dve.max(top[u][:, t, :], lg[u][:, t, :]))
                    c.wait()
                    dve.tensor_tensor(dl[u][:, :, 0:E], lg[u][:, :, :], top[u][:, :, 0:1].to_broadcast([P, TT, E]),
                                      ALU.subtract)
                    dve.tensor_tensor(dl[u][:, :, E], top[u][:, :, 1], top[u][:, :, 0], ALU.subtract)\
                        .then_inc(dl_ready[u], 1)
                    for t in range(TT):
                        c.done(dve.max_index(topi[u][:, t, :], top[u][:, t, :], lg[u][:, t, :]))
                    c.wait()
                    c.done(dve.tensor_copy(topf[u][:, :, :], topi[u][:, :, 0:TOPK].rearrange("p t k -> p k t")))
                    c.wait()
                    wide = [P, TOPK * TT, E]
                    c.done(dve.tensor_tensor(oh[u][:, :, :, :].rearrange("p k t e -> p (k t) e"),
                                             iotas[:, 0, :].unsqueeze(1).to_broadcast(wide),
                                             flat(topf[u][:, :, :]).unsqueeze(2).to_broadcast(wide), ALU.is_equal))
                    c.wait()
                    dve.tensor_tensor(chosen[u][:, :, :], oh[u][:, 0, :, :], oh[u][:, 1, :, :], ALU.add)\
                        .then_inc(oh_ready[u], 1)

            def take_ranks(i, c):
                for u in range(2):
                    dve.wait_ge(rank_ps[u], START + i + 1)
                    dve.tensor_copy(ranks[u][:, :, :, :].rearrange("p m t e -> p (m t e)"),
                                    ring[u][:, TT * E:3 * TT * E]).then_inc(rank_taken[u], 1)

            def place(i, c):
                for u in range(2):
                    dve.wait_ge(rank_taken[u], START + i + 1)
                    dve.tensor_tensor(pos[u][:, 0, :], fill[:, :], ranks[u][:, 0, 0, :], ALU.add)
                    c.done(dve.tensor_tensor(fill1[:, :], fill[:, :], ranks[u][:, 1, 0, :], ALU.add))
                    c.wait()
                    dve.tensor_tensor(pos[u][:, 1, :], fill1[:, :], ranks[u][:, 0, 1, :], ALU.add)
                    c.done(dve.tensor_tensor(fill[:, :], fill1[:, :], ranks[u][:, 1, 1, :], ALU.add))
                    c.wait()
                    for k in range(TOPK):
                        c.done(dve.tensor_tensor(ohpos[u][:, k, :, :], oh[u][:, k, :, :], pos[u][:, :, :], ALU.mult))
                    c.wait()
                    dve.wait_ge(z3_free[u], START + i)
                    c.done(dve.tensor_reduce(slotf[u][:, :], ohpos[u][:, :, :, :].rearrange("p k t e -> p (k t) e"),
                                             AX_X, ALU.add))
                    c.wait()
                    dve.tensor_copy(slot[u][:, :], slotf[u][:, :]).then_inc(slot_ready[u], 1)
                    dve.tensor_copy(slotres[:, bass.ds(2 * i + u, 1), :].rearrange("p n s -> p (n s)"), slotf[u][:, :])
                    dve.tensor_copy(expres[:, bass.ds(2 * i + u, 1), :].rearrange("p n s -> p (n s)"),
                                    flat(topf[u][:, :, :]))

            def layer0_mix(i, c):
                for u in range(2):
                    dve.wait_ge(y_ps[u], START + i + 1)
                    dve.wait_ge(th_ready[u], START + i + 1)
                    c.done(dve.scalar_tensor_tensor(flat(yb[u][:, :, :]), flat(th[u][:, :, :]), 1.0, mb[u][:, :],
                                                    ALU.add, ALU.mult))
                    c.wait()
                    dve.scalar_tensor_tensor(flat(residual(i, u)), flat(yb[u][:, :, :]), half_tg[:, 0:1],
                                             flat(x[u][:, :, :]), ALU.mult, ALU.add).then_inc(x2_done[u], 1)
                    dve.wait_ge(x2_done[u], START + i + 1)
                    statistics(c, residual(i, u), moments(u), var_ready[u])
                    normalise(i, 2, u, residual(i, u))
                    if u == 1:
                        continue
                    for w in range(2):
                        dve.wait_ge(v_ps[w], START + i + 1)
                        dve.wait_ge(pv_done, START + 16 * i)
                        dve.tensor_tensor(v[w][:, :, 0:HD], ring[2 + w][0:C, 0:D].rearrange("p (h c) -> p h c", h=H),
                                          rows[0:C, 0, :].rearrange("p (h c) -> p h c", h=H), ALU.add)\
                            .then_inc(v_ready[w], 1)

            def maxima(i, c):
                for u in range(2):
                    for n in range(8):
                        t, hq = n // 4, n % 4
                        dve.wait_ge(s_ps, START + 16 * i + 8 * u + n + 1)
                        dve.tensor_reduce(mx[u][:, t, 4 * hq:4 * hq + 4],
                                          ring[n % 4][:, 0:4 * C].rearrange("p (h c) -> p h c", h=4),
                                          AX_X, ALU.max).then_inc(max_done, 1)
                    dve.wait_ge(max_done, START + 16 * i + 8 * u + 8)
                    dve.wait_ge(mT_ps[u], START + i)
                    dve.tensor_copy(flat(mx16[u][:, :, :]), flat(mx[u][:, :, :])).then_inc(mx_ready[u], 1)

            def turn(i, c, more):
                for u in range(2):
                    for t in range(TT):
                        c.done(dve.tensor_tensor(residual(i, u)[:, t, :], residual(i, u)[:, t, :], rows[:, 1, :], ALU.add))
                if more:
                    layer0_enter(i + 1, c)
                for u in range(2):
                    dve.wait_ge(pv_done, START + 16 * i + 8 * u + 8)
                    for t in range(TT):
                        ps = (mb, tb)[t][u][:, 0:H * (HD + 1)].rearrange("p (h c) -> p h c", h=H)
                        c.done(dve.reciprocal(rden[u][:, t, :], ps[:, :, HD]))
                    c.wait()
                    for t in range(TT):
                        ps = (mb, tb)[t][u][:, 0:H * (HD + 1)].rearrange("p (h c) -> p h c", h=H)
                        ins = dve.tensor_tensor(att[u][:, t, :].rearrange("p (h c) -> p h c", h=H), ps[:, :, 0:HD],
                                                rden[u][:, t, :].unsqueeze(2).to_broadcast([P, H, HD]), ALU.mult)
                    ins.then_inc(att_ready[u], 1)
                for u in range(2):
                    dve.wait_ge(out_ps[u], START + i + 1)
                    c.done(dve.scalar_tensor_tensor(flat(residual(i, u)), mb[u][:, :], tg[:, 2:3],
                                                    flat(residual(i, u)), ALU.mult, ALU.add))
                    c.wait()
                    statistics(c, residual(i, u), (stats3[u], mv3[u], vare3[u]), var3_ready[u])
                if more:
                    layer0_gate(i + 1, c)
                for u in range(2):
                    dve.wait_ge(rstd3_ready[u], START + i + 1)
                    dve.wait_ge(z3T_ps[u], START + i)
                    dve.wait_ge(z3_free[u], START + i)
                    for t in range(TT):
                        ins = dve.tensor_scalar(z3[u][:, t, :], residual(i, u)[:, t, :], mv3[u][:, t, 0:1],
                                                rstd3[u][:, t:t + 1], ALU.subtract, ALU.mult)
                    ins.then_inc(z3_ready[u], 1)
                if more:
                    layer0_context(i + 1, c)

                if more:
                    layer0_shift(i + 1, c)
                choose(i, c)
                if more:
                    layer0_mix(i + 1, c)
                take_ranks(i, c)
                if more:
                    maxima(i + 1, c)
                place(i, c)
                if more:
                    weights(i, c)
                return c.n

            c = Steps(dve, vec_step, 0)
            layer0_enter(0, c)
            layer0_gate(0, c)
            layer0_context(0, c)
            layer0_shift(0, c)
            dve.wait_ge(s_small, 128)
            dve.tensor_copy(fill[:, :], iotas[:, 1, :]).then_inc(s_const, 1)
            dve.tensor_scalar(rows[:, 1, :], rows[:, 1, :], tg[:, 2:3], None, ALU.mult).then_inc(s_const, 1)
            dve.tensor_scalar(rows[:, 2, :], rows[:, 2, :], tg[:, 3:4], None, ALU.mult).then_inc(s_const, 1)
            dve.wait_ge(s_const, 4)
            layer0_mix(0, c)
            maxima(0, c)
            steps = c.n
            with dve.Fori(0, IT - 1) as i:
                made = turn(i, Steps(dve, vec_step, steps + VEC_STEPS * i), True)
                assert made == VEC_STEPS, made
            last = Steps(dve, vec_step, steps + VEC_STEPS * (IT - 1))
            turn(IT - 1, last, False)

            c = Steps(dve, tab_step, 0)
            c.done(dve.tensor_copy(fill_i[:, :], fill[0:1, :]))
            c.done(dve.tensor_tensor(filled[:, :], fill[:, :], iotas[:, 1, :], ALU.subtract))
            c.wait()
            c.done(dve.tensor_scalar(filled_i[:, :], filled[:, :], float(P - 1), None, ALU.add))
            c.wait()
            c.done(dve.tensor_scalar(filled_i[:, :], filled_i[:, :], 7, None, ALU.arith_shift_right))
            c.wait()
            c.done(dve.tensor_copy(ntiles[:, :], filled_i[:, :]))
            c.wait()
            c.done(dve.tensor_tensor_scan(cum[:, :], ones_row[:, :], ntiles[:, :], 0.0, ALU.mult, ALU.add))
            c.wait()
            wide = [1, TILES, E]
            c.done(dve.tensor_tensor(past[:, :, :], cum[0:1, :].unsqueeze(1).to_broadcast(wide),
                                     tile_no[:, 0:TILES].unsqueeze(2).to_broadcast(wide), ALU.is_le))
            c.wait()
            c.done(dve.tensor_tensor(pastn[:, :, :], past[:, :, :], ntiles[0:1, :].unsqueeze(1).to_broadcast(wide), ALU.mult))
            c.done(dve.tensor_reduce(tile_e[:, :], past[:, :, :], AX_X, ALU.add))
            c.wait()
            c.done(dve.tensor_reduce(tile_c[:, :], pastn[:, :, :], AX_X, ALU.add))
            c.done(dve.tensor_scalar(tile_w[:, :], tile_e[:, :], float(E - 1), None, ALU.min))
            c.wait()
            c.done(dve.tensor_tensor(tile_c[:, :], tile_no[:, 0:TILES], tile_c[:, :], ALU.subtract))
            c.done(dve.tensor_scalar(tile_e[:, :], tile_e[:, :], float(CAP), None, ALU.mult))
            c.wait()
            c.done(dve.scalar_tensor_tensor(tile_r[:, :], tile_c[:, :], float(P), tile_e[:, :], ALU.mult, ALU.add))
            c.wait()
            dve.tensor_copy(filled[:, :], ntiles[:, :]).then_inc(tab_ready, 1)
            weights(IT - 1, last)

            c.wait()
            c.done(dve.tensor_tensor(shift[:, :], cum[:, :], ntiles[:, :], ALU.subtract))
            c.wait()
            c.done(dve.scalar_tensor_tensor(shift[:, :], shift[:, :], float(P), iotas[:, 1, :], ALU.mult, ALU.subtract))
            wide = [P, B * TOPK * TT, E]
            c.done(dve.tensor_tensor(moved, flat(expres[:, :, :]).unsqueeze(2).to_broadcast(wide),
                                     iotas[:, 0, :].unsqueeze(1).to_broadcast(wide), ALU.is_equal))
            c.wait()
            c.done(dve.tensor_tensor(moved, moved, shift[:, :].unsqueeze(1).to_broadcast(wide), ALU.mult))
            c.wait()
            c.done(dve.tensor_reduce(flat(expres[:, :, :]), moved, AX_X, ALU.add))
            c.wait()
            c.done(dve.tensor_tensor(flat(packed[:, :, :]), flat(expres[:, :, :]), flat(slotres[:, :, :]), ALU.add))
            c.wait()

            hid = [[mb[0], mb[1]], [ring[0], ring[1]]]
            dve.wait_ge(s_b1, 32)
            dve.wait_ge(tab_ready, 1)

            def glu(j, i, u):
                e = dve.value_load(tile_w[0:1, bass.ds(j, 1)], min_val=0, max_val=E - 1)

                def bias(m):
                    return b_1[:, bass.ds(e, 1), m * F:(m + 1) * F].rearrange("p e f -> p (e f)")

                dve.wait_ge(hh_ps[u], START + 2 * i + 1)
                dve.wait_ge(sig_ready[u], START + i)
                dve.tensor_tensor(gate_h[u], hid[u][1][:, :], bias(1), ALU.add).then_inc(gate_ready[u], 1)
                dve.wait_ge(hh_ps[u], START + 2 * i + 2)
                dve.tensor_tensor(val_h[u], hid[u][0][:, :], bias(0), ALU.add).then_inc(val_ready[u], 1)
                dve.wait_ge(val_ready[u], START + i + 1)
                dve.wait_ge(sig_ready[u], START + i + 1)
                dve.wait_ge(ghT_ps[u], START + i)
                dve.tensor_tensor(g_h[u], val_h[u], sig_h[u], ALU.mult).then_inc(gh_ready[u], 1)

            with dve.Fori(0, TILES // 2) as i:
                for u in range(2):
                    glu(2 * i + u, i, u)
            glu(TILES - 1, TILES // 2, 0)

            def indices(i, u):
                dve.tensor_copy(slot[u][:, :], packed[:, bass.ds(2 * i + u, 1), :].rearrange(
                    "p n s -> p (n s)")).then_inc(fidx_ready[u], 1)

            def combine(i, u, more):
                dve.wait_ge(fetched[u], 16 * TOPK * TT * (i + 1))
                if more:
                    indices(i + 1, u)
                dve.wait_ge(y_out_done[u], START + 16 * i)
                for k in range(TOPK):
                    for t in range(TT):
                        base = (xres[:, bass.ds(2 * i + u, 1), t, :].rearrange("p n d -> p (n d)") if k == 0
                                else y_out[u][:, t, :])
                        ins = dve.scalar_tensor_tensor(
                            y_out[u][:, t, :], got[u][:, k * TT + t, :],
                            wres[:, bass.ds(2 * i + u, 1), t, k:k + 1].rearrange("p n k -> p (n k)"), base,
                            ALU.mult, ALU.add)
                    if k == 0:
                        ins.then_inc(half_y[u], 1)
                        dve.wait_ge(half_y[u], START + i + 1)
                ins.then_inc(y_ready[u], 1)

            for u in range(2):
                indices(0, u)
            with dve.Fori(0, IT - 1) as i:
                for u in range(2):
                    combine(i, u, True)
            for u in range(2):
                combine(IT - 1, u, False)


def kernel(x, ctx_1024, g_xattn, g_ffn, L0_ffn_W_r, L0_ffn_W_k, L0_ffn_W_v, L0_ffn_mu_r, L0_ffn_mu_k,
           L1_xattn_w_q, L1_xattn_b_q, L1_xattn_w_kv, L1_xattn_b_kv, L1_xattn_w_out, L1_xattn_b_out,
           L1_ffn_Wg, L1_ffn_W1, L1_ffn_b1, L1_ffn_Wo, L1_ffn_bo):
    import ml_dtypes
    import concourse.bacc as bacc
    from concourse.bass_utils import run_bass_kernel_spmd

    def blocks(w):
        w = np.asarray(w)
        return np.ascontiguousarray(w.reshape(-1, P, w.shape[1]).transpose(1, 0, 2))

    def every(a):
        a = np.asarray(a)
        return np.ascontiguousarray(np.broadcast_to(a[None], (P,) + a.shape))

    def per_channel(a):
        return np.asarray(a).reshape(KT, P).T

    f32, bf16 = np.float32, ml_dtypes.bfloat16
    tri = np.triu(np.ones((P, P), f32), 1)
    negsel = np.zeros((H, H, C), f32)
    negsel[np.arange(H), np.arange(H)] = -1.0
    arrays = {
        "x": np.asarray(x),
        "ctx": np.asarray(ctx_1024),
        "ctxT": np.ascontiguousarray(np.asarray(ctx_1024).transpose(0, 2, 1)),
        "gates": every(np.stack([np.asarray(g)[l] for l in range(2) for g in (g_xattn, g_ffn)])),
        "w_r": blocks(np.asarray(L0_ffn_W_r).T),
        "w_k": blocks(np.asarray(L0_ffn_W_k).T),
        "w_v": blocks(np.asarray(L0_ffn_W_v).T),
        "w_q": blocks(L1_xattn_w_q),
        "w_kv": blocks(L1_xattn_w_kv),
        "w_out": blocks(L1_xattn_w_out),
        "w_g": blocks(np.asarray(L1_ffn_Wg).T),
        "w_o": blocks(np.asarray(L1_ffn_Wo).T),
        "w_1": np.ascontiguousarray(np.asarray(L1_ffn_W1).transpose(0, 2, 1)),
        "b_1": every(L1_ffn_b1),
        "chan": np.ascontiguousarray(np.stack(
            [per_channel(a) for a in (L0_ffn_mu_r, L0_ffn_mu_k, L1_xattn_b_q, np.asarray(L1_xattn_b_kv)[:D])], 1)),
        "rows": every(np.stack([np.asarray(L1_xattn_b_kv)[D:], np.asarray(L1_xattn_b_out), np.asarray(L1_ffn_bo)])),
        "ident": np.eye(P, dtype=f32),
        "ident16": np.eye(P, dtype=f32).astype(bf16),
        "tri_ones": np.ascontiguousarray(np.stack([tri, np.ones((P, P), f32)], 1)).astype(bf16),
        "headmask": (np.arange(P)[:, None] // HD == np.arange(HB)[None]).astype(f32),
        "negsel": negsel.astype(bf16),
        "iotas": every(np.stack([np.arange(E), np.arange(E) * CAP]).astype(f32)),
        "tile_no": np.arange(TILES + 1, dtype=f32)[None],
    }
    nc = bacc.Bacc("TRN2", target_bir_lowering=False, num_devices=1)
    feed, d = {}, {}
    for name, a in arrays.items():
        feed[f"in_{name}"] = a
        d[name] = nc.dram_tensor(f"in_{name}", a.shape, mybir.dt.from_np(a.dtype), kind="ExternalInput").ap()
    out = nc.dram_tensor("out_0_dram", (B, T, D), F32, kind="ExternalOutput").ap()
    build(nc, d, out)
    return run_bass_kernel_spmd(nc, [feed], core_ids=[0]).results[0]["out_0_dram"]
```

```python
from contextlib import ExitStack

import numpy as np

import concourse.bass as bass
from concourse import mybir
from concourse.alu_op_type import AluOpType as ALU

F32 = mybir.dt.float32
F32R = mybir.dt.float32r
BF16 = mybir.dt.bfloat16
U32 = mybir.dt.uint32
I32 = mybir.dt.int32
ACT = mybir.ActivationFunctionType
AX_X = mybir.AxisListType.X

P = 128
B, T, D = 8, 256, 256
KT = D // P
TT = T // P
C = 77
H, HD = 16, 16
HB = P // HD
E, TOPK = 8, 2
F = 512
FT = F // P
IT = B // 2
EPS = 1e-5
CAP = B * T + P
TILES = (B * T * TOPK + E * (P - 1)) // P
IDLE = TILES - B * T * TOPK // P
SLOTS = E * CAP + IDLE * P
ROW = D + 16
WAYS = 3
TURNS = TILES // WAYS
assert TILES == WAYS * TURNS
EARLY = 2
assert WAYS * EARLY * P <= B * T * TOPK * (IT - 1) // IT - E * (P - 1)
QT = 4
START = 1
VEC_STEPS = 82


def start(eng, *sems, value=START):
    for s in sems:
        for one in s if isinstance(s, list) else [s]:
            eng.sem_inc(one, value)


def this(i, w):
    return WAYS * i + w + 1 + WAYS


def before(i, w):
    return WAYS * i + w + 1


class Steps:

    def __init__(self, eng, sem, base):
        self.eng, self.sem, self.base, self.n = eng, sem, base, 0

    def done(self, instruction):
        self.n += 1
        instruction.then_inc(self.sem, 1)

    def wait(self):
        self.eng.wait_ge(self.sem, self.base + self.n)


def build(nc, d, out):
    with ExitStack() as ctx:
        def sb(name, shape, dt=F32):
            return ctx.enter_context(nc.sbuf_tensor(name, shape, dt))

        def sem(name):
            return ctx.enter_context(nc.semaphore(name))

        def pair(make, name, *a):
            return [make(f"{name}{u}", *a) for u in range(2)]

        w_r, w_k, w_v, w_q, w_out = (sb(n, [P, KT, D]) for n in ("w_r", "w_k", "w_v", "w_q", "w_out"))
        w_kv = sb("w_kv", [P, KT, 2 * D])
        w_g = sb("w_g", [P, KT, E])
        w_o = sb("w_o", [P, FT, D])
        w_1 = sb("w_1", [P, E, KT, 2 * F])
        b_1 = sb("b_1", [P, E, 2 * F])
        chan = sb("chan", [P, 4, KT])
        rows = sb("rows", [P, 3, D])
        gates = sb("gates", [P, 4])
        tg = sb("tg", [P, 4])
        half_tg = sb("half_tg", [P, 1])
        ident = sb("ident", [P, P])
        tri_ones16 = sb("tri_ones16", [P, 2, P], BF16)
        ident16 = sb("ident16", [P, P], BF16)
        headmask = sb("headmask", [P, HB])
        negsel16 = sb("negsel16", [H, H, C], BF16)
        iotas = sb("iotas", [P, 2, E])
        tile_no = sb("tile_no", [1, TILES + 1])
        half_power = sb("half_power", [P, TT])
        zeros = sb("zeros", [P, ROW])
        numbers = sb("numbers", [P, 2 * TT + 1 + WAYS])
        carrier = sb("carrier", [P, 15])
        table_in = sb("table_in", [P, 1])
        stats = pair(sb, "stats", [P, TT, 6])
        mv = pair(sb, "mv", [P, TT, 2])
        vare = pair(sb, "vare", [P, TT])
        rstd = pair(sb, "rstd", [P, TT])
        cx = pair(sb, "cx", [C, D])
        cxT = pair(sb, "cxT", [P, KT, C])
        aT = pair(sb, "aT", [P, KT, T])
        aTs = pair(sb, "aTs", [P, KT, T + 1])
        lower = b_1[:, 0:E // 2, :].rearrange("p e f -> p (e f)")
        diff = lower[:, 0:KT * T].rearrange("p (k t) -> p k t", k=KT)
        ge = [lower[0:C, KT * T + u * T:KT * T + (u + 1) * T] for u in range(2)]
        gT = [lower[0:C, (KT + 2) * T + u * T:(KT + 2) * T + (u + 1) * T] for u in range(2)]
        kT = pair(sb, "kT", [P, KT, C])
        kbd16 = pair(sb, "kbd16", [P, H, C], BF16)
        v = pair(sb, "v", [C, H, HD + 1])
        xr = pair(sb, "xr", [P, KT, T])
        xk = pair(sb, "xk", [P, KT, T])
        qT16 = pair(sb, "qT16", [P, KT, T], BF16)
        mx = pair(sb, "mx", [P, TT, H])
        mx16 = pair(sb, "mx16", [P, TT, H], BF16)
        mT = pair(sb, "mT", [H, T], BF16)
        probs = b_1[0:C, E // 2:E, :].rearrange("p e f -> p (e f)").rearrange("p (c h t) -> p c h t", h=2, t=T)
        rden = pair(sb, "rden", [P, TT, H])
        z3 = pair(sb, "z3", [P, TT, ROW])
        stats3 = pair(sb, "stats3", [P, TT, 6])
        mv3 = pair(sb, "mv3", [P, TT, 2])
        vare3 = pair(sb, "vare3", [P, TT])
        rstd3 = pair(sb, "rstd3", [P, TT])
        lg = pair(sb, "lg", [P, TT, E])
        top = pair(sb, "top", [P, TT, 8])
        topi = pair(sb, "topi", [P, TT, 8], U32)
        topf = pair(sb, "topf", [P, TOPK, TT])
        dl = pair(sb, "dl", [P, TT, E + 1])
        el = sb("el", [P, 2 * TT, E + 1])
        zsum = sb("zsum", [P, 2 * TT])
        den = sb("den", [P, 2 * TT])
        wsum = sb("wsum", [P, 2 * TT])
        meta = sb("meta", [P, TOPK, 2 * TT, 2])
        oh = pair(sb, "oh", [P, TOPK, TT, E])
        chosen = pair(sb, "chosen", [P, TT, E], BF16)
        pos = pair(sb, "pos", [P, TT, E])
        ohpos = pair(sb, "ohpos", [P, TOPK, TT, E])
        slotf = pair(sb, "slotf", [P, TOPK * TT])
        ranks = pair(sb, "ranks", [P, 2, TT, E])
        slot = pair(sb, "slot", [P, TOPK * TT], U32)
        fill = sb("fill", [P, E])
        fill1 = sb("fill1", [P, E])
        xres = sb("xres", [P, B, TT, D])
        filled = sb("filled", [P, E])
        filled_i = sb("filled_i", [P, E], I32)
        fill_i = sb("fill_i", [1, E], I32)
        ntiles = sb("ntiles", [P, E])
        ones_row = sb("ones_row", [P, E])
        cum = sb("cum", [P, E])
        used = sb("used", [P, E + 1])
        step = sb("step", [P, E])
        past = sb("past", [1, TILES, E])
        pastn = sb("pastn", [1, TILES, E])
        tile_e = sb("tile_e", [1, TILES])
        tile_c = sb("tile_c", [1, TILES])
        tile_w = sb("tile_w", [1, TILES], I32)
        tile_r = sb("tile_r", [1, TILES], I32)
        numbers_u = sb("numbers_u", [P, WAYS], U32)
        weight = sb("weight", [P, WAYS])
        until_last_loop = ExitStack()

        def early_sb(name, shape, dt=F32):
            return until_last_loop.enter_context(nc.sbuf_tensor(name, shape, dt))

        kbd = pair(early_sb, "kbd", [P, H, C])
        x = pair(early_sb, "x", [P, TT, D])
        z = pair(early_sb, "z", [P, TT, D])
        th = pair(early_sb, "th", [P, TT, D])
        ka = pair(early_sb, "ka", [P, KT, T])
        yb, qT, att, attT = xr, xk, th, aTs
        sl, gate_h, val_h, sig_h, g_h = ([a[:, :, :].rearrange("p a b -> p (a b)") for a in three] for three in (
            (x[0], x[1], z[0]), (xr[0], xr[1], z[1]), (xk[0], xk[1], w_r), (ka[0], ka[1], w_k), (th[0], th[1], w_v)))
        slT = [a[:, :, 0:P] for a in (aT[0], aT[1], w_q)]
        number = [numbers_u[:, w:w + 1] for w in range(WAYS)]
        all_b = b_1[:, :, :].rearrange("p e f -> p (e f)")
        got = [all_b[:, q * TOPK * F:(q + 1) * TOPK * F] for q in range(QT)]
        g_sum = [all_b[:, (QT * TOPK + q) * F:(QT * TOPK + q + 1) * F] for q in range(QT)]
        until_last_loop.close()
        assert FT * D <= H * C
        w_o_hi, w_o_lo = (sb(n, [P, FT, D], F32R) for n in ("w_o_hi", "w_o_lo"))
        sumT_hi = [sb(f"sumT_hi{q}", [P, FT, P], F32R) for q in range(QT)]
        sumT_lo = [sb(f"sumT_lo{q}", [P, FT, P], F32R) for q in range(QT)]
        y_out = [xr[u] for u in range(2)]

        bank = [ctx.enter_context(nc.psum_tensor(f"bank{i}", [P, 512], F32)) for i in range(8)]
        tb, mb, ring = bank[0:2], bank[2:4], bank[4:8]
        slT_bank = [tb[0][:, 0:D], tb[1][:, 0:D], tb[0][:, D:2 * D]]
        hid = [mb, ring[0:2], ring[2:4]]

        slots_dram = nc.dram_tensor("slots_dram", (SLOTS, ROW), F32, kind="Internal").ap()
        hidden_dram = nc.dram_tensor("hidden_dram", (TOPK * B * T + WAYS * P, F), F32, kind="Internal").ap()

        s_first, s_small, s_w, s_w1, s_b1 = (sem(n) for n in ("s_first", "s_small", "s_w", "s_w1", "s_b1"))
        s_const = sem("s_const")
        s_tg = sem("s_tg")
        s_idle = sem("s_idle")
        x_in, cx_in = pair(sem, "x_in"), pair(sem, "cx_in")
        var_ready, rstd_ready = pair(sem, "var_ready"), pair(sem, "rstd_ready")
        z_ready, zT_ps, aT_ready = pair(sem, "z_ready"), pair(sem, "zT_ps"), pair(sem, "aT_ready")
        h_ps, ge_ready, g_ready = pair(sem, "h_ps"), pair(sem, "ge_ready"), pair(sem, "g_ready")
        k_ps, kT_ready, kbd_ready = pair(sem, "k_ps"), pair(sem, "kT_ready"), pair(sem, "kbd_ready")
        o_ps = pair(sem, "o_ps")
        xr_ready, xk_ready = pair(sem, "xr_ready"), pair(sem, "xk_ready")
        r_ps, th_ready, kk_ps, rk_ready, ka_ready = (
            pair(sem, n) for n in ("r_ps", "th_ready", "kk_ps", "rk_ready", "ka_ready"))
        y_ps, v_ps, v_ready = pair(sem, "y_ps"), pair(sem, "v_ps"), pair(sem, "v_ready")
        x2_done = pair(sem, "x2_done")
        q_ps, q_ready, q16_ready, kbd16_ready = (pair(sem, n) for n in ("q_ps", "q_ready", "q16_ready", "kbd16_ready"))
        s_ps, max_done = sem("s_ps"), sem("max_done")
        mx_ready, mT_ps, mT_ready = pair(sem, "mx_ready"), pair(sem, "mT_ps"), pair(sem, "mT_ready")
        st_ps, exp_done, pv_done = sem("st_ps"), sem("exp_done"), sem("pv_done")
        att_ready, attT_ps, attT_ready, out_ps = (pair(sem, n) for n in ("att_ready", "attT_ps", "attT_ready", "out_ps"))
        var3_ready, rstd3_ready, z3_ready, z3T_ps, aT3_ready = (
            pair(sem, n) for n in ("var3_ready", "rstd3_ready", "z3_ready", "z3T_ps", "aT3_ready"))
        lg_ps, dl_ready, el_ready, oh_ready, rank_ps, slot_ready = (
            pair(sem, n) for n in ("lg_ps", "dl_ready", "el_ready", "oh_ready", "rank_ps", "slot_ready"))
        rank_taken = pair(sem, "rank_taken")
        sent_first, sent, z3_free, meta_put = (pair(sem, n) for n in ("sent_first", "sent", "z3_free", "meta_put"))
        vec_step = sem("vec_step")
        early_ready = sem("early_ready")
        tab_step, fill_ready, tab_ready, pad_done = (sem(n) for n in ("tab_step", "fill_ready", "tab_ready", "pad_done"))
        sl_in, g_sent = ([sem(f"{n}{w}") for w in range(WAYS)] for n in ("sl_in", "g_sent"))
        slT_ps, slT_ready, hh_ps, gate_ready, sig_ready, val_ready, gh_ready, number_ready, g_free = (sem(n) for n in (
            "slT_ps", "slT_ready", "hh_ps", "gate_ready", "sig_ready", "val_ready", "gh_ready", "number_ready", "g_free"))
        got_in = [sem(f"got_in{q}") for q in range(QT)]
        sum_ready, sumT_ps, sumT_ready, sumT_lo_ready, out4_ps, y_ready = (
            sem(n) for n in ("sum_ready", "sumT_ps", "sumT_ready", "sumT_lo_ready", "out4_ps", "y_ready"))
        w_o_hi_ready, w_o_lo_ready = sem("w_o_hi_ready"), sem("w_o_lo_ready")
        y_out_done = pair(sem, "y_out_done")
        s_init = sem("s_init")
        block = ctx.enter_context(nc.Block())

        def m_tok(u):
            return mb[u][:, :].rearrange("p (t d) -> p t d", t=TT)

        def t_chan(u):
            return tb[u][:, :].rearrange("p (k t) -> p k t", k=KT)

        def flat(a):
            return a.rearrange("p a b -> p (a b)")

        def pad(eng, experts):
            eng.wait_ge(s_init, 10)
            eng.wait_ge(fill_ready, 1)
            for e in experts:
                at = eng.value_load(fill_i[0:1, e:e + 1], min_val=0, max_val=E * CAP - P)
                eng.dma_start(slots_dram[bass.ds(at, P), :], zeros[:, :]).then_inc(pad_done, 16)

        def score_bank(u, c):
            return (ring if u == 0 else ring[2:4] + [mb[1], tb[1]])[c % 4]


        @block.sync
        def _(sp):
            def load_x(n, u):
                sp.dma_start(x[u][:, :, :], d["x"][bass.ds(n, 1), :, :].rearrange(
                    "n (t p) d -> p (n t) d", p=P)).then_inc(x_in[u], 16)

            def load_context(n, u):
                sp.dma_start(cxT[u][:, :, :], d["ctxT"][bass.ds(n, 1), :, :].rearrange(
                    "n (k p) c -> p (n k) c", p=P)).then_inc(cx_in[u], 16)
                sp.dma_start(cx[u][:, :], d["ctx"][bass.ds(n, 1), :, :].rearrange(
                    "n c d -> (n c) d")).then_inc(cx_in[u], 16)

            def load_expert(e):
                sp.dma_start(w_1[:, bass.ds(e, 1), :, :].rearrange("p e k f -> p (e k) f"),
                             d["w_1"][bass.ds(e, 1), :, :].rearrange("e (k p) f -> p (e k) f", p=P)).then_inc(s_w1, 16)

            start(sp, x_in, cx_in, sl_in, got_in, y_out_done)
            for u in range(2):
                load_x(u, u)
            for u in range(2):
                load_context(u, u)
            for t, n in ((w_r, "w_r"), (w_k, "w_k"), (w_v, "w_v"), (w_q, "w_q"), (w_out, "w_out"), (w_o, "w_o")):
                sp.dma_start(t[:], d[n]).then_inc(s_w, 16)
            for t, n in ((rows, "rows"), (headmask, "headmask"), (w_g, "w_g"), (ident16, "ident16"),
                         (negsel16, "negsel"), (tri_ones16, "tri_ones"), (iotas, "iotas"), (tile_no, "tile_no"),
                         (numbers, "numbers")):
                sp.dma_start(t[:], d[n]).then_inc(s_small, 16)
            with sp.Fori(0, IT - 1) as i:
                for u in range(2):
                    sp.wait_ge(x2_done[u], START + i + 1)
                    load_x(2 * i + 2 + u, u)
                for u in range(2):
                    sp.wait_ge(v_ps[u], START + i + 1)
                    sp.wait_ge(o_ps[u], START + i + 1)
                    load_context(2 * i + 2 + u, u)
                for j in range(2):
                    load_expert(2 * i + j)
            for e in range(2 * (IT - 1), E):
                load_expert(e)
            for u in range(2):
                sp.wait_ge(xk_ready[u], START + IT)
                sp.wait_ge(o_ps[u], START + IT)
            sp.dma_start(b_1[:, 0:E // 2, :], d["b_1"][:, 0:E // 2, :]).then_inc(s_b1, 16)

            def load_slots(i):
                for w in range(WAYS):
                    row = sp.value_load(tile_r[0:1, bass.ds(WAYS * i + w, 1)], min_val=0, max_val=SLOTS - P)
                    sp.wait_ge(slT_ps, before(i, w))
                    sp.wait_ge(number_ready, before(i, w))
                    sp.dma_start(sl[w][:, 0:ROW], slots_dram[bass.ds(row, P), :]).then_inc(sl_in[w], 16)

            sp.wait_ge(early_ready, 1)
            for u in range(2):
                sp.wait_ge(sent_first[u], 16 * TT * (IT - 1))
                sp.wait_ge(sent[u], 16 * TT * (IT - 1))
                sp.wait_ge(x2_done[u], START + IT)
            sp.wait_ge(zT_ps[0], START + 3 * IT)
            load_slots(0)
            sp.wait_ge(pv_done, START + 16 * IT)
            sp.dma_start(b_1[:, E // 2:E, :], d["b_1"][:, E // 2:E, :]).then_inc(s_b1, 16)
            pad(sp, range(0, E - 2))
            for i in range(1, EARLY):
                load_slots(i)
            sp.wait_ge(tab_ready, 1)
            sp.wait_ge(pad_done, 16 * E)
            sp.wait_ge(s_idle, 16 * IDLE)
            for u in range(2):
                sp.wait_ge(sent_first[u], 16 * TT * IT)
                sp.wait_ge(sent[u], 16 * TT * IT)
            with sp.Fori(EARLY, TURNS) as i:
                load_slots(i)

            def load_hidden(i, q):
                sp.wait_ge(sum_ready, QT * i + q + 1)
                sp.dma_start(got[q], hidden_dram[0:TOPK * B * T, :].rearrange(
                    "(i q p k) f -> q i p (k f)", q=QT, p=P, k=TOPK)[q, bass.ds(i, 1), :, :].rearrange(
                    "i p f -> p (i f)")).then_inc(got_in[q], 16)

            def store(i, u):
                sp.wait_ge(y_ready, QT * i + TT * (u + 1) + QT)
                sp.dma_start(out.rearrange("(i u) (t p) d -> u i p t d", u=2, p=P)[u, bass.ds(i, 1), :, :, :].rearrange(
                    "i p t d -> p (i t) d"),
                             y_out[u][:, :, :]).then_inc(y_out_done[u], 16)

            for w in range(WAYS):
                sp.wait_ge(g_sent[w], 16 * TURNS)
            sp.wait_ge(gh_ready, TILES + WAYS)
            for q in range(QT):
                load_hidden(0, q)
            load_hidden(1, 0)
            load_hidden(1, 1)
            with sp.Fori(0, IT - 2) as i:
                for t in range(TT):
                    load_hidden(i + 1, TT + t)
                store(i, 0)
                for t in range(TT):
                    load_hidden(i + 2, t)
                store(i, 1)
            for t in range(TT):
                load_hidden(IT - 1, TT + t)
            for i in range(IT - 2, IT):
                for u in range(2):
                    store(i, u)
            for u in range(2):
                sp.wait_ge(y_out_done[u], START + 16 * IT)

        @block.gpsimd
        def _(pool):
            start(pool, rstd_ready, kbd_ready, kbd16_ready, rstd3_ready, z3_free, meta_put)
            start(pool, number_ready, g_free, value=WAYS)
            start(pool, sum_ready, value=QT)
            pool.memset(half_power[:, :], -0.5).then_inc(s_init, 1)
            for u in range(2):
                pool.memset(aTs[u][:, :, 0:1], 0.0).then_inc(s_init, 1)
                pool.memset(v[u][:, :, HD:HD + 1], 1.0).then_inc(s_init, 1)
            pool.memset(ones_row[:, :], 1.0).then_inc(s_init, 1)
            pool.memset(zeros[:, :], 0.0).then_inc(s_init, 1)
            for u in range(2):
                pool.memset(z3[u][:, :, D:ROW], 0.0).then_inc(s_init, 1)
            pool.wait_ge(s_init, 9)

            def inverse_deviation(i, k):
                for u in range(2):
                    pool.wait_ge(var_ready[u], START + 3 * i + k + 1)
                    pool.tensor_tensor(rstd[u][:, :], vare[u][:, :], half_power[:, :], ALU.pow)\
                        .then_inc(rstd_ready[u], 1)

            def keys(i):
                for dst, ready, used in ((kbd16, kbd16_ready, s_ps), (kbd, kbd_ready, st_ps)):
                    for u in range(2):
                        pool.wait_ge(kT_ready[u], START + i + 1)
                        pool.wait_ge(used, START + 16 * i)
                        for k in range(KT):
                            pool.tensor_tensor(
                                dst[u][:, k * HB:(k + 1) * HB, :],
                                kT[u][:, k, :].unsqueeze(1).to_broadcast([P, HB, C]),
                                headmask[:, :].unsqueeze(2).to_broadcast([P, HB, C]), ALU.mult).then_inc(ready[u], 1)

            def note(i, w):
                pool.wait_ge(sl_in[w], START + 16 * (i + 1))
                pool.wait_ge(gh_ready, before(i, w))
                pool.tensor_tensor(weight[:, w:w + 1], sl[w][:, D + 1:D + 2], zeros[:, 0:1], ALU.add)
                pool.tensor_scalar(number[w], sl[w][:, D:D + 1], numbers[:, 2 * TT + 1 + w:2 * TT + 2 + w], None,
                                   ALU.min).then_inc(number_ready, 1)

            def turn(i, more):
                if more:
                    inverse_deviation(i + 1, 0)
                else:
                    for w in range(WAYS):
                        note(0, w)
                for u in range(2):
                    pool.wait_ge(var3_ready[u], START + i + 1)
                    pool.tensor_tensor(rstd3[u][:, :], vare3[u][:, :], half_power[:, :], ALU.pow)\
                        .then_inc(rstd3_ready[u], 1)
                if more:
                    inverse_deviation(i + 1, 1)
                    keys(i + 1)
                    inverse_deviation(i + 1, 2)
                for k, counts in enumerate((sent_first, sent)):
                    for u in range(2):
                        if k == 0:
                            pool.wait_ge(slot_ready[u], START + i + 1)
                        else:
                            pool.wait_ge(sent_first[u], 16 * TT * (i + 1))
                        pool.tensor_tensor(z3[u][:, :, D:D + 2], meta[:, k, TT * u:TT * (u + 1), :],
                                           zeros[:, 0:2 * TT].rearrange("p (t c) -> p t c", t=TT), ALU.add)\
                            .then_inc(meta_put[u], 1)
                        pool.wait_ge(meta_put[u], START + TOPK * i + k + 1)
                        pool.tensor_tensor(carrier[:, 3 + u:4 + u], zeros[:, 0:1], zeros[:, 0:1], ALU.add)
                        for t in range(TT):
                            c = k * TT + t
                            pool.indirect_dma_start(
                                out=slots_dram, out_offset=bass.IndirectOffsetOnAxis(ap=slot[u][:, c:c + 1], axis=0),
                                in_=z3[u][:, t, :], in_offset=None).then_inc(counts[u], 16)
                for u in range(2):
                    pool.wait_ge(sent[u], 16 * TT * (i + 1))
                    pool.tensor_tensor(carrier[:, 7 + u:8 + u], zeros[:, 0:1], zeros[:, 0:1], ALU.add)\
                        .then_inc(z3_free[u], 1)

            inverse_deviation(0, 0)
            inverse_deviation(0, 1)
            pool.wait_ge(s_small, 144)
            keys(0)
            inverse_deviation(0, 2)
            pool.tensor_copy(zeros[:, D:D + 1], numbers[:, 2 * TT:2 * TT + 1]).then_inc(s_init, 1)
            pool.wait_ge(s_init, 10)
            for i in range(IDLE):
                pool.dma_start(slots_dram[E * CAP + i * P:E * CAP + (i + 1) * P, :],
                               zeros[:, :]).then_inc(s_idle, 16)
            with pool.Fori(0, IT - 1) as i:
                turn(i, True)
            turn(IT - 1, False)

            def send(i, w):
                pool.wait_ge(number_ready, this(i, w))
                pool.wait_ge(gh_ready, this(i, w))
                pool.tensor_tensor(carrier[:, 9 + w:10 + w], zeros[:, 0:1], zeros[:, 0:1], ALU.add)
                pool.indirect_dma_start(out=hidden_dram, out_offset=bass.IndirectOffsetOnAxis(ap=number[w], axis=0),
                                        in_=g_h[w], in_offset=None).then_inc(g_sent[w], 16)

            def free(i, w):
                pool.wait_ge(g_sent[w], 16 * (i + 1))
                pool.tensor_tensor(carrier[:, 12 + w:13 + w], zeros[:, 0:1], zeros[:, 0:1], ALU.add)\
                    .then_inc(g_free, 1)

            send(0, 0)
            send(0, 1)
            with pool.Fori(0, TURNS - 1) as i:
                free(i, 0)
                note(i + 1, 0)
                send(i, 2)
                free(i, 1)
                note(i + 1, 1)
                send(i + 1, 0)
                free(i, 2)
                note(i + 1, 2)
                send(i + 1, 1)
            free(TURNS - 1, 0)
            send(TURNS - 1, 2)

            with pool.Fori(0, IT) as i:
                for q in range(QT):
                    pool.wait_ge(got_in[q], START + 16 * (i + 1))
                    pool.wait_ge(sumT_ps, QT * i + q + 1)
                    pool.tensor_tensor(g_sum[q], got[q][:, 0:F], got[q][:, F:2 * F], ALU.add).then_inc(sum_ready, 1)

        @block.scalar
        def _(act):
            for t, n in ((gates, "gates"), (ident, "ident"), (chan, "chan"), (w_kv, "w_kv")):
                act.dma_start(t[:], d[n]).then_inc(s_first, 16)
            start(act, aT_ready, ge_ready, kT_ready, th_ready, rk_ready, ka_ready, q16_ready, q_ready,
                  mT_ready, exp_done, attT_ready, aT3_ready, el_ready)
            start(act, slT_ready, sig_ready, value=WAYS)
            start(act, sumT_ready, value=QT)
            act.wait_ge(s_first, 64)
            act.activation(tg[:, :], gates[:, :], ACT.Tanh).then_inc(s_tg, 1)

            def table(function):
                act.activation(table_in[:, :], half_tg[:, :], function)

            def transposed(i, k, u, before):
                dst = aTs[u][:, :, 1:T + 1] if k == 1 else aT[u][:, :, :]
                act.wait_ge(zT_ps[u], START + 3 * i + k + 1)
                before()
                act.activation(dst, t_chan(u), ACT.Copy).then_inc(aT_ready[u], 1)

            def layer0_context(i):
                for u in range(2):
                    transposed(i, 0, u, lambda: act.wait_ge(q_ps[u], START + i))
                for u in range(2):
                    act.wait_ge(h_ps[u], START + i + 1)
                    act.wait_ge(g_ready[u], START + i)
                    act.activation(ge[u], mb[u][0:C, 0:T], ACT.Gelu).then_inc(ge_ready[u], 1)
                for u in range(2):
                    act.wait_ge(k_ps[u], START + i + 1)
                    act.wait_ge(kbd16_ready[u], START + KT * i)
                    act.wait_ge(kbd_ready[u], START + KT * i)
                    for k in range(KT):
                        ins = act.activation(kT[u][:, k, :], tb[u][:, k * C:(k + 1) * C], ACT.Identity,
                                             bias=chan[:, 3, k:k + 1])
                    ins.then_inc(kT_ready[u], 1)

            def layer0_mix(i, router):
                for u in range(2):
                    transposed(i, 1, u, lambda: act.wait_ge(lg_ps[u], START + i))
                for u in range(2):
                    act.wait_ge(r_ps[u], START + i + 1)
                    act.wait_ge(attT_ps[u], START + i)
                    act.activation(flat(th[u][:, :, :]), tb[u][:, :], ACT.Tanh, scale=0.5).then_inc(th_ready[u], 1)
                    act.wait_ge(kk_ps[u], START + i + 1)
                    act.wait_ge(y_ps[u], START + i)
                    act.activation(flat(ka[u][:, :, :]), mb[u][:, :], ACT.Relu).then_inc(rk_ready[u], 1)
                    act.wait_ge(rk_ready[u], START + i + 1)
                    act.activation(flat(ka[u][:, :, :]), flat(ka[u][:, :, :]), ACT.Square).then_inc(ka_ready[u], 1)
                table(ACT.Exp)
                router()

            def queries(i):
                for u in range(2):
                    transposed(i, 2, u, lambda: act.wait_ge(h_ps[u], START + i + 1))
                    act.wait_ge(q_ps[u], START + i + 1)
                    act.wait_ge(s_ps, START + 16 * i)
                    for dst, ready in ((qT16, q16_ready), (qT, q_ready)):
                        for k in range(KT):
                            ins = act.activation(dst[u][:, k, :], mb[u][:, k * T:(k + 1) * T], ACT.Identity,
                                                 bias=chan[:, 2, k:k + 1])
                        ins.then_inc(ready[u], 1)

            def maxima(i, u):
                act.wait_ge(mT_ps[u], START + i + 1)
                act.activation(mT[u][:, :], tb[u][0:H, 0:T], ACT.Copy).then_inc(mT_ready[u], 1)

            def router(i):
                for u in range(2):
                    act.wait_ge(dl_ready[u], START + i + 1)
                    act.activation(el[:, TT * u:TT * (u + 1), :], dl[u][:, :, :], ACT.Exp).then_inc(el_ready[u], 1)

            def turn(i, more):
                maxima(i, 0)
                for u in range(2):
                    for c in range(H // 2):
                        if u == 0 and c == 2:
                            maxima(i, 1)
                        act.wait_ge(st_ps, START + 16 * i + 8 * u + c + 1)
                        if u == 0 and c == 0:
                            act.wait_ge(pv_done, START + 16 * i)
                        if u == 1:
                            act.wait_ge(pv_done, START + 16 * i + c + 1)
                        act.activation(flat(probs[:, c, :, :]), ring[c % 4][0:C, :], ACT.Exp,
                                       scale=HD ** -0.5).then_inc(exp_done, 1)
                if more:
                    table(ACT.Gelu)
                for u in range(2):
                    act.wait_ge(attT_ps[u], START + i + 1)
                    act.activation(attT[u][:, :, 1:T + 1], t_chan(u), ACT.Copy).then_inc(attT_ready[u], 1)
                if more:
                    layer0_context(i + 1)
                for u in range(2):
                    act.wait_ge(z3T_ps[u], START + i + 1)
                    act.wait_ge(out_ps[u], START + i + 1)
                    act.activation(aTs[u][:, :, 1:T + 1], ring[2 + u][:, :].rearrange("p (k t) -> p k t", k=KT),
                                   ACT.Copy).then_inc(aT3_ready[u], 1)
                if more:
                    table(ACT.Tanh)
                    layer0_mix(i + 1, lambda: router(i))
                    queries(i + 1)
                else:
                    router(i)

            layer0_context(0)
            layer0_mix(0, lambda: None)
            queries(0)
            with act.Fori(0, IT - 1) as i:
                turn(i, True)
            turn(IT - 1, False)

            def take_in(i, w):
                act.wait_ge(slT_ps, this(i, w))
                act.activation(slT[w], slT_bank[w].rearrange("p (k t) -> p k t", k=KT), ACT.Copy)\
                    .then_inc(slT_ready, 1)

            def gate(i, w):
                act.wait_ge(gate_ready, this(i, w))
                act.wait_ge(gh_ready, before(i, w))
                act.activation(sig_h[w], gate_h[w], ACT.Sigmoid).then_inc(sig_ready, 1)

            def slot_turn(i, more):
                table(ACT.Sigmoid)
                for w in range(WAYS):
                    if w < WAYS - 1:
                        take_in(i, w + 1)
                    elif more:
                        take_in(i + 1, 0)
                    gate(i, w)

            for w in range(WAYS):
                take_in(0, w)
            pad(act, range(E - 2, E))
            table(ACT.Sigmoid)
            gate(0, 0)
            take_in(1, 0)
            gate(0, 1)
            gate(0, 2)
            with act.Fori(1, TURNS - 1) as i:
                slot_turn(i, True)
            slot_turn(TURNS - 1, False)

            def transposed_sum(i, q):
                act.wait_ge(sumT_ps, QT * i + q + 1 + QT)
                act.wait_ge(out4_ps, QT * i + q + 1)
                act.activation(sumT_hi[q][:, :, :], (tb + ring[2:4])[q][:, :].rearrange("p (a b) -> p a b", a=FT), ACT.Copy)\
                    .then_inc(sumT_ready, 1)

            act.wait_ge(hh_ps, 2 * TILES)
            act.activation(w_o_hi[:, :, :], w_o[:, :, :], ACT.Copy).then_inc(w_o_hi_ready, 1)

            with act.Fori(0, IT) as i:
                for q in range(QT):
                    transposed_sum(i, q)

        @block.tensor
        def _(pe):
            start(pe, zT_ps, h_ps, k_ps, o_ps, r_ps, kk_ps, y_ps, v_ps, q_ps, s_ps, mT_ps, st_ps, pv_done, attT_ps, out_ps,
                  z3T_ps, lg_ps, rank_ps)
            start(pe, slT_ps, value=WAYS)
            start(pe, sumT_ps, out4_ps, value=QT)
            pe.wait_ge(s_first, 64)

            def transposes(dst, src):
                for kt in range(KT):
                    for t in range(TT):
                        ins = pe.transpose(dst[:, kt, t * P:(t + 1) * P], src[:, t, kt * P:(kt + 1) * P], ident[:, :])
                return ins

            def transpose(i, k, u):
                pe.wait_ge(z_ready[u], START + 3 * i + k + 1)
                transposes(t_chan(u), z[u]).then_inc(zT_ps[u], 1)

            def by_token(dst, actT, w):
                for t in range(TT):
                    for kt in range(KT):
                        ins = pe.matmul(dst[:, t, :], actT[:, kt, t * P:(t + 1) * P], w[:, kt, :],
                                        start=(kt == 0), stop=(kt == KT - 1))
                return ins

            def by_channel(dst, w, actT, off=0):
                for m in range(KT):
                    for kt in range(KT):
                        ins = pe.matmul(dst[:, m, :], w[:, kt, off + m * P:off + (m + 1) * P], actT[:, kt, :],
                                        start=(kt == 0), stop=(kt == KT - 1))
                return ins

            def layer0_hidden(i):
                for u in range(2):
                    pe.wait_ge(aT_ready[u], START + 3 * i + 1)
                    pe.wait_ge(cx_in[u], START + 32 * (i + 1))
                    pe.wait_ge(var3_ready[u], START + i)
                    for kt in range(KT):
                        ins = pe.matmul(mb[u][0:C, 0:T], cxT[u][:, kt, :], aT[u][:, kt, :],
                                        start=(kt == 0), stop=(kt == KT - 1))
                    ins.then_inc(h_ps[u], 1)
                    for m in range(KT):
                        for kt in range(KT):
                            ins = pe.matmul(tb[u][:, m * C:(m + 1) * C], w_kv[:, kt, m * P:(m + 1) * P],
                                            cxT[u][:, kt, :], start=(kt == 0), stop=(kt == KT - 1))
                    ins.then_inc(k_ps[u], 1)

            def layer0_context(i):
                for u in range(2):
                    pe.wait_ge(g_ready[u], START + i + 1)
                    for t in range(TT):
                        ins = pe.matmul(m_tok(u)[:, t, :], gT[u][:, t * P:(t + 1) * P], cx[u][:, :],
                                        start=True, stop=True)
                    ins.then_inc(o_ps[u], 1)

            def layer0_mix(i, router):
                for u in range(2):
                    pe.wait_ge(kT_ready[u], START + i + 1)
                    transpose(i, 1, u)

                def receptance(u):
                    pe.wait_ge(aT_ready[u], START + 3 * i + 2)
                    pe.wait_ge(xr_ready[u], START + i + 1)
                    by_token(tb[u][:, :].rearrange("p (t d) -> p t d", t=TT), xr[u], w_r).then_inc(r_ps[u], 1)

                def key(u):
                    pe.wait_ge(xk_ready[u], START + i + 1)
                    by_channel(mb[u][:, :].rearrange("p (k t) -> p k t", k=KT), w_k, xk[u]).then_inc(kk_ps[u], 1)

                def value(u):
                    pe.wait_ge(ka_ready[u], START + i + 1)
                    by_token(m_tok(u), ka[u], w_v).then_inc(y_ps[u], 1)

                receptance(0)
                key(0)
                receptance(1)
                value(0)
                key(1)
                for u in range(2):
                    pe.wait_ge(aT3_ready[u], START + i)
                    for kt in range(KT):
                        ins = pe.matmul(ring[2 + u][0:C, 0:D], cxT[u][:, kt, :], w_kv[:, kt, D:2 * D],
                                        start=(kt == 0), stop=(kt == KT - 1))
                    ins.then_inc(v_ps[u], 1)
                value(1)
                router()

            def queries(i):
                def project(u):
                    pe.wait_ge(aT_ready[u], START + 3 * i + 3)
                    by_channel(mb[u][:, :].rearrange("p (k t) -> p k t", k=KT), w_q, aT[u]).then_inc(q_ps[u], 1)

                def scores(u, chunks):
                    pe.wait_ge(q16_ready[u], START + i + 1)
                    pe.wait_ge(kbd16_ready[u], START + KT * (i + 1))
                    for c in chunks:
                        t, hq = c // 4, c % 4
                        if c >= 4:
                            pe.wait_ge(max_done, START + 16 * i + 8 * u + c - 3)
                        elif u == 1 and c < 2:
                            pe.wait_ge(max_done, START + 16 * i + c + 7)
                        elif u == 1 and c == 2:
                            pe.wait_ge(q_ready[1], START + i + 1)
                        elif u == 0 and c == 0:
                            pe.wait_ge(exp_done, START + 16 * i)
                            for b in range(2):
                                pe.wait_ge(rank_taken[b], START + i)
                                pe.wait_ge(v_ready[b], START + i + 1)
                        pe.matmul(score_bank(u, c)[:, 0:4 * C], qT16[u][:, hq // 2, t * P:(t + 1) * P],
                                  flat(kbd16[u][:, 4 * hq:4 * hq + 4, :]), start=True, stop=True).then_inc(s_ps, 1)

                pe.wait_ge(th_ready[0], START + i + 1)
                transpose(i, 2, 0)
                project(0)
                pe.wait_ge(th_ready[1], START + i + 1)
                transpose(i, 2, 1)
                scores(0, range(0, 4))
                project(1)
                scores(0, range(4, 8))
                scores(1, range(0, 4))
                maxima(i, 0)
                start_attention(i, 0)
                less_maxima(i, 0, 0)
                scores(1, range(4, 6))
                less_maxima(i, 0, 1)
                scores(1, range(6, 8))

            def start_attention(i, u):
                pe.wait_ge(q_ready[u], START + i + 1)
                pe.wait_ge(kbd_ready[u], START + KT * (i + 1))
                pe.wait_ge(mT_ready[u], START + i + 1)

            def less_maxima(i, u, c):
                if u == 0 and c < 4:
                    pe.wait_ge(max_done, START + 16 * i + c + (5 if c < 2 else 11))
                else:
                    pe.wait_ge(exp_done, START + 16 * i + 8 * u + c - 3)
                for h in (2 * c, 2 * c + 1):
                    dst = ring[c % 4][0:C, (h % 2) * T:(h % 2 + 1) * T]
                    pe.matmul(dst, negsel16[:, h, :], mT[u][:, :], start=True, stop=False)
                    ins = pe.matmul(dst, kbd[u][:, h, :], qT[u][:, h // HB, :], start=False, stop=True)
                ins.then_inc(st_ps, 1)

            def maxima(i, u):
                pe.wait_ge(mx_ready[u], START + i + 1)
                for t in range(TT):
                    ins = pe.matmul(tb[u][0:H, t * P:(t + 1) * P], mx16[u][:, t, :], ident16[:, :],
                                    start=True, stop=True)
                ins.then_inc(mT_ps[u], 1)

            def weigh(i, u, c):
                pe.wait_ge(exp_done, START + 16 * i + 8 * u + c + 1)
                if c == 0:
                    pe.wait_ge(q_ready[u], START + i + 1)
                    pe.wait_ge(mT_ready[u], START + i + 1)
                for h in (2 * c, 2 * c + 1):
                    for t in range(TT):
                        dst = (mb, tb)[t][u]
                        ins = pe.matmul(dst[:, h * (HD + 1):(h + 1) * (HD + 1)],
                                        probs[:, c, h % 2, t * P:(t + 1) * P], v[u][:, h, :],
                                        start=True, stop=True)
                ins.then_inc(pv_done, 1)

            def ranks_of(i):
                for u in range(2):
                    pe.wait_ge(oh_ready[u], START + i + 1)
                    for m in range(2):
                        ins = pe.matmul(ring[u][:, (1 + m) * TT * E:(2 + m) * TT * E], tri_ones16[:, m, :],
                                        flat(chosen[u][:, :, :]), start=True, stop=True)
                    ins.then_inc(rank_ps[u], 1)

            def turn(i, more):
                for u in range(2):
                    if u == 1:
                        start_attention(i, 1)
                    for c in range(8):
                        if u == 0 and c == 2:
                            maxima(i, 1)
                        if 8 * u + c >= 2:
                            less_maxima(i, u, c)
                        if 8 * u + c >= 2:
                            weigh(i, (8 * u + c - 2) // 8, (c - 2) % 8)
                weigh(i, 1, 6)
                weigh(i, 1, 7)
                for u in range(2):
                    pe.wait_ge(att_ready[u], START + i + 1)
                    transposes(t_chan(u), att[u]).then_inc(attT_ps[u], 1)
                for u in range(2):
                    pe.wait_ge(attT_ready[u], START + i + 1)
                    by_token(m_tok(u), attT[u][:, :, 1:T + 1], w_out).then_inc(out_ps[u], 1)
                    if more:
                        transpose(i + 1, 0, u)
                if more:
                    layer0_hidden(i + 1)
                for u in range(2):
                    pe.wait_ge(z3_ready[u], START + i + 1)
                    transposes(ring[2 + u][:, :].rearrange("p (k t) -> p k t", k=KT), z3[u]).then_inc(z3T_ps[u], 1)
                if more:
                    layer0_context(i + 1)
                for u in range(2):
                    pe.wait_ge(aT3_ready[u], START + i + 1)
                    for t in range(TT):
                        for kt in range(KT):
                            ins = pe.matmul(ring[u][:, t * E:(t + 1) * E], aTs[u][:, kt, 1 + t * P:1 + (t + 1) * P],
                                            w_g[:, kt, :], start=(kt == 0), stop=(kt == KT - 1))
                    ins.then_inc(lg_ps[u], 1)
                if more:
                    layer0_mix(i + 1, lambda: ranks_of(i))
                    queries(i + 1)
                else:
                    ranks_of(i)

            for u in range(2):
                transpose(0, 0, u)
            layer0_hidden(0)
            layer0_context(0)
            pe.wait_ge(s_w, 96)
            pe.wait_ge(s_small, 144)
            layer0_mix(0, lambda: None)
            queries(0)
            with pe.Fori(0, IT - 1) as i:
                turn(i, True)
            turn(IT - 1, False)

            pe.wait_ge(early_ready, 1)
            pe.wait_ge(s_w1, 16 * E)
            for u in range(2):
                pe.wait_ge(rank_taken[u], START + IT)
                pe.wait_ge(var3_ready[u], START + IT)

            def take_in(i, w):
                pe.wait_ge(sl_in[w], START + 16 * (i + 1))
                pe.wait_ge(slT_ready, before(i, w))
                for kt in range(KT):
                    ins = pe.transpose(slT_bank[w][:, kt * P:(kt + 1) * P], sl[w][:, kt * P:(kt + 1) * P], ident[:, :])
                ins.then_inc(slT_ps, 1)

            def hidden(i, w, between):
                e = pe.value_load(tile_w[0:1, bass.ds(WAYS * i + w, 1)], min_val=0, max_val=E - 1)
                pe.wait_ge(slT_ready, this(i, w))
                pe.wait_ge(gh_ready, before(i, w))
                for m in (1, 0):
                    for kt in range(KT):
                        ins = pe.matmul(hid[w][m][:, :], slT[w][:, kt, :],
                                        w_1[:, bass.ds(e, 1), kt, m * F:(m + 1) * F].rearrange("p e f -> p (e f)"),
                                        start=(kt == 0), stop=(kt == KT - 1))
                    ins.then_inc(hh_ps, 1)
                    if m == 1:
                        between()

            def slot_turn(i, more):
                for w in range(WAYS):
                    hidden(i, w, lambda: take_in(i, w + 1) if w < WAYS - 1 else take_in(i + 1, 0) if more else None)

            take_in(0, 0)
            for i in range(EARLY):
                slot_turn(i, True)
            pe.wait_ge(tab_ready, 1)
            with pe.Fori(EARLY, TURNS - 1) as i:
                slot_turn(i, True)
            slot_turn(TURNS - 1, False)

            def transpose_sum(i, q):
                pe.wait_ge(sum_ready, QT * i + q + 1 + QT)
                pe.wait_ge(sumT_lo_ready, QT * i + q + 1)
                for a in range(FT):
                    ins = pe.transpose((tb + ring[2:4])[q][:, a * P:(a + 1) * P],
                                       g_sum[q][:, a * P:(a + 1) * P], ident[:, :])
                ins.then_inc(sumT_ps, 1)

            def project(i, q):
                pe.wait_ge(sumT_ready, QT * i + q + 1 + QT)
                pe.wait_ge(y_ready, QT * i + q + 1)
                products = (mb + ring[0:2])[q][:, 0:D]
                for a in range(FT):
                    pe.matmul(products, sumT_hi[q][:, a, :], w_o_hi[:, a, :], start=(a == 0), stop=False)
                    pe.matmul(products, sumT_hi[q][:, a, :], w_o_lo[:, a, :], start=False, stop=False)
                pe.wait_ge(sumT_lo_ready, QT * i + q + 1 + QT)
                for a in range(FT):
                    ins = pe.matmul(products, sumT_lo[q][:, a, :], w_o_hi[:, a, :], start=False, stop=(a == FT - 1))
                ins.then_inc(out4_ps, 1)

            def last_turn(i, more):
                for q in range(QT):
                    if q < QT - 1:
                        transpose_sum(i, q + 1)
                    elif more:
                        transpose_sum(i + 1, 0)
                    project(i, q)

            transpose_sum(0, 0)
            pe.wait_ge(w_o_hi_ready, 1)
            pe.wait_ge(w_o_lo_ready, 1)
            with pe.Fori(0, IT - 1) as i:
                last_turn(i, True)
            last_turn(IT - 1, False)

        @block.vector
        def _(dve):
            start(dve, var_ready, z_ready, g_ready, xr_ready, xk_ready, v_ready, x2_done, max_done, mx_ready, att_ready,
                  dl_ready, var3_ready, z3_ready, rank_taken,
                  oh_ready, slot_ready)
            start(dve, gate_ready, gh_ready, val_ready, value=WAYS)
            start(dve, sumT_lo_ready, y_ready, value=QT)
            dve.wait_ge(s_init, 9)

            def residual(i, u):
                return xres[:, bass.ds(2 * i + u, 1), :, :].rearrange("p n t d -> p (n t) d")

            def statistics(c, src, buffers, ready):
                stats_u, mv_u, vare_u = buffers
                dve.memset(carrier[:, 0:1], 0.0)
                for t in range(TT):
                    c.done(dve.bn_stats(stats_u[:, t, :], src[:, t, :]))
                c.wait()
                dve.memset(carrier[:, 0:1], 0.0)
                for t in range(TT):
                    c.done(dve.bn_aggr(mv_u[:, t, :], stats_u[:, t, :]))
                c.wait()
                dve.tensor_scalar(vare_u[:, :], mv_u[:, :, 1], EPS, None, ALU.add).then_inc(ready, 1)

            def moments(u):
                return stats[u], mv[u], vare[u]

            def normalise(i, k, u, src):
                dve.wait_ge(rstd_ready[u], START + 3 * i + k + 1)
                dve.wait_ge(zT_ps[u], START + 3 * i + k)
                for t in range(TT):
                    ins = dve.tensor_scalar(z[u][:, t, :], src[:, t, :], mv[u][:, t, 0:1], rstd[u][:, t:t + 1],
                                            ALU.subtract, ALU.mult)
                ins.then_inc(z_ready[u], 1)

            def layer0_enter(i, c):
                for u in range(2):
                    dve.wait_ge(x_in[u], START + 16 * (i + 1))
                    statistics(c, x[u], moments(u), var_ready[u])
                for u in range(2):
                    normalise(i, 0, u, x[u])

            def layer0_gate(i, c):
                for u in range(2):
                    dve.wait_ge(ge_ready[u], START + i + 1)
                    dve.wait_ge(o_ps[u], START + i)
                    dve.tensor_tensor(gT[u], ge[u], mb[u][0:C, 0:T], ALU.mult).then_inc(g_ready[u], 1)

            def layer0_context(i, c):
                for u in range(2):
                    dve.wait_ge(o_ps[u], START + i + 1)
                    c.done(dve.scalar_tensor_tensor(flat(x[u][:, :, :]), mb[u][:, :], tg[:, 0:1], flat(x[u][:, :, :]),
                                                    ALU.mult, ALU.add))
                    c.wait()
                    statistics(c, x[u], moments(u), var_ready[u])
                for u in range(2):
                    normalise(i, 1, u, x[u])

            def layer0_shift(i, c):
                for u in range(2):
                    dve.wait_ge(aT_ready[u], START + 3 * i + 2)
                    dve.wait_ge(xk_ready[1 - u], START + i + u)
                    cur, prev = aTs[u][:, :, 1:T + 1], aTs[u][:, :, 0:T]
                    c.done(dve.tensor_tensor(diff[:, :, :], cur, prev, ALU.subtract))
                    c.wait()
                    dve.wait_ge(st_ps, START + 16 * i)
                    for dst, m, s in ((xr, 0, xr_ready), (xk, 1, xk_ready)):
                        for k in range(KT):
                            ins = dve.scalar_tensor_tensor(dst[u][:, k, :], diff[:, k, :], chan[:, m, k:k + 1],
                                                           prev[:, k, :], ALU.mult, ALU.add)
                        ins.then_inc(s[u], 1)

            def weights(i, c):
                for u in range(2):
                    dve.wait_ge(el_ready[u], START + i + 1)
                    dve.wait_ge(z3_free[u], START + i)
                second = el[:, :, E]
                c.done(dve.tensor_reduce(zsum[:, :], el[:, :, 0:E], AX_X, ALU.add))
                c.wait()
                c.done(dve.scalar_tensor_tensor(den[:, :], zsum[:, :], 1e-9, second, ALU.mult, ALU.add))
                c.wait()
                c.done(dve.tensor_scalar(zsum[:, :], den[:, :], 1.0, None, ALU.add))
                c.wait()
                c.done(dve.reciprocal(den[:, :], zsum[:, :]))
                c.wait()
                c.done(dve.tensor_scalar(meta[:, 0, :, 1], den[:, :], tg[:, 3:4], None, ALU.mult))
                c.done(dve.scalar_tensor_tensor(meta[:, 1, :, 1], den[:, :], tg[:, 3:4], second, ALU.mult, ALU.mult))
                for k in range(TOPK):
                    c.done(dve.tensor_scalar(meta[:, k, :, 0], numbers[:, 0:2 * TT], float(k), None, ALU.add))
                c.done(dve.scalar_tensor_tensor(wsum[:, :], second, 1.0, den[:, :], ALU.add, ALU.mult))
                c.wait()
                c.done(dve.tensor_scalar(numbers[:, 0:2 * TT], numbers[:, 0:2 * TT], float(2 * T * TOPK), None, ALU.add))

            def output_bias(i, c):
                for u in range(2):
                    for t in range(TT):
                        dve.scalar_tensor_tensor(
                            xres[:, bass.ds(2 * i + u, 1), t, :].rearrange("p n d -> p (n d)"), rows[:, 2, :],
                            wsum[:, TT * u + t:TT * u + t + 1], residual(i, u)[:, t, :], ALU.mult, ALU.add)

            def choose(i, c):
                for u in range(2):
                    dve.wait_ge(lg_ps[u], START + i + 1)
                    c.done(dve.tensor_copy(flat(lg[u][:, :, :]), ring[u][:, 0:TT * E]))
                    c.wait()
                    dve.memset(carrier[:, 0:1], 0.0)
                    for t in range(TT):
                        c.done(dve.max(top[u][:, t, :], lg[u][:, t, :]))
                    c.wait()
                    dve.tensor_tensor(dl[u][:, :, 0:E], lg[u][:, :, :], top[u][:, :, 0:1].to_broadcast([P, TT, E]),
                                      ALU.subtract)
                    dve.tensor_tensor(dl[u][:, :, E], top[u][:, :, 1], top[u][:, :, 0], ALU.subtract)\
                        .then_inc(dl_ready[u], 1)
                    for t in range(TT):
                        c.done(dve.max_index(topi[u][:, t, :], top[u][:, t, :], lg[u][:, t, :]))
                    c.wait()
                    c.done(dve.tensor_copy(topf[u][:, :, :], topi[u][:, :, 0:TOPK].rearrange("p t k -> p k t")))
                    c.wait()
                    wide = [P, TOPK * TT, E]
                    c.done(dve.tensor_tensor(oh[u][:, :, :, :].rearrange("p k t e -> p (k t) e"),
                                             iotas[:, 0, :].unsqueeze(1).to_broadcast(wide),
                                             flat(topf[u][:, :, :]).unsqueeze(2).to_broadcast(wide), ALU.is_equal))
                    c.wait()
                    dve.tensor_tensor(chosen[u][:, :, :], oh[u][:, 0, :, :], oh[u][:, 1, :, :], ALU.add)\
                        .then_inc(oh_ready[u], 1)

            def take_ranks(i, c):
                for u in range(2):
                    dve.wait_ge(rank_ps[u], START + i + 1)
                    dve.tensor_copy(ranks[u][:, :, :, :].rearrange("p m t e -> p (m t e)"),
                                    ring[u][:, TT * E:3 * TT * E]).then_inc(rank_taken[u], 1)

            def place(i, c):
                for u in range(2):
                    dve.wait_ge(rank_taken[u], START + i + 1)
                    dve.tensor_tensor(pos[u][:, 0, :], fill[:, :], ranks[u][:, 0, 0, :], ALU.add)
                    c.done(dve.tensor_tensor(fill1[:, :], fill[:, :], ranks[u][:, 1, 0, :], ALU.add))
                    c.wait()
                    dve.tensor_tensor(pos[u][:, 1, :], fill1[:, :], ranks[u][:, 0, 1, :], ALU.add)
                    c.done(dve.tensor_tensor(fill[:, :], fill1[:, :], ranks[u][:, 1, 1, :], ALU.add))
                    c.wait()
                    for k in range(TOPK):
                        c.done(dve.tensor_tensor(ohpos[u][:, k, :, :], oh[u][:, k, :, :], pos[u][:, :, :], ALU.mult))
                    c.wait()
                    dve.wait_ge(z3_free[u], START + i)
                    c.done(dve.tensor_reduce(slotf[u][:, :], ohpos[u][:, :, :, :].rearrange("p k t e -> p (k t) e"),
                                             AX_X, ALU.add))
                    c.wait()
                    dve.tensor_copy(slot[u][:, :], slotf[u][:, :]).then_inc(slot_ready[u], 1)

            def layer0_mix(i, c):
                for u in range(2):
                    dve.wait_ge(y_ps[u], START + i + 1)
                    dve.wait_ge(th_ready[u], START + i + 1)
                    c.done(dve.scalar_tensor_tensor(flat(yb[u][:, :, :]), flat(th[u][:, :, :]), 1.0, mb[u][:, :],
                                                    ALU.add, ALU.mult))
                    c.wait()
                    dve.scalar_tensor_tensor(flat(residual(i, u)), flat(yb[u][:, :, :]), half_tg[:, 0:1],
                                             flat(x[u][:, :, :]), ALU.mult, ALU.add).then_inc(x2_done[u], 1)
                    dve.wait_ge(x2_done[u], START + i + 1)
                    statistics(c, residual(i, u), moments(u), var_ready[u])
                    normalise(i, 2, u, residual(i, u))
                    if u == 1:
                        continue
                    for w in range(2):
                        dve.wait_ge(v_ps[w], START + i + 1)
                        dve.wait_ge(pv_done, START + 16 * i)
                        dve.tensor_tensor(v[w][:, :, 0:HD], ring[2 + w][0:C, 0:D].rearrange("p (h c) -> p h c", h=H),
                                          rows[0:C, 0, :].rearrange("p (h c) -> p h c", h=H), ALU.add)\
                            .then_inc(v_ready[w], 1)

            def maxima(i, c):
                for u in range(2):
                    for n in range(8):
                        t, hq = n // 4, n % 4
                        dve.wait_ge(s_ps, START + 16 * i + 8 * u + n + 1)
                        dve.tensor_reduce(mx[u][:, t, 4 * hq:4 * hq + 4],
                                          score_bank(u, n)[:, 0:4 * C].rearrange("p (h c) -> p h c", h=4),
                                          AX_X, ALU.max).then_inc(max_done, 1)
                    dve.wait_ge(max_done, START + 16 * i + 8 * u + 8)
                    dve.wait_ge(mT_ps[u], START + i)
                    dve.tensor_copy(flat(mx16[u][:, :, :]), flat(mx[u][:, :, :])).then_inc(mx_ready[u], 1)

            def tiles_filled(c, more):
                c.done(dve.tensor_tensor(filled[:, :], fill[:, :], iotas[:, 1, :], ALU.subtract))
                c.wait()
                c.done(dve.tensor_scalar(filled_i[:, :], filled[:, :], float(more), None, ALU.add))
                c.wait()
                c.done(dve.tensor_scalar(filled_i[:, :], filled_i[:, :], 7, None, ALU.arith_shift_right))
                c.wait()
                c.done(dve.tensor_copy(ntiles[:, :], filled_i[:, :]))
                c.wait()

            def table(c, first, count):
                past_n, pastn_n, no = past[:, 0:count, :], pastn[:, 0:count, :], tile_no[:, 0:count]
                e_n, c_n = tile_e[:, 0:count], tile_c[:, 0:count]
                wide = [1, count, E]
                c.done(dve.tensor_tensor_scan(cum[:, :], ones_row[:, :], ntiles[:, :], 0.0, ALU.mult, ALU.add))
                c.wait()
                c.done(dve.tensor_tensor(past_n, cum[0:1, :].unsqueeze(1).to_broadcast(wide),
                                         no.unsqueeze(2).to_broadcast(wide), ALU.is_le))
                c.wait()
                c.done(dve.tensor_tensor(pastn_n, past_n, step[0:1, :].unsqueeze(1).to_broadcast(wide), ALU.mult))
                c.done(dve.tensor_reduce(e_n, past_n, AX_X, ALU.add))
                c.wait()
                c.done(dve.tensor_reduce(c_n, pastn_n, AX_X, ALU.add))
                c.done(dve.tensor_scalar(tile_w[:, first:first + count], e_n, float(E - 1), None, ALU.min))
                c.wait()
                c.done(dve.scalar_tensor_tensor(c_n, no, used[0:1, 0:1], c_n, ALU.add, ALU.subtract))
                c.done(dve.tensor_scalar(e_n, e_n, float(CAP), None, ALU.mult))
                c.wait()
                c.done(dve.scalar_tensor_tensor(tile_r[:, first:first + count], c_n, float(P), e_n, ALU.mult, ALU.add))
                c.wait()

            def early_table(c):
                c.done(dve.memset(used[:, :], 0.0))
                tiles_filled(c, 0)
                c.done(dve.tensor_copy(step[:, :], ntiles[:, :]))
                c.wait()
                table(c, 0, WAYS * EARLY)
                c.done(dve.tensor_tensor(used[:, 0:E], ntiles[:, :], cum[:, :], ALU.subtract))
                c.wait()
                c.done(dve.tensor_scalar(used[:, 0:E], used[:, 0:E], float(WAYS * EARLY), 0.0, ALU.add, ALU.max))
                c.wait()
                c.done(dve.tensor_tensor(used[:, 0:E], used[:, 0:E], ntiles[:, :], ALU.min))
                c.wait()
                dve.tensor_copy(filled[:, :], ntiles[:, :]).then_inc(early_ready, 1)

            tab = Steps(dve, tab_step, 0)

            def turn(i, c, more):
                for u in range(2):
                    for t in range(TT):
                        c.done(dve.tensor_tensor(residual(i, u)[:, t, :], residual(i, u)[:, t, :], rows[:, 1, :], ALU.add))
                if more:
                    layer0_enter(i + 1, c)
                else:
                    early_table(tab)
                for u in range(2):
                    dve.wait_ge(pv_done, START + 16 * i + 8 * u + 8)
                    for t in range(TT):
                        ps = (mb, tb)[t][u][:, 0:H * (HD + 1)].rearrange("p (h c) -> p h c", h=H)
                        c.done(dve.reciprocal(rden[u][:, t, :], ps[:, :, HD]))
                    c.wait()
                    for t in range(TT):
                        ps = (mb, tb)[t][u][:, 0:H * (HD + 1)].rearrange("p (h c) -> p h c", h=H)
                        ins = dve.tensor_tensor(att[u][:, t, :].rearrange("p (h c) -> p h c", h=H), ps[:, :, 0:HD],
                                                rden[u][:, t, :].unsqueeze(2).to_broadcast([P, H, HD]), ALU.mult)
                    ins.then_inc(att_ready[u], 1)
                for u in range(2):
                    dve.wait_ge(out_ps[u], START + i + 1)
                    c.done(dve.scalar_tensor_tensor(flat(residual(i, u)), mb[u][:, :], tg[:, 2:3],
                                                    flat(residual(i, u)), ALU.mult, ALU.add))
                    c.wait()
                    statistics(c, residual(i, u), (stats3[u], mv3[u], vare3[u]), var3_ready[u])
                if more:
                    layer0_gate(i + 1, c)
                for u in range(2):
                    dve.wait_ge(rstd3_ready[u], START + i + 1)
                    dve.wait_ge(z3T_ps[u], START + i)
                    dve.wait_ge(z3_free[u], START + i)
                    for t in range(TT):
                        ins = dve.tensor_scalar(z3[u][:, t, 0:D], residual(i, u)[:, t, :], mv3[u][:, t, 0:1],
                                                rstd3[u][:, t:t + 1], ALU.subtract, ALU.mult)
                    ins.then_inc(z3_ready[u], 1)
                if more:
                    layer0_context(i + 1, c)

                if more:
                    layer0_shift(i + 1, c)
                choose(i, c)
                if more:
                    layer0_mix(i + 1, c)
                take_ranks(i, c)
                if more:
                    maxima(i + 1, c)
                weights(i, c)
                place(i, c)
                if more:
                    output_bias(i, c)
                return c.n

            c = Steps(dve, vec_step, 0)
            layer0_enter(0, c)
            dve.wait_ge(s_first, 64)
            dve.wait_ge(s_tg, 1)
            dve.tensor_scalar(half_tg[:, :], tg[:, 1:2], 0.5, None, ALU.mult).then_inc(s_const, 1)
            layer0_gate(0, c)
            layer0_context(0, c)
            layer0_shift(0, c)
            dve.wait_ge(s_small, 144)
            dve.tensor_copy(fill[:, :], iotas[:, 1, :]).then_inc(s_const, 1)
            dve.tensor_scalar(rows[:, 1, :], rows[:, 1, :], tg[:, 2:3], None, ALU.mult).then_inc(s_const, 1)
            dve.tensor_scalar(rows[:, 2, :], rows[:, 2, :], tg[:, 3:4], None, ALU.mult).then_inc(s_const, 1)
            dve.wait_ge(s_const, 4)
            layer0_mix(0, c)
            maxima(0, c)
            steps = c.n
            with dve.Fori(0, IT - 1) as i:
                made = turn(i, Steps(dve, vec_step, steps + VEC_STEPS * i), True)
                assert made == VEC_STEPS, made
            last = Steps(dve, vec_step, steps + VEC_STEPS * (IT - 1))
            turn(IT - 1, last, False)

            dve.tensor_copy(fill_i[:, :], fill[0:1, :]).then_inc(fill_ready, 1)
            tiles_filled(tab, P - 1)
            tab.done(dve.tensor_tensor(ntiles[:, :], ntiles[:, :], used[:, 0:E], ALU.subtract))
            tab.wait()
            tab.done(dve.tensor_tensor(step[:, :], ntiles[:, :], used[:, 0:E], ALU.add))
            tab.wait()
            tab.done(dve.tensor_tensor(step[:, :], step[:, :], used[:, 1:E + 1], ALU.subtract))
            tab.wait()
            table(tab, WAYS * EARLY, TILES - WAYS * EARLY)
            dve.tensor_copy(filled[:, :], ntiles[:, :]).then_inc(tab_ready, 1)
            output_bias(IT - 1, last)

            dve.wait_ge(s_b1, 32)
            dve.wait_ge(tab_ready, 1)
            with dve.Fori(0, TURNS) as i:
                for w in range(WAYS):
                    e = dve.value_load(tile_w[0:1, bass.ds(WAYS * i + w, 1)], min_val=0, max_val=E - 1)
                    bias = [b_1[:, bass.ds(e, 1), m * F:(m + 1) * F].rearrange("p e f -> p (e f)") for m in range(2)]
                    dve.wait_ge(hh_ps, 2 * WAYS * i + 2 * w + 1)
                    dve.wait_ge(sig_ready, before(i, w))
                    dve.tensor_tensor(gate_h[w], hid[w][1][:, :], bias[1], ALU.add).then_inc(gate_ready, 1)
                    dve.wait_ge(hh_ps, 2 * WAYS * i + 2 * w + 2)
                    dve.tensor_tensor(val_h[w], hid[w][0][:, :], bias[0], ALU.add).then_inc(val_ready, 1)
                    dve.wait_ge(val_ready, this(i, w))
                    dve.wait_ge(sig_ready, this(i, w))
                    dve.wait_ge(number_ready, this(i, w))
                    dve.wait_ge(g_free, before(i, w))
                    dve.scalar_tensor_tensor(g_h[w], val_h[w], weight[:, w:w + 1], sig_h[w], ALU.mult, ALU.mult)\
                        .then_inc(gh_ready, 1)

            dve.wait_ge(w_o_hi_ready, 1)
            dve.tensor_tensor(w_o_lo[:, :, :], w_o[:, :, :], w_o_hi[:, :, :], ALU.subtract).then_inc(w_o_lo_ready, 1)

            def low_part(i, q):
                dve.wait_ge(sumT_ready, QT * i + q + 1 + QT)
                dve.wait_ge(out4_ps, QT * i + q + 1)
                dve.tensor_tensor(sumT_lo[q][:, :, :], (tb + ring[2:4])[q][:, :].rearrange("p (a b) -> p a b", a=FT),
                                  sumT_hi[q][:, :, :], ALU.subtract).then_inc(sumT_lo_ready, 1)

            def finish(i, q):
                u, t = q // TT, q % TT
                dve.wait_ge(out4_ps, QT * i + q + 1 + QT)
                dve.wait_ge(y_out_done[u], START + 16 * i)
                dve.tensor_tensor(y_out[u][:, t, :], (mb + ring[0:2])[q][:, 0:D], residual(i, u)[:, t, :], ALU.add)\
                    .then_inc(y_ready, 1)

            def last_turn(i, more):
                for q in range(QT):
                    if q < QT - 1:
                        low_part(i, q + 1)
                    elif more:
                        low_part(i + 1, 0)
                    finish(i, q)

            low_part(0, 0)
            with dve.Fori(0, IT - 1) as i:
                last_turn(i, True)
            last_turn(IT - 1, False)


def kernel(x, ctx_1024, g_xattn, g_ffn, L0_ffn_W_r, L0_ffn_W_k, L0_ffn_W_v, L0_ffn_mu_r, L0_ffn_mu_k,
           L1_xattn_w_q, L1_xattn_b_q, L1_xattn_w_kv, L1_xattn_b_kv, L1_xattn_w_out, L1_xattn_b_out,
           L1_ffn_Wg, L1_ffn_W1, L1_ffn_b1, L1_ffn_Wo, L1_ffn_bo):
    import ml_dtypes
    import concourse.bacc as bacc
    from concourse.bass_utils import run_bass_kernel_spmd

    def blocks(w):
        w = np.asarray(w)
        return np.ascontiguousarray(w.reshape(-1, P, w.shape[1]).transpose(1, 0, 2))

    def every(a):
        a = np.asarray(a)
        return np.ascontiguousarray(np.broadcast_to(a[None], (P,) + a.shape))

    def per_channel(a):
        return np.asarray(a).reshape(KT, P).T

    f32, bf16 = np.float32, ml_dtypes.bfloat16
    tri = np.triu(np.ones((P, P), f32), 1)
    negsel = np.zeros((H, H, C), f32)
    negsel[np.arange(H), np.arange(H)] = -1.0
    arrays = {
        "x": np.asarray(x),
        "ctx": np.asarray(ctx_1024),
        "ctxT": np.ascontiguousarray(np.asarray(ctx_1024).transpose(0, 2, 1)),
        "gates": every(np.stack([np.asarray(g)[l] for l in range(2) for g in (g_xattn, g_ffn)])),
        "w_r": blocks(np.asarray(L0_ffn_W_r).T),
        "w_k": blocks(np.asarray(L0_ffn_W_k).T),
        "w_v": blocks(np.asarray(L0_ffn_W_v).T),
        "w_q": blocks(L1_xattn_w_q),
        "w_kv": blocks(L1_xattn_w_kv),
        "w_out": blocks(L1_xattn_w_out),
        "w_g": blocks(np.asarray(L1_ffn_Wg).T),
        "w_o": blocks(np.asarray(L1_ffn_Wo).T),
        "w_1": np.ascontiguousarray(np.asarray(L1_ffn_W1).transpose(0, 2, 1)),
        "b_1": every(L1_ffn_b1),
        "chan": np.ascontiguousarray(np.stack(
            [per_channel(a) for a in (L0_ffn_mu_r, L0_ffn_mu_k, L1_xattn_b_q, np.asarray(L1_xattn_b_kv)[:D])], 1)),
        "rows": every(np.stack([np.asarray(L1_xattn_b_kv)[D:], np.asarray(L1_xattn_b_out), np.asarray(L1_ffn_bo)])),
        "ident": np.eye(P, dtype=f32),
        "ident16": np.eye(P, dtype=f32).astype(bf16),
        "tri_ones": np.ascontiguousarray(np.stack([tri, np.ones((P, P), f32)], 1)).astype(bf16),
        "headmask": (np.arange(P)[:, None] // HD == np.arange(HB)[None]).astype(f32),
        "negsel": negsel.astype(bf16),
        "iotas": every(np.stack([np.arange(E), np.arange(E) * CAP]).astype(f32)),
        "numbers": np.concatenate(
            [TOPK * (np.arange(2 * TT)[None] * P + np.arange(P)[:, None]), np.full((P, 1), SLOTS * P),
             TOPK * B * T + np.arange(WAYS)[None] * P + np.arange(P)[:, None]], 1).astype(f32),
        "tile_no": np.arange(TILES + 1, dtype=f32)[None],
    }
    nc = bacc.Bacc("TRN2", target_bir_lowering=False, num_devices=1)
    feed, d = {}, {}
    for name, a in arrays.items():
        feed[f"in_{name}"] = a
        d[name] = nc.dram_tensor(f"in_{name}", a.shape, mybir.dt.from_np(a.dtype), kind="ExternalInput").ap()
    out = nc.dram_tensor("out_0_dram", (B, T, D), F32, kind="ExternalOutput").ap()
    build(nc, d, out)
    return run_bass_kernel_spmd(nc, [feed], core_ids=[0]).results[0]["out_0_dram"]
```
